# Optimizing a Trainium2 kernel written in Bass

```python
import numpy as np
import jax
import jax.numpy as jnp

def _softmax(x, axis=-1):
    return jax.nn.softmax(x, axis=axis)

def _gelu(x):
    return jax.nn.gelu(x, approximate=True)

def _silu(x):
    return jax.nn.silu(x)

def _sigmoid(x):
    return jax.nn.sigmoid(x)

def _layernorm(x, axis=-1, eps=1e-05):
    m = jnp.mean(x, axis=axis, keepdims=True)
    v = jnp.var(x, axis=axis, keepdims=True)
    return (x - m) / jnp.sqrt(v + eps)

def _scatter_add(tgt, idx, src, axis=0):
    return tgt.at[idx].add(src)

def _segment_sum(src, seg, n):
    return jax.ops.segment_sum(src, seg, n)
kernel_name = 'mk_perceiver_d1_seqx_r8_ccee16'

def setup_inputs(seed: int=0):
    np.random.seed(seed)
    _w = jnp.asarray

    def _rec_inputs():
        import jax
        import jax.numpy as jnp
        _rk = jax.random.key(seed)
        x = -0.0003929 + 0.9999 * jax.random.normal(jax.random.fold_in(_rk, 1), (8, 64, 512), jnp.float32)
        _lenS = 64 - jax.random.randint(jax.random.fold_in(_rk, 7), (8,), 0, max(1, 64 // 4) + 1, jnp.int32)
        _lenS2 = 1601 - jax.random.randint(jax.random.fold_in(_rk, 8), (8,), 0, max(1, 1601 // 4) + 1, jnp.int32)
        _ctx_4096P = jax.random.normal(jax.random.fold_in(_rk, 11), (8, 16, 512), jnp.float32)
        _ctx_4096c = jax.random.dirichlet(jax.random.fold_in(_rk, 511), 0.3 * jnp.ones((16,), jnp.float32), (8, 1601))
        _ctx_4096t = jnp.einsum('bsk,bkd->bsd', _ctx_4096c, _ctx_4096P)
        _ctx_4096t = _ctx_4096t * jax.lax.rsqrt(jnp.mean(jnp.square(_ctx_4096t)) + 1e-12) * 0.953939
        ctx_4096 = 2.81802e-05 + 1.00001 * (_ctx_4096t + 0.3 * jax.random.normal(jax.random.fold_in(_rk, 611), (8, 1601, 512), jnp.float32))
        return (x, ctx_4096)
    x, ctx_4096 = _rec_inputs()

    def _L0_xattn_setup():
        import jax, jax.numpy as jnp
        import numpy as np
        B, N, NKV = (2, 256, 256)
        E = 512
        H = 16
        HD = E // H
        LQ = E // 8
        LKV = E // 16
        key = jax.random.key(seed)
        ks = jax.random.split(key, 6)
        Q = jax.random.normal(ks[0], (B, N, E), dtype=jnp.float32)
        K = jax.random.normal(ks[1], (B, NKV, E), dtype=jnp.float32)
        Wq_d = jax.random.normal(ks[2], (E, LQ), dtype=jnp.float32) / np.sqrt(E)
        W_qk = jax.random.normal(ks[3], (LQ, H * LKV), dtype=jnp.float32) / np.sqrt(LQ)
        Wkv_d = jax.random.normal(ks[4], (E, LKV), dtype=jnp.float32) / np.sqrt(E)
        Wv_u = jax.random.normal(ks[5], (LKV, H * HD), dtype=jnp.float32) / np.sqrt(LKV)
        return {'Q': Q, 'K': K, 'Wq_d': Wq_d, 'W_qk': W_qk, 'Wkv_d': Wkv_d, 'Wv_u': Wv_u}
    _L0_xattn_all = _L0_xattn_setup()
    _L0_xattn_in = {k: v for k, v in _L0_xattn_all.items() if k in ('Wq_d', 'W_qk', 'Wkv_d', 'Wv_u')}
    del _L0_xattn_all

    def _L0_attn_setup():
        import jax, jax.numpy as jnp
        import numpy as np
        import math
        DIM, NH, NKV, HD = (512, 32, 8, 128)
        BLOCK, NBLK, TOPK = (32, 128, 16)

        def apply_rope(x, cos, sin):
            b, l, h, d = x.shape
            xr = x.reshape(b, l, h, d // 2, 2)
            xe, xo = (xr[..., 0], xr[..., 1])
            c = cos[None, :, None, :]
            s = sin[None, :, None, :]
            oe = xe * c - xo * s
            oo = xe * s + xo * c
            return jnp.stack([oe, oo], axis=-1).reshape(b, l, h, d)
        key = jax.random.key(seed)
        ks = jax.random.split(key, 8)
        x = jax.random.normal(ks[0], (1, 1, DIM), dtype=jnp.float32)
        start_pos = 512
        inv_freq = 1.0 / 500000.0 ** (np.arange(0, HD, 2, dtype=np.float32) / HD)
        ang = np.float32(start_pos) * inv_freq
        freqs_cos = jnp.asarray(np.cos(ang))[None, :]
        freqs_sin = jnp.asarray(np.sin(ang))[None, :]
        sc = 0.02
        wq = jax.random.normal(ks[1], (NH * HD, DIM), dtype=jnp.float32) * sc
        wk = jax.random.normal(ks[2], (NKV * HD, DIM), dtype=jnp.float32) * sc
        wv = jax.random.normal(ks[3], (NKV * HD, DIM), dtype=jnp.float32) * sc
        wo = jax.random.normal(ks[4], (DIM, NH * HD), dtype=jnp.float32) * sc
        k_cache = jax.random.normal(ks[5], (NBLK, BLOCK, NKV, HD), dtype=jnp.float32)
        v_cache = jax.random.normal(ks[6], (NBLK, BLOCK, NKV, HD), dtype=jnp.float32)
        block_idx = jnp.sort(jax.random.randint(ks[7], (TOPK,), 0, NBLK, dtype=jnp.int32))
        return {'x': x, 'freqs_cos': freqs_cos, 'freqs_sin': freqs_sin, 'wq': wq, 'wk': wk, 'wv': wv, 'wo': wo, 'k_cache': k_cache, 'v_cache': v_cache, 'block_idx': block_idx}
    _L0_attn_all = _L0_attn_setup()
    _L0_attn_in = {k: v for k, v in _L0_attn_all.items() if k in ('freqs_cos', 'freqs_sin', 'wq', 'wk', 'wv', 'wo', 'k_cache', 'v_cache', 'block_idx')}
    del _L0_attn_all

    def _L0_ffn_setup():
        import jax, jax.numpy as jnp
        import numpy as np
        HID, INTER = (512, 1792)
        B, S = (2, 256)

        def _binary_diff_weight(w, base):
            d = w - base
            coeff = jnp.mean(jnp.abs(d))
            return base + coeff * jnp.sign(d)
        key = jax.random.key(seed)
        ks = jax.random.split(key, 7)
        return {'hidden_states': jax.random.normal(ks[0], (B, S, HID), dtype=jnp.float32), 'w1': jax.random.normal(ks[1], (INTER, HID), dtype=jnp.float32) * 0.02, 'mean_w1': jax.random.normal(ks[2], (INTER, HID), dtype=jnp.float32) * 0.02, 'w2': jax.random.normal(ks[3], (HID, INTER), dtype=jnp.float32) * 0.02, 'mean_w2': jax.random.normal(ks[4], (HID, INTER), dtype=jnp.float32) * 0.02, 'w3': jax.random.normal(ks[5], (INTER, HID), dtype=jnp.float32) * 0.02, 'mean_w3': jax.random.normal(ks[6], (INTER, HID), dtype=jnp.float32) * 0.02}
    _L0_ffn_all = _L0_ffn_setup()
    _L0_ffn_in = {k: v for k, v in _L0_ffn_all.items() if k in ('w1', 'mean_w1', 'w2', 'mean_w2', 'w3', 'mean_w3')}
    del _L0_ffn_all
    return {'x': x, 'ctx_4096': ctx_4096, 'L0_xattn_Wq_d': _L0_xattn_in['Wq_d'], 'L0_xattn_W_qk': _L0_xattn_in['W_qk'], 'L0_xattn_Wkv_d': _L0_xattn_in['Wkv_d'], 'L0_xattn_Wv_u': _L0_xattn_in['Wv_u'], 'L0_attn_freqs_cos': _L0_attn_in['freqs_cos'], 'L0_attn_freqs_sin': _L0_attn_in['freqs_sin'], 'L0_attn_wq': _L0_attn_in['wq'], 'L0_attn_wk': _L0_attn_in['wk'], 'L0_attn_wv': _L0_attn_in['wv'], 'L0_attn_wo': _L0_attn_in['wo'], 'L0_attn_k_cache': _L0_attn_in['k_cache'], 'L0_attn_v_cache': _L0_attn_in['v_cache'], 'L0_attn_block_idx': _L0_attn_in['block_idx'], 'L0_ffn_w1': _L0_ffn_in['w1'], 'L0_ffn_mean_w1': _L0_ffn_in['mean_w1'], 'L0_ffn_w2': _L0_ffn_in['w2'], 'L0_ffn_mean_w2': _L0_ffn_in['mean_w2'], 'L0_ffn_w3': _L0_ffn_in['w3'], 'L0_ffn_mean_w3': _L0_ffn_in['mean_w3']}

def reference(x, ctx_4096, L0_xattn_Wq_d, L0_xattn_W_qk, L0_xattn_Wkv_d, L0_xattn_Wv_u, L0_attn_freqs_cos, L0_attn_freqs_sin, L0_attn_wq, L0_attn_wk, L0_attn_wv, L0_attn_wo, L0_attn_k_cache, L0_attn_v_cache, L0_attn_block_idx, L0_ffn_w1, L0_ffn_mean_w1, L0_ffn_w2, L0_ffn_mean_w2, L0_ffn_w3, L0_ffn_mean_w3):
    import jax
    import jax.numpy as jnp

    def _L0_xattn_ref(Q, K, Wq_d, W_qk, Wkv_d, Wv_u):
        import jax, jax.numpy as jnp
        import numpy as np
        B, N, NKV = (2, 256, 256)
        E = 512
        H = 16
        HD = E // H
        LQ = E // 8
        LKV = E // 16
        b, n, _ = Q.shape
        nkv = K.shape[1]
        C_q = Q @ Wq_d
        C_kv = K @ Wkv_d
        CqWqk = (C_q @ W_qk).reshape(b, n, H, LKV)
        scores = jnp.einsum('bnhl,bkl->bhnk', CqWqk, C_kv) / jnp.sqrt(jnp.asarray(LKV, dtype=Q.dtype))
        attn = jax.nn.softmax(scores, axis=-1)
        V_up = (C_kv @ Wv_u).reshape(b, nkv, H, HD)
        out = jnp.einsum('bhnk,bkhd->bnhd', attn, V_up)
        return out.reshape(b, n, H * HD)

    def _L0_attn_ref(x, freqs_cos, freqs_sin, wq, wk, wv, wo, k_cache, v_cache, block_idx):
        import jax, jax.numpy as jnp
        import numpy as np
        import math
        DIM, NH, NKV, HD = (512, 32, 8, 128)
        BLOCK, NBLK, TOPK = (32, 128, 16)

        def apply_rope(x, cos, sin):
            b, l, h, d = x.shape
            xr = x.reshape(b, l, h, d // 2, 2)
            xe, xo = (xr[..., 0], xr[..., 1])
            c = cos[None, :, None, :]
            s = sin[None, :, None, :]
            oe = xe * c - xo * s
            oo = xe * s + xo * c
            return jnp.stack([oe, oo], axis=-1).reshape(b, l, h, d)
        b, l, _ = x.shape
        n_rep = NH // NKV
        q = (x @ wq.T).reshape(b, l, NH, HD)
        k = (x @ wk.T).reshape(b, l, NKV, HD)
        v = (x @ wv.T).reshape(b, l, NKV, HD)
        q = apply_rope(q, freqs_cos, freqs_sin)
        k = apply_rope(k, freqs_cos, freqs_sin)
        k_sel = k_cache[block_idx].reshape(-1, NKV, HD)
        v_sel = v_cache[block_idx].reshape(-1, NKV, HD)
        k_full = jnp.concatenate([k_sel, k[0]], axis=0)
        v_full = jnp.concatenate([v_sel, v[0]], axis=0)
        k_full = jnp.repeat(k_full.transpose(1, 0, 2)[None], n_rep, axis=1)
        v_full = jnp.repeat(v_full.transpose(1, 0, 2)[None], n_rep, axis=1)
        qh = q.transpose(0, 2, 1, 3)
        scores = jnp.einsum('bhld,bhtd->bhlt', qh, k_full) / math.sqrt(HD)
        attn = jax.nn.softmax(scores, axis=-1)
        out = jnp.einsum('bhlt,bhtd->bhld', attn, v_full)
        out = out.transpose(0, 2, 1, 3).reshape(b, l, NH * HD)
        return out @ wo.T

    def _L0_ffn_ref(hidden_states, w1, mean_w1, w2, mean_w2, w3, mean_w3):
        import jax, jax.numpy as jnp
        import numpy as np
        HID, INTER = (512, 1792)
        B, S = (2, 256)

        def _binary_diff_weight(w, base):
            d = w - base
            coeff = jnp.mean(jnp.abs(d))
            return base + coeff * jnp.sign(d)
        W1 = _binary_diff_weight(w1, mean_w1)
        W2 = _binary_diff_weight(w2, mean_w2)
        W3 = _binary_diff_weight(w3, mean_w3)
        gate = jnp.einsum('bsh,ih->bsi', hidden_states, W1)
        up = jnp.einsum('bsh,ih->bsi', hidden_states, W3)
        h = jax.nn.silu(gate) * up
        return jnp.einsum('bsi,hi->bsh', h, W2)
    x = x + _L0_xattn_ref(_layernorm(x, axis=-1), ctx_4096, L0_xattn_Wq_d, L0_xattn_W_qk, L0_xattn_Wkv_d, L0_xattn_Wv_u)
    x = x + _L0_attn_ref(_layernorm(x, axis=-1), L0_attn_freqs_cos, L0_attn_freqs_sin, L0_attn_wq, L0_attn_wk, L0_attn_wv, L0_attn_wo, L0_attn_k_cache, L0_attn_v_cache, L0_attn_block_idx)
    x = x + _L0_ffn_ref(_layernorm(x, axis=-1), L0_ffn_w1, L0_ffn_mean_w1, L0_ffn_w2, L0_ffn_mean_w2, L0_ffn_w3, L0_ffn_mean_w3)
    return x

_drawn_inputs = setup_inputs


def setup_inputs(seed=0):
    import zlib

    import numpy as np

    out = dict(_drawn_inputs(seed))
    spreads = {}
    factors = {'L0_attn_freqs_cos': 2.821,
     'L0_attn_freqs_sin': 4.041,
     'L0_attn_wk': 8.0,
     'L0_attn_k_cache': 8.0,
     'L0_attn_v_cache': 8.0,
     'L0_ffn_w1': 4.165,
     'L0_ffn_mean_w1': 5.012,
     'L0_ffn_w2': 4.105,
     'L0_ffn_mean_w2': 4.976,
     'L0_ffn_w3': 4.103,
     'L0_ffn_mean_w3': 4.986}
    for name, (base, spread) in spreads.items():
        noise = np.random.default_rng([zlib.crc32(name.encode()), seed]).standard_normal(out[name].shape)
        drawn = base * np.exp(spread * noise) if base else spread * noise
        out[name] = jnp.asarray(drawn.astype(out[name].dtype))
    for name, factor in factors.items():
        out[name] = (out[name] * factor).astype(out[name].dtype)
    return out
```

```python
from contextlib import ExitStack

import concourse.bass as bass
from concourse import mybir

F32 = mybir.dt.float32
F32R = mybir.dt.float32r
I32 = mybir.dt.int32
ALU = mybir.AluOpType
ACT = mybir.ActivationFunctionType
AX = mybir.AxisListType

P = 128
BANK = 512

BATCH, SEQ, DIM = 8, 64, 512
TOK = BATCH * SEQ
TT = TOK // P
DC = DIM // P
EPS = 1e-5

XH, LQ, LKV, XHD = 16, 64, 32, 32
NCTX = 1601
FULL = NCTX // P
TAIL = NCTX - FULL * P
KT = FULL + 1
XQ = XH * SEQ
QTILES = XQ // P
GROUPS = P // LKV
PER_GROUP = FULL // GROUPS
MAIN = PER_GROUP * P
SHIFT = 3 * LKV
STACK = SHIFT + 1
UW = 64
OW = XHD + 2
XSCALE = float(LKV) ** -0.5

NH, NKV, HD = 32, 8, 128
REP = NH // NKV
BLOCK, NBLK, TOPK = 32, 128, 16
NSEL = TOPK * BLOCK
ST = NSEL // P
KEYS = NSEL + SEQ
GSCALE = float(HD) ** -0.5

INTER = 1792
CH = INTER // P
PASSES = ((0, 0), (0, 1), (1, 0))

WSIZE = INTER * DIM
PIECE = WSIZE // P // BATCH


def wait(eng, sem, count):
    if isinstance(count, int) and count <= 0:
        return
    eng.wait_ge(sem, count)


def stand_alone(eng, core):
    eng.wait_ge(core.first_stage, 1)


class Core:

    def __init__(self, nc, ctx, arg, out):
        self.nc, self.ctx, self.arg, self.out = nc, ctx, arg, out
        self.psum = ctx.enter_context(nc.psum_tensor("psum", [P, 8, BANK], F32))
        self.x = self.sb("x", [P, TT, DIM])
        self.ident = self.sb("ident", [P, P])
        self.rope = self.sb("rope", [P, P])
        self.rope_t = self.sb("rope_t", [P, P])
        self.abs_sum = self.sb("abs_sum", [P, BATCH, 3])
        self.cache_in = self.sem("cache_in")
        self.first_stage = self.sem("first_stage_reached")

    def sb(self, name, shape, dt=F32, ctx=None):
        return (ctx or self.ctx).enter_context(self.nc.sbuf_tensor(name, shape, dt))

    def sem(self, name, ctx=None):
        return (ctx or self.ctx).enter_context(self.nc.semaphore(name))


def layer_norm_t(core, name, parts, ctx, exact=None, exact_tokens=0):
    nc = core.nc
    with ExitStack() as own:
        stats = core.sb(f"{name}_stats", [P, TT, 6], ctx=own)
        mean_var = core.sb(f"{name}_mean_var", [P, TT, 2], ctx=own)
        rstd = core.sb(f"{name}_rstd", [P, TT], ctx=own)
        normed = core.sb(f"{name}_normed", [P, TT, DIM], ctx=own)
        s_stats = core.sem(f"{name}_stats_done", own)
        s_agg = core.sem(f"{name}_moments_done", own)
        s_var = core.sem(f"{name}_variance_done", own)
        s_root = core.sem(f"{name}_root_done", own)
        s_rstd = core.sem(f"{name}_rstd_done", own)
        s_norm = core.sem(f"{name}_normed_done", own)
        s_tr = core.sem(f"{name}_transposed", own)
        s_high = core.sem(f"{name}_high_done", own)
        s_exact = core.sem(f"{name}_exact_done", own)
        with nc.Block() as block:

            @block.vector
            def _(dve):
                for j in range(TT):
                    dve.bn_stats(stats[:, j, :], core.x[:, j, :]).then_inc(s_stats, 1)
                for j in range(TT):
                    dve.wait_ge(s_stats, j + 1)
                    dve.bn_aggr(mean_var[:, j, :], stats[:, j, :]).then_inc(s_agg, 1)
                dve.wait_ge(s_agg, TT)
                dve.tensor_scalar(rstd[:, :], mean_var[:, :, 1], EPS, None, ALU.add).then_inc(s_var, 1)
                dve.wait_ge(s_root, 1)
                dve.reciprocal(rstd[:, :], rstd[:, :]).then_inc(s_rstd, 1)
                dve.wait_ge(s_rstd, 1)
                for j in range(TT):
                    dve.tensor_scalar(normed[:, j, :], core.x[:, j, :], mean_var[:, j, 0:1], rstd[:, j:j + 1],
                                      ALU.subtract, ALU.mult).then_inc(s_norm, 1)
                if parts:
                    for j in range(TT):
                        dve.wait_ge(s_tr, j + 1)
                        dve.wait_ge(s_high, j + 1)
                        cols = slice(j * P, (j + 1) * P)
                        dve.tensor_tensor(parts[1][:, :, cols],
                                          core.psum[:, j, :].rearrange("p (c t) -> p c t", c=DC),
                                          parts[0][:, :, cols], ALU.subtract)
                if exact is not None:
                    dve.wait_ge(s_exact, (exact_tokens + P - 1) // P)

            @block.tensor
            def _(pe):
                for j in range(TT):
                    pe.wait_ge(s_norm, j + 1)
                    for c in range(DC):
                        mm = pe.transpose(core.psum[:, j, c * P:(c + 1) * P],
                                          normed[:, j, c * P:(c + 1) * P], core.ident[:, :])
                    mm.then_inc(s_tr, 1)

            @block.scalar
            def _(act):
                act.wait_ge(s_var, 1)
                act.activation(rstd[:, :], rstd[:, :], ACT.Sqrt).then_inc(s_root, 1)
                for j in range(TT):
                    act.wait_ge(s_tr, j + 1)
                    src = core.psum[:, j, :].rearrange("p (c t) -> p c t", c=DC)
                    cols = slice(j * P, (j + 1) * P)
                    n = min(P, exact_tokens - j * P)
                    if exact is not None and n > 0:
                        act.activation(exact[:, :, j * P:j * P + n], src[:, :, 0:n], ACT.Copy).then_inc(s_exact, 1)
                    if parts:
                        act.activation(parts[0][:, :, cols], src, ACT.Copy).then_inc(s_high, 1)


def load_and_constants(core, w):
    nc, arg = core.nc, core.arg
    with ExitStack() as own:
        cos_col = core.sb("cos_col", [P, 1], ctx=own)
        sin_col = core.sb("sin_col", [P, 1], ctx=own)
        swap = core.sb("swap", [P, P], ctx=own)
        turned = core.sb("turned", [P, P], ctx=own)
        diag = core.sb("diag", [P, P], ctx=own)
        s_in = core.sem("x_in", own)
        s_w = core.sem("weights_in", own)
        s_rot = core.sem("angles_in", own)
        s_zero = core.sem("zeroed", own)
        s_mask = core.sem("masks_done", own)
        s_step = core.sem("rope_step", own)
        with nc.Block() as block:

            @block.sync
            def _(sp):
                sp.dma_start(core.x[:, :, :], arg["x"].rearrange("b n e -> (b n) e")
                             .rearrange("(j p) e -> p j e", p=P)).then_inc(s_in, 16)
                sp.wait_ge(s_in, 16)

            @block.scalar
            def _(act):
                act.dma_start(w["wq_d"][:, :, :], arg["Wq_d"].rearrange("(c p) q -> p c q", p=P)).then_inc(s_w, 16)
                qk = arg["W_qk"].rearrange("q (h l) -> q h l", h=XH)
                for r in range(3):
                    act.dma_start(w["w_qk"][:, :, r, :], qk).then_inc(s_w, 16)
                act.dma_start(w["wkv_d"][:, :, :], arg["Wkv_d"].rearrange("(c p) l -> p c l", p=P)).then_inc(s_w, 16)
                act.wait_ge(s_zero, 2)
                for base in (0, UW):
                    act.dma_start(w["wv_u"][base:base + LKV, :, 0:XHD],
                                  arg["Wv_u"].rearrange("l (h d) -> l h d", h=XH)).then_inc(s_w, 16)
                for col, src in ((cos_col, arg["cos"]), (sin_col, arg["sin"])):
                    for odd in range(2):
                        act.dma_start(col[odd:P:2, 0:1], src.rearrange("a i -> i a")).then_inc(s_rot, 16)
                act.wait_ge(s_w, 7 * 16)

            @block.gpsimd
            def _(pool):
                pool.memset(core.ident[:, :], 0.0).then_inc(s_zero, 1)
                pool.memset(swap[:, :], 0.0).then_inc(core.first_stage, 1)
                pool.memset(w["wv_u"][:, :, :], 0.0).then_inc(s_zero, 1)
                pool.memset(w["c_stack"][:, :, :], 0.0).then_inc(s_zero, 1)
                pool.memset(w["c_stage"][:, :, :], 0.0).then_inc(s_zero, 1)
                pool.memset(w["c_nat"][:, :, :, :], 0.0).then_inc(s_zero, 1)
                pool.memset(w["max_row"][:, :, :], 0.0).then_inc(s_zero, 1)
                pool.memset(w["c_t"][:, :, :].bitcast(F32), 0.0).then_inc(s_zero, 1)
                pool.wait_ge(s_zero, 7)
                pool.wait_ge(core.first_stage, 1)
                pool.memset(w["c_nat"][:, :, :, LKV:LKV + 1], 1.0).then_inc(s_mask, 1)
                pool.wait_ge(s_mask, 1)
                pool.memset(w["c_stack"][:, :, SHIFT:SHIFT + 1], 1.0).then_inc(s_mask, 1)
                for n, base in enumerate((LKV, UW + LKV)):
                    pool.wait_ge(s_mask, 2 + n)
                    pool.memset(w["wv_u"][base:base + 1, :, XHD:XHD + 1], 1.0).then_inc(s_mask, 1)
                pool.wait_ge(s_mask, 4)
                pool.affine_select(out=core.ident[:, :], in_=core.ident[:, :], compare_op=ALU.not_equal, fill=1.0,
                                   base=0, pattern=[[-1, P]], channel_multiplier=1).then_inc(s_mask, 1)
                pair = swap[:, :].rearrange("p (i e) -> p i e", e=2)
                pool.wait_ge(s_mask, 5)
                pool.affine_select(out=pair[:, :, 0], in_=pair[:, :, 0], compare_op=ALU.not_equal, fill=1.0,
                                   base=-1, pattern=[[-2, P // 2]], channel_multiplier=1).then_inc(s_mask, 1)
                pool.wait_ge(s_mask, 6)
                pool.affine_select(out=pair[:, :, 1], in_=pair[:, :, 1], compare_op=ALU.not_equal, fill=-1.0,
                                   base=0, pattern=[[-2, P // 2]], channel_multiplier=1).then_inc(s_mask, 1)
                pool.wait_ge(s_mask, 7)

            @block.vector
            def _(dve):
                dve.wait_ge(s_mask, 7)
                dve.wait_ge(s_rot, 4 * 16)
                dve.tensor_scalar(diag[:, :], core.ident[:, :], cos_col[:, 0:1], None, ALU.mult).then_inc(s_step, 1)
                dve.tensor_scalar(turned[:, :], swap[:, :], sin_col[:, 0:1], None, ALU.mult).then_inc(s_step, 1)
                dve.wait_ge(s_step, 2)
                dve.tensor_tensor(core.rope[:, :], diag[:, :], turned[:, :], ALU.add).then_inc(s_step, 1)
                dve.tensor_tensor(core.rope_t[:, :], diag[:, :], turned[:, :], ALU.subtract).then_inc(s_step, 1)
                dve.wait_ge(s_step, 4)


def gather_cache(core, k_sel, v_sel):
    nc, arg = core.nc, core.arg
    with ExitStack() as own:
        index = core.sb("index", [1, TOPK], I32, ctx=own)
        s_idx = core.sem("index_in", own)
        with nc.Block() as block:

            @block.sync
            def _(sp):
                sp.dma_start(index[:, :], arg["block_idx"].rearrange("(a k) -> a k", a=1)).then_inc(s_idx, 16)
                sp.wait_ge(s_idx, 16)
                for n in range(TOPK):
                    blk = sp.value_load(index[0:1, n:n + 1], min_val=0, max_val=NBLK - 1)
                    rows = slice((n * BLOCK) % P, (n * BLOCK) % P + BLOCK)
                    for cache, dst in (("v_cache", v_sel), ("k_cache", k_sel)):
                        sp.dma_start(dst[rows, n * BLOCK // P, :],
                                     arg[cache][bass.ds(blk, 1)].rearrange("a k h d -> (a k) (h d)")
                                     ).then_inc(core.cache_in, 16)


def cross_queries(core, w, xn_t):
    nc = core.nc
    with ExitStack() as own:
        cq_t = core.sb("cq_t", [LQ, TOK], ctx=own)
        high_c = core.sb("q_high_c", [P, 2, TOK], F32R, ctx=own)
        s_cq = core.sem("cq_done", own)
        s_cq_sb = core.sem("cq_copied", own)
        s_q = core.sem("q_done", own)
        s_hi = core.sem("q_high_done", own)
        s_lo = core.sem("q_low_done", own)
        qt = w["q_t"]
        with nc.Block() as block:

            @block.tensor
            def _(pe):
                for c in range(DC):
                    mm = pe.matmul(core.psum[0:LQ, 4, :], w["wq_d"][:, c, :], xn_t[:, c, :],
                                   start=(c == 0), stop=(c == DC - 1))
                mm.then_inc(s_cq, 1)
                pe.wait_ge(s_cq_sb, 1)
                for h in range(XH):
                    wait(pe, s_lo, h - 3)
                    wait(pe, s_hi, 2 * (h - 3))
                    pe.matmul(core.psum[0:SHIFT, h % 4, :], w["w_qk"][:, h, :, :], cq_t[:, :],
                              start=True, stop=True).then_inc(s_q, 1)

            @block.scalar
            def _(act):
                act.wait_ge(s_cq, 1)
                act.activation(cq_t[:, :], core.psum[0:LQ, 4, :], ACT.Copy).then_inc(s_cq_sb, 1)
                for h in range(XH):
                    act.wait_ge(s_q, h + 1)
                    act.activation(qt[0:2 * LKV, :, h, :],
                                   core.psum[0:2 * LKV, h % 4, :].rearrange("p (b n) -> p b n", b=BATCH),
                                   ACT.Copy).then_inc(s_hi, 1)
                    wait(act, s_lo, h - 1)
                    act.activation(high_c[2 * LKV:SHIFT, h % 2, :], core.psum[2 * LKV:SHIFT, h % 4, :],
                                   ACT.Copy).then_inc(s_hi, 1)

            @block.vector
            def _(dve):
                for h in range(XH):
                    dve.wait_ge(s_hi, 2 * h + 2)
                    dve.tensor_tensor(qt[2 * LKV:SHIFT, :, h, :],
                                      core.psum[2 * LKV:SHIFT, h % 4, :].rearrange("p (b n) -> p b n", b=BATCH),
                                      high_c[2 * LKV:SHIFT, h % 2, :].rearrange("p (b n) -> p b n", b=BATCH),
                                      ALU.subtract).then_inc(s_lo, 1)
                dve.wait_ge(s_lo, XH)


PREP = [("turn", t) for t in range(KT)] + [("compress", 0), ("natural", 0)] + [("stack", k) for k in range(4)]
PREP_SLOT = [0, 0, 1, 1, 2, 2, 3, 3, 4, 4, 5, 5, 6, 7, 8, 9, 10, 11, 12]
PREP_ON_ACT = [kind == "turn" and t % 2 == 1 or kind == "compress" or kind == "stack" and t % 2 == 0
               for kind, t in PREP]
ACT_PREPS = sum(PREP_ON_ACT)
DVE_PREPS = len(PREP) - ACT_PREPS
MAX_SLOT = [i * 12 // (2 * QTILES) for i in range(2 * QTILES)]


def stack_tiles(k):
    return [t for t in range(4 * k, min(4 * k + 4, KT))]


def rows_of(t):
    return P if t < FULL else TAIL


def cross_attention(core, w, own):
    nc, arg, psum = core.nc, core.arg, core.psum
    ctx_nat = [core.sb(f"ctx_nat{i}", [P, KT, DIM], ctx=own) for i in range(2)]
    ctx_t = core.sb("ctx_t", [P, DC, KT * P], ctx=own)
    c_parts = core.sb("c_parts", [P, MAIN + TAIL], ctx=own)
    q_now = [core.sb(f"q_now{i}", [P, XQ], F32R, ctx=own) for i in range(2)]
    max_half = core.sb("max_half", [P, QTILES, 2], ctx=own)
    probs = [core.sb(f"probs{i}", [P, XQ], ctx=own) for i in range(2)]
    u_t = core.sb("u_t", [P, XQ // 2], ctx=own)
    rden = core.sb("rden", [P, XH], ctx=own)
    mixed = core.sb("mixed", [P, XH, XHD], ctx=own)
    zero = core.sb("zero", [P, 1], ctx=own)
    w_raw = core.sb("w_raw", [P, 3, 2, PIECE], ctx=own)
    c_stage = w["c_stage"]
    c_nat, c_stack, c_t, max_row, q_t = w["c_nat"], w["c_stack"], w["c_t"], w["max_row"], w["q_t"]

    s_ctx = [core.sem(f"ctx_in{i}", own) for i in range(2)]
    s_zero = core.sem("zero_ready", own)
    s_raw = core.sem("w_raw_in", own)
    s_diff = core.sem("w_diff_done", own)
    s_abs = core.sem("w_abs_done", own)
    s_prep = core.sem("prep_psum_done", own)
    s_pact = core.sem("prep_out_by_act", own)
    s_pdve = core.sem("prep_out_by_dve", own)
    s_part = core.sem("c_stack_part_done", own)
    s_cnat = core.sem("values_placed", own)
    s_qnow = core.sem("q_now_done", own)
    s_sa = core.sem("max_scores_done", own)
    s_max = core.sem("max_half_done", own)
    s_neg = core.sem("max_negated", own)
    s_mt = core.sem("max_turned", own)
    s_shift = core.sem("shift_row_done", own)
    s_sb = core.sem("scores_done", own)
    s_exp = core.sem("probs_done", own)
    s_pv = core.sem("probs_used", own)
    s_u = core.sem("u_copied", own)
    s_o = core.sem("mix_done", own)
    s_rd = core.sem("den_inverted", own)
    s_mix = core.sem("mix_scaled", own)
    s_x = core.sem("x_updated", own)

    wnames = (("w1", "mean_w1"), ("w3", "mean_w3"), ("w2", "mean_w2"))
    flat = {n: arg[n].rearrange("r c -> (r c)").rearrange("(p f) -> p f", p=P) for pair in wnames for n in pair}

    def prep_out_wait(eng, b, n):
        wait(eng, s_pact, ACT_PREPS * b + sum(PREP_ON_ACT[:n]))
        wait(eng, s_pdve, DVE_PREPS * b + n - sum(PREP_ON_ACT[:n]))

    steps_static = [(-2, None, None, 0), (-1, None, 0, 1)]
    steps_end = [(6, 6, 7, None), (7, 7, None, None)]

    def run(eng, step):
        for s, back, lead, prep in steps_static:
            step(back, lead, prep, s % 2, None)
        with eng.Fori(0, (BATCH - 2) // 2) as j:
            step(2 * j, 2 * j + 1, 2 * j + 2, 0, j)
            step(2 * j + 1, 2 * j + 2, 2 * j + 3, 1, j)
        for s, back, lead, prep in steps_end:
            step(back, lead, prep, s % 2, s // 2)

    with nc.Block() as block:

        @block.sync
        def _(sp):
            def load(b, par):
                wait(sp, s_prep, len(PREP) * (b - 2) + KT)
                sp.dma_start(ctx_nat[par][:, 0:FULL, :],
                             arg["ctx"][bass.ds(b, 1), 0:FULL * P, :].rearrange("a (p t) e -> p (a t) e", t=FULL)
                             ).then_inc(s_ctx[par], 16)
                sp.dma_start(ctx_nat[par][0:TAIL, FULL, :],
                             arg["ctx"][bass.ds(b, 1), FULL * P:NCTX, :].rearrange("a p e -> (a p) e")
                             ).then_inc(s_ctx[par], 16)
                wait(sp, s_abs, b)
                for k, pair in enumerate(wnames):
                    for i, n in enumerate(pair):
                        sp.dma_start(w_raw[:, k, i, :], flat[n][:, bass.ds(b * PIECE, PIECE)]).then_inc(s_raw, 16)

            load(0, 0)
            load(1, 1)
            with sp.Fori(1, BATCH // 2) as j:
                load(2 * j, 0)
                load(2 * j + 1, 1)

        @block.gpsimd
        def _(pool):
            def step(back, lead, prep, par, pair):
                if prep is None:
                    return
                pool.wait_ge(s_raw, 96 * (prep + 1))
                if isinstance(prep, int) and prep == 0:
                    pool.wait_ge(s_zero, 1)
                for k in range(3):
                    pool.tensor_tensor(w_raw[:, k, 0, :], w_raw[:, k, 0, :], w_raw[:, k, 1, :],
                                       ALU.subtract).then_inc(s_diff, 1)
                natural = PREP.index(("natural", 0))
                pool.wait_ge(s_pdve, DVE_PREPS * prep + natural + 1 - sum(PREP_ON_ACT[:natural + 1]))
                stand_alone(pool, core)
                wait(pool, s_prep, len(PREP) * prep)
                hi = c_stack[:, :, 0:LKV]
                pool.tensor_tensor(hi.bitcast(F32R), c_stage[:, :, :],
                                   zero[:, 0:1].unsqueeze(2).to_broadcast([P, KT, LKV]), ALU.add).then_inc(s_part, 1)
                stand_alone(pool, core)
                pool.wait_ge(s_part, 3 * prep + 1)
                pool.tensor_tensor(c_stack[:, :, LKV:2 * LKV], c_stage[:, :, :], hi, ALU.subtract).then_inc(s_part, 1)
                pool.tensor_copy(c_stack[:, :, 2 * LKV:SHIFT], hi).then_inc(s_part, 1)
                stand_alone(pool, core)
                wait(pool, s_sb, KT * (prep - 1))
                pool.tensor_copy(q_now[par][0:SHIFT, :].rearrange("p (h n) -> p h n", h=XH),
                                 q_t[:, bass.ds(prep, 1), :, :].rearrange("p a h n -> p (a h) n")
                                 ).then_inc(s_qnow, 1)
                stand_alone(pool, core)
                wait(pool, s_pv, KT * (prep - 1))
                pool.tensor_copy(c_nat[:, par, :, 0:LKV], c_stage[:, :, :]).then_inc(s_cnat, 1)

            pool.memset(zero[:, :], 0.0).then_inc(s_zero, 1)
            run(pool, step)

        @block.tensor
        def _(pe):
            def prep_item(b, par, n):
                kind, t = PREP[n]
                prep_out_wait(pe, b, n)
                if kind == "turn":
                    if t == 0:
                        pe.wait_ge(s_ctx[par], 16 * b + (32 if par == 0 else 16))
                    rows = rows_of(t)
                    for c in range(DC):
                        mm = pe.transpose(psum[:, 7, c * P:c * P + rows], ctx_nat[par][0:rows, t, c * P:(c + 1) * P],
                                          core.ident[0:rows, 0:rows])
                elif kind == "compress":
                    for c in range(DC):
                        for g in range(GROUPS):
                            pe.matmul(psum[g * LKV:(g + 1) * LKV, 7, 0:MAIN], w["wkv_d"][:, c, :],
                                      ctx_t[:, c, g * MAIN:(g + 1) * MAIN], start=(c == 0), stop=(c == DC - 1))
                    for c in range(DC):
                        mm = pe.matmul(psum[0:LKV, 7, MAIN:MAIN + TAIL], w["wkv_d"][:, c, :],
                                       ctx_t[:, c, FULL * P:NCTX], start=(c == 0), stop=(c == DC - 1))
                elif kind == "natural":
                    for i in range(PER_GROUP):
                        pe.transpose(psum[:, 7, i * P:(i + 1) * P], c_parts[:, i * P:(i + 1) * P], core.ident[:, :])
                    mm = pe.transpose(psum[0:TAIL, 7, MAIN:MAIN + LKV], c_parts[0:LKV, MAIN:MAIN + TAIL],
                                      core.ident[0:LKV, 0:LKV])
                else:
                    pe.wait_ge(s_part, 3 * (b + 1))
                    for i, tile in enumerate(stack_tiles(t)):
                        rows = rows_of(tile)
                        mm = pe.transpose(psum[0:STACK, 7, i * P:i * P + rows], c_stack[0:rows, tile, 0:STACK],
                                          core.ident[0:rows, 0:rows])
                mm.then_inc(s_prep, 1)

            def max_scores(b, par, i):
                qt, half = divmod(i, 2)
                wait(pe, s_max, 2 * QTILES * b + i - 1)
                if i == 0:
                    prep_out_wait(pe, b, len(PREP))
                    pe.wait_ge(s_qnow, b + 1)
                    wait(pe, s_shift, b)
                lhs = q_now[par][0:SHIFT, qt * P:(qt + 1) * P]
                for n, k0 in enumerate(range(half * 2 * BANK, min((half + 1) * 2 * BANK, NCTX), BANK)):
                    width = min(BANK, NCTX + 1 - k0)
                    mm = pe.matmul(psum[:, 2 * half + n, 0:width], lhs, c_t[0:SHIFT, par, k0:k0 + width],
                                   start=True, stop=True)
                mm.then_inc(s_sa, 1)

            def turn_max(b):
                pe.wait_ge(s_neg, b + 1)
                for qt in range(QTILES):
                    mm = pe.transpose(psum[0:STACK, qt // 4, (qt % 4) * P:(qt % 4 + 1) * P], max_row[:, qt, :],
                                      core.ident[:, :])
                mm.then_inc(s_mt, 1)

            def scores(b, par, t):
                wait(pe, s_exp, KT * b + t)
                if t == 0:
                    wait(pe, s_mix, b)
                    pe.wait_ge(s_shift, b + 1)
                lhs = c_t[0:STACK, par, t * P:t * P + rows_of(t)]
                for half in range(2):
                    mm = pe.matmul(psum[0:rows_of(t), 4 + half, :], lhs,
                                   q_now[par][0:STACK, half * BANK:(half + 1) * BANK], start=True, stop=True)
                mm.then_inc(s_sb, 1)

            def values(b, par, t):
                pe.wait_ge(s_exp, KT * b + t + 1)
                if t == 0:
                    pe.wait_ge(s_cnat, b + 1)
                    wait(pe, s_u, b)
                for half in range(2):
                    mm = pe.matmul(psum[half * UW:(half + 1) * UW, 6, :], c_nat[0:rows_of(t), par, t, :],
                                   probs[t % 2][0:rows_of(t), half * BANK:(half + 1) * BANK],
                                   start=(t == 0), stop=(t == KT - 1))
                mm.then_inc(s_pv, 1)

            def mix(b, par):
                stand_alone(pe, core)
                pe.wait_ge(s_u, b + 1)
                for h in range(XH):
                    base = UW * (h // 8)
                    cols = slice((h % 8) * SEQ, (h % 8 + 1) * SEQ)
                    mm = pe.matmul(psum[par * SEQ:(par + 1) * SEQ, 4 + h // 8, (h % 8) * OW:(h % 8 + 1) * OW],
                                   u_t[base:base + LKV + 1, cols], w["wv_u"][base:base + LKV + 1, h, :],
                                   start=True, stop=True)
                mm.then_inc(s_o, 1)

            def step(back, lead, prep, par, pair):
                for slot in range(KT):
                    if back is not None:
                        scores(back, par, slot)
                    if prep is not None:
                        for n, at in enumerate(PREP_SLOT):
                            if at == slot:
                                prep_item(prep, par, n)
                    if lead is not None:
                        for i, at in enumerate(MAX_SLOT):
                            if at == slot:
                                max_scores(lead, 1 - par, i)
                    if back is not None and slot > 0:
                        values(back, par, slot - 1)
                if lead is not None:
                    turn_max(lead)
                if back is not None:
                    values(back, par, KT - 1)
                    mix(back, par)

            run(pe, step)

        def prep_out(eng, on_act, b, par, n):
            kind, t = PREP[n]
            done = s_pact if on_act else s_pdve

            def copy(dst, src):
                return eng.activation(dst, src, ACT.Copy) if on_act else eng.tensor_copy(dst, src)

            eng.wait_ge(s_prep, len(PREP) * b + n + 1)
            if kind == "turn":
                rows = rows_of(t)
                copy(ctx_t[:, :, t * P:t * P + rows],
                     psum[:, 7, :].rearrange("p (c r) -> p c r", c=DC)[:, :, 0:rows]).then_inc(done, 1)
            elif kind == "compress":
                copy(c_parts[:, 0:MAIN], psum[:, 7, 0:MAIN])
                copy(c_parts[0:LKV, MAIN:MAIN + TAIL], psum[0:LKV, 7, MAIN:MAIN + TAIL]).then_inc(done, 1)
            elif kind == "natural":
                wait(eng, s_cnat, b)
                copy(c_stage[:, 0:FULL, :].rearrange("p (g i) l -> p i g l", g=GROUPS),
                     psum[:, 7, 0:MAIN].rearrange("p (i g l) -> p i g l", i=PER_GROUP, g=GROUPS))
                copy(c_stage[0:TAIL, FULL, :], psum[0:TAIL, 7, MAIN:MAIN + LKV]).then_inc(done, 1)
            else:
                tiles = stack_tiles(t)
                width = sum(rows_of(x) for x in tiles)
                wait(eng, s_sb, KT * (b - 2) + tiles[-1] + 1)
                copy(c_t[0:STACK, par, t * BANK:t * BANK + width], psum[0:STACK, 7, 0:width]).then_inc(done, 1)

        @block.scalar
        def _(act):
            def step(back, lead, prep, par, pair):
                for slot in range(KT):
                    if back is not None:
                        rows = rows_of(slot)
                        act.wait_ge(s_sb, KT * back + slot + 1)
                        wait(act, s_pv, KT * back + (slot - 1 if slot else 0))
                        act.activation(probs[slot % 2][0:rows, :].rearrange("p (a n) -> p a n", a=2),
                                       psum[0:rows, 4:6, :], ACT.Exp, scale=XSCALE).then_inc(s_exp, 1)
                    if prep is not None:
                        for n, at in enumerate(PREP_SLOT):
                            if at == slot and PREP_ON_ACT[n]:
                                prep_out(act, True, prep, par, n)
                if lead is not None:
                    act.wait_ge(s_mt, lead + 1)
                    act.activation(q_now[1 - par][SHIFT:STACK, :].rearrange("p (a n) -> p a n", a=2),
                                   psum[SHIFT:STACK, 0:2, :], ACT.Copy).then_inc(s_shift, 1)

            run(act, step)

        @block.vector
        def _(dve):
            def take_max(b, i):
                qt, half = divmod(i, 2)
                width = 2 * BANK if half == 0 else NCTX - 2 * BANK
                dve.wait_ge(s_sa, 2 * QTILES * b + i + 1)
                if i == 0:
                    wait(dve, s_neg, b)
                dve.tensor_reduce(max_half[:, qt, half:half + 1],
                                  psum[:, 2 * half:2 * half + 2, :].rearrange("p a n -> p (a n)")[:, 0:width],
                                  AX.X, ALU.max).then_inc(s_max, 1)

            def step(back, lead, prep, par, pair):
                for slot in range(KT):
                    if prep is not None:
                        for n, at in enumerate(PREP_SLOT):
                            if at == slot and not PREP_ON_ACT[n]:
                                prep_out(dve, False, prep, par, n)
                    if lead is not None:
                        for i, at in enumerate(MAX_SLOT):
                            if at == slot:
                                take_max(lead, i)
                if lead is not None:
                    dve.wait_ge(s_max, 2 * QTILES * (lead + 1))
                    wait(dve, s_mt, lead)
                    dve.tensor_reduce(max_row[:, :, SHIFT], max_half[:, :, :], AX.X, ALU.max,
                                      negate=True).then_inc(s_neg, 1)
                if back is not None:
                    dve.wait_ge(s_pv, KT * (back + 1))
                    wait(dve, s_o, back)
                    dve.tensor_copy(u_t[:, :], psum[:, 6, :]).then_inc(s_u, 1)
                if prep is not None:
                    dve.wait_ge(s_diff, 3 * (prep + 1))
                    dve.tensor_reduce(core.abs_sum[:, bass.ds(prep, 1), :].rearrange("p a k -> p (a k)"),
                                      w_raw[:, :, 0, :], AX.X, ALU.add,
                                      apply_absolute_value=True).then_inc(s_abs, 1)
                if back is not None:
                    half_rows = slice(par * SEQ, (par + 1) * SEQ)
                    out = psum[half_rows, 4:6, 0:8 * OW].rearrange("p a (h w) -> p a h w", h=8)
                    dve.wait_ge(s_o, back + 1)
                    dve.reciprocal(rden[half_rows, :].rearrange("p (a h) -> p a h", a=2),
                                   out[:, :, :, XHD]).then_inc(s_rd, 1)
                    dve.wait_ge(s_rd, back + 1)
                    mixed_v = mixed[half_rows, :, :]
                    for a in range(2):
                        mm = dve.tensor_tensor(mixed_v[:, 8 * a:8 * a + 8, :], out[:, a, :, 0:XHD],
                                               rden[half_rows, 8 * a:8 * a + 8].unsqueeze(2).to_broadcast(
                                                   [SEQ, 8, XHD]), ALU.mult)
                    mm.then_inc(s_mix, 1)
                    dve.wait_ge(s_mix, back + 1)
                    row = core.x[half_rows, bass.ds(pair, 1), :].rearrange("p a e -> p (a e)")
                    dve.tensor_tensor(row, row, mixed_v.rearrange("p h d -> p (h d)"), ALU.add).then_inc(s_x, 1)

            run(dve, step)
            dve.wait_ge(s_x, BATCH)


def rotated_keys(core, own, k_sel, xe, k_high, k_low, v_new):
    nc, arg, psum = core.nc, core.arg, core.psum
    kv_nat = [core.sb(f"kv_weight{i}", [P, 2, DIM], ctx=own) for i in range(2)]
    kv_t = core.sb("kv_weight_t", [P, 2, DC, P], ctx=own)
    k_group = core.sb("k_group", [P, ST, HD], ctx=own)
    new_t = core.sb("new_key_t", [P, SEQ], ctx=own)
    keys_t = core.sb("keys_t", [P, KEYS], ctx=own)
    s_w = [core.sem(f"kv_weight_in{i}", own) for i in range(2)]
    s_kg = core.sem("group_keys_placed", own)
    s_tr = core.sem("kv_weight_turned", own)
    s_sel = core.sem("group_keys_turned", own)
    s_kt = core.sem("key_weight_copied", own)
    s_vt = core.sem("value_weight_copied", own)
    s_new = core.sem("new_key_done", own)
    s_vnew = core.sem("new_value_done", own)
    s_newsb = core.sem("new_key_copied", own)
    s_vsb = core.sem("new_value_copied", own)
    s_rot = core.sem("new_key_rotated", own)
    s_selsb = core.sem("group_keys_copied", own)
    s_rotsb = core.sem("rotated_copied", own)
    s_back = core.sem("rotated_back", own)
    s_hi = core.sem("keys_high_done", own)
    s_lo = core.sem("keys_low_done", own)

    with nc.Block() as block:

        @block.sync
        def _(sp):
            def load(g, par):
                wait(sp, s_tr, g - 1)
                rows = bass.ds(g * HD, HD)
                sp.dma_start(kv_nat[par][:, 0, :], arg["wk"][rows, :]).then_inc(s_w[par], 16)
                sp.dma_start(kv_nat[par][:, 1, :], arg["wv"][rows, :]).then_inc(s_w[par], 16)

            load(0, 0)
            load(1, 1)
            with sp.Fori(1, NKV // 2) as j:
                load(2 * j, 0)
                load(2 * j + 1, 1)

        @block.gpsimd
        def _(pool):
            pool.wait_ge(core.cache_in, 2 * TOPK * 16)
            pool.tensor_copy(k_group[:, :, :], k_sel[:, :, 0:HD]).then_inc(s_kg, 1)
            with pool.Fori(1, NKV) as g:
                pool.wait_ge(s_sel, g)
                pool.tensor_copy(k_group[:, :, :], k_sel[:, :, bass.ds(g * HD, HD)]).then_inc(s_kg, 1)

        @block.tensor
        def _(pe):
            def group(g, par):
                pe.wait_ge(s_w[par], 16 * g + (32 if par == 0 else 16))
                wait(pe, s_kt, g)
                wait(pe, s_vt, g)
                for k in range(2):
                    for c in range(DC):
                        mm = pe.transpose(psum[:, k, c * P:(c + 1) * P], kv_nat[par][:, k, c * P:(c + 1) * P],
                                          core.ident[:, :])
                mm.then_inc(s_tr, 1)
                pe.wait_ge(s_kg, g + 1)
                wait(pe, s_selsb, g)
                for t in range(ST):
                    mm = pe.transpose(psum[:, 2, t * P:(t + 1) * P], k_group[:, t, :], core.ident[:, :])
                mm.then_inc(s_sel, 1)
                pe.wait_ge(s_kt, g + 1)
                wait(pe, s_newsb, g)
                for c in range(DC):
                    mm = pe.matmul(psum[:, 3, 0:SEQ], kv_t[:, 0, c, :], xe[:, c, :], start=(c == 0), stop=(c == DC - 1))
                mm.then_inc(s_new, 1)
                pe.wait_ge(s_vt, g + 1)
                wait(pe, s_vsb, g)
                for c in range(DC):
                    mm = pe.matmul(psum[0:SEQ, 4, 0:P], xe[:, c, :], kv_t[:, 1, c, :],
                                   start=(c == 0), stop=(c == DC - 1))
                mm.then_inc(s_vnew, 1)
                pe.wait_ge(s_newsb, g + 1)
                wait(pe, s_rotsb, g)
                pe.matmul(psum[:, 5, 0:SEQ], core.rope_t[:, :], new_t[:, :], start=True, stop=True).then_inc(s_rot, 1)
                pe.wait_ge(s_selsb, g + 1)
                wait(pe, s_lo, 2 * g)
                pe.matmul(psum[:, 6, :], core.rope[:, :], keys_t[:, 0:NSEL], start=True, stop=True).then_inc(s_back, 1)
                pe.wait_ge(s_rotsb, g + 1)
                pe.matmul(psum[:, 7, 0:SEQ], core.rope[:, :], keys_t[:, NSEL:KEYS],
                          start=True, stop=True).then_inc(s_back, 1)

            with pe.Fori(0, NKV // 2) as j:
                group(2 * j, 0)
                group(2 * j + 1, 1)

        @block.scalar
        def _(act):
            with act.Fori(0, NKV) as g:
                act.wait_ge(s_tr, g + 1)
                act.activation(kv_t[:, 0, :, :], psum[:, 0, :].rearrange("p (c t) -> p c t", c=DC),
                               ACT.Copy).then_inc(s_kt, 1)
                act.wait_ge(s_sel, g + 1)
                act.activation(keys_t[:, 0:NSEL], psum[:, 2, :], ACT.Copy).then_inc(s_selsb, 1)
                act.wait_ge(s_vnew, g + 1)
                act.activation(v_new[0:SEQ, bass.ds(g, 1), :].rearrange("p a d -> p (a d)"),
                               psum[0:SEQ, 4, 0:P], ACT.Copy).then_inc(s_vsb, 1)
                for n, (keys, src) in enumerate(((bass.ds(g * KEYS, NSEL), psum[:, 6, :]),
                                                 (bass.ds(g * KEYS + NSEL, SEQ), psum[:, 7, 0:SEQ]))):
                    act.wait_ge(s_back, 2 * g + n + 1)
                    act.activation(k_high[:, keys], src, ACT.Copy, scale=GSCALE).then_inc(s_hi, 1)

        @block.vector
        def _(dve):
            with dve.Fori(0, NKV) as g:
                dve.wait_ge(s_tr, g + 1)
                dve.tensor_copy(kv_t[:, 1, :, :], psum[:, 1, :].rearrange("p (c t) -> p c t", c=DC)).then_inc(s_vt, 1)
                dve.wait_ge(s_new, g + 1)
                dve.tensor_copy(new_t[:, :], psum[:, 3, 0:SEQ]).then_inc(s_newsb, 1)
                dve.wait_ge(s_rot, g + 1)
                dve.tensor_copy(keys_t[:, NSEL:KEYS], psum[:, 5, 0:SEQ]).then_inc(s_rotsb, 1)
                for n, (keys, src) in enumerate(((bass.ds(g * KEYS, NSEL), psum[:, 6, :]),
                                                 (bass.ds(g * KEYS + NSEL, SEQ), psum[:, 7, 0:SEQ]))):
                    dve.wait_ge(s_hi, 2 * g + n + 1)
                    dve.scalar_tensor_tensor(out=k_low[:, keys], in0=src, scalar=GSCALE, in1=k_high[:, keys],
                                             op0=ALU.mult, op1=ALU.subtract).then_inc(s_lo, 1)
            dve.wait_ge(s_lo, 2 * NKV)


HEAD_FIRST_USE = (0, 10, 16, 22)


def turn_use(g, i, k, this=True, nxt=True):
    late = 0 if nxt else 1 if this else 2
    bank = 4 + (k + 1 + late) % 2
    if isinstance(g, int) and g == 0 and i == 0:
        return (1 if k == 0 else 2), bank
    return 28 * g + HEAD_FIRST_USE[i] + k - 7 - late, bank


def grouped_attention(core, own, xh, xl, k_high, k_low, v_sel, v_new):
    nc, arg, psum = core.nc, core.arg, core.psum
    wq_nat = core.sb("wq_nat", [P, REP, DIM], ctx=own)
    wo_nat = core.sb("wo_nat", [P, REP, DC, HD], ctx=own)
    wq_t = [core.sb(f"wq_t_{s}", [P, DC, HD], F32R, ctx=own) for s in ("high", "low")]
    wo_t = [core.sb(f"wo_t_{s}", [P, REP, DIM], F32R, ctx=own) for s in ("high", "low")]
    q_t = [core.sb(f"query_t_{s}", [P, TOK], F32R, ctx=own) for s in ("high", "low")]
    value = [core.sb(f"value_{s}", [P, ST + 1, HD], F32R, ctx=own) for s in ("high", "low")]
    probs = core.sb("head_probs", [P, TT, KEYS], ctx=own)
    probs_t = [core.sb(f"probs_t_{s}", [P, ST + 1, TOK], F32R, ctx=own) for s in ("high", "low")]
    mixed_t = [core.sb(f"mixed_t_{s}", [P, REP, TOK], F32R, ctx=own) for s in ("high", "low")]
    neg_max = core.sb("neg_max", [P, TT], ctx=own)
    den = core.sb("den", [P, TT], ctx=own)
    rden = core.sb("inverse_den", [P, TT], ctx=own)
    names = {
        "wqt": "query_weight_turned",
        "wot": "output_weight_turned", "q": "queries_done", "qh": "queries_high_done", "ql": "queries_low_done",
        "s": "head_scores_done", "max": "head_max_done", "exp": "head_probs_done", "rd": "head_den_inverted",
        "norm": "head_probs_scaled", "pt": "head_probs_turned", "th": "turned_high_done", "tl": "turned_low_done",
        "tailh": "tail_high_done", "taill": "tail_low_done", "wqh": "query_weight_high_done",
        "woh": "output_weight_high_done", "vh": "value_high_done", "vl": "value_low_done", "pv": "head_mix_done",
        "ah": "mix_high_done", "al": "mix_low_done", "o": "output_tile_done",
    }
    s = {k: core.sem(v, own) for k, v in names.items()}
    wq_in = [core.sem(f"query_weight_in{i}", own) for i in range(REP)]
    wo_in = [core.sem(f"output_weight_in{i}", own) for i in range(REP)]

    def run(eng, head):
        for i in range(REP):
            head(0, i, True, i > 0, True)
        with eng.Fori(1, NKV - 1) as g:
            for i in range(REP):
                head(g, i, True, True, True)
        for i in range(REP):
            head(NKV - 1, i, True, True, i < REP - 1)
        head(NKV, 0, False, True, False)

    with nc.Block() as block:

        @block.sync
        def _(sp):
            def load_q(g, i):
                wait(sp, s["wqt"], REP * (g - 1) + i + 1)
                sp.dma_start(wq_nat[:, i, :], arg["wq"][bass.ds(g * (REP * HD) + i * HD, HD), :]).then_inc(wq_in[i], 16)

            def load_o(g, i):
                stand_alone(sp, core)
                wait(sp, s["wot"], REP * (g - 1) + i + 1)
                sp.dma_start(wo_nat[:, i, :, :],
                             arg["wo"].rearrange("(c o) n -> o c n", o=P)[:, :, bass.ds(g * (REP * HD) + i * HD, HD)]
                             ).then_inc(wo_in[i], 16)

            for i in range(REP):
                load_q(0, i)
                load_o(0, i)
            with sp.Fori(1, NKV) as g:
                for i in range(REP):
                    load_q(g, i)
                    load_o(g, i)

        @block.tensor
        def _(pe):
            def use_bank(use):
                before, bank = use
                wait(pe, s["tl"], before - 1)
                return psum[:, bank, :]

            def queries(n):
                for step, (a, b) in enumerate(PASSES):
                    for c in range(DC):
                        mm = pe.matmul(psum[:, 7, :], wq_t[a][:, c, :], (xh, xl)[b][:, c, :],
                                       start=(step == 0 and c == 0), stop=(step == 2 and c == DC - 1))
                mm.then_inc(s["q"], 1)

            def score(g, n, qt):
                wait(pe, s["exp"], TT * n + qt - 1)
                if qt == 0:
                    pe.wait_ge(s["ql"], n + 1)
                for k0, width, bank in ((0, NSEL, 2 * (qt % 2)), (NSEL, SEQ, 2 * (qt % 2) + 1)):
                    keys = bass.ds(g * KEYS + k0, width)
                    for step, (a, b) in enumerate(PASSES):
                        mm = pe.matmul(psum[:, bank, 0:width], q_t[a][:, qt * P:(qt + 1) * P],
                                       (k_high, k_low)[b][:, keys], start=(step == 0), stop=(step == 2))
                mm.then_inc(s["s"], 1)

            def turn_probs(bank, last, qt):
                pe.wait_ge(s["norm"], TT * last + qt + 1)
                if qt == 0:
                    wait(pe, s["al"], last)
                for t in range(ST):
                    pe.transpose(bank[:, t * P:(t + 1) * P], probs[:, qt, t * P:(t + 1) * P], core.ident[:, :])
                pe.transpose(psum[0:SEQ, 6, qt * P:(qt + 1) * P], probs[:, qt, NSEL:KEYS],
                             core.ident[:, :]).then_inc(s["pt"], 1)

            def mix(last):
                pe.wait_ge(s["taill"], last + 1)
                pe.wait_ge(s["vl"], 2 * ((last // REP) + 1) if isinstance(last, int) else vl_at[0])
                for step, (a, b) in enumerate(PASSES):
                    for t in range(ST + 1):
                        rows = P if t < ST else SEQ
                        mm = pe.matmul(psum[:, 6, :], value[a][0:rows, t, :], probs_t[b][0:rows, t, :],
                                       start=(step == 0 and t == 0), stop=(step == 2 and t == ST))
                mm.then_inc(s["pv"], 1)

            def output(g, qt, bank):
                wait(pe, s["al"], REP * g)
                for i in range(REP):
                    for step, (a, b) in enumerate(PASSES):
                        mm = pe.matmul(bank, mixed_t[a][:, i, qt * P:(qt + 1) * P], wo_t[b][:, i, :],
                                       start=(i == 0 and step == 0), stop=(i == REP - 1 and step == 2))
                mm.then_inc(s["o"], 1)

            vl_at = [None]

            def head(g, i, this, last, nxt):
                n = REP * g + i
                vl_at[0] = 2 * g + (2 if i else 0)
                if nxt:
                    weight = turn_use(g, i, 0)
                    bank = use_bank(weight)
                    j = (i + 1) % REP
                    pe.wait_ge(wq_in[j], 16 * (g + (2 if j == 0 else 1)))
                    for c in range(DC):
                        mm = pe.transpose(bank[:, c * P:(c + 1) * P], wq_nat[:, j, c * P:(c + 1) * P], core.ident[:, :])
                    mm.then_inc(s["wqt"], 1)
                for qt in range(TT):
                    if this:
                        score(g, n, qt)
                    if last:
                        turn_probs(use_bank(turn_use(g, i, 1 + qt, this, nxt)), n - 1, qt)
                if nxt:
                    pe.wait_ge(s["tl"], weight[0] + 1)
                    queries(n + 1)
                if last:
                    mix(n - 1)
                if i == 0 and last:
                    for qt in range(TT):
                        output(g, qt, use_bank(turn_use(g, 0, 5 + qt, this, nxt)))
                if this:
                    bank = use_bank(turn_use(g, i, 9 if i == 0 else 5, this, nxt))
                    pe.wait_ge(wo_in[i], 16 * (g + 1))
                    for c in range(DC):
                        mm = pe.transpose(bank[:, c * P:(c + 1) * P], wo_nat[:, i, c, :], core.ident[:, :])
                    mm.then_inc(s["wot"], 1)

            pe.wait_ge(wq_in[0], 16)
            for c in range(DC):
                mm = pe.transpose(psum[:, 4, c * P:(c + 1) * P], wq_nat[:, 0, c * P:(c + 1) * P], core.ident[:, :])
            mm.then_inc(s["wqt"], 1)
            pe.wait_ge(s["tl"], 1)
            queries(0)
            run(pe, head)

        @block.scalar
        def _(act):
            def weight_high(done, count, bank, dst):
                act.wait_ge(done, count)
                act.activation(dst, psum[:, bank, :], ACT.Copy).then_inc(s["th"], 1)

            def queries_high(n):
                act.wait_ge(s["q"], n + 1)
                act.activation(q_t[0][:, :], psum[:, 7, :], ACT.Copy).then_inc(s["qh"], 1)

            def head(g, i, this, last, nxt):
                n = REP * g + i
                if nxt:
                    weight_high(s["wqt"], n + 2, turn_use(g, i, 0)[1], wq_t[0][:, :, :].rearrange("p c d -> p (c d)"))
                for qt in range(TT):
                    if this:
                        act.wait_ge(s["max"], TT * n + qt + 1)
                        wait(act, s["pt"], TT * (n - 1) + qt + 1)
                        act.activation(probs[:, qt, :],
                                       psum[:, 2 * (qt % 2):2 * (qt % 2) + 2, :].rearrange("p a k -> p (a k)")[:, 0:KEYS],
                                       ACT.Exp, bias=neg_max[:, qt:qt + 1],
                                       accum_out=den[:, qt:qt + 1]).then_inc(s["exp"], 1)
                    if last:
                        act.wait_ge(s["pt"], TT * (n - 1) + qt + 1)
                        act.activation(probs_t[0][:, 0:ST, qt * P:(qt + 1) * P],
                                       psum[:, turn_use(g, i, 1 + qt, this, nxt)[1], :].rearrange("p (t q) -> p t q", t=ST),
                                       ACT.Copy).then_inc(s["th"], 1)
                if last:
                    act.activation(probs_t[0][0:SEQ, ST, :], psum[0:SEQ, 6, :], ACT.Copy).then_inc(s["tailh"], 1)
                if nxt:
                    queries_high(n + 1)
                if last:
                    act.wait_ge(s["pv"], n)
                    act.activation(mixed_t[0][:, (i - 1) % REP, :], psum[:, 6, :], ACT.Copy).then_inc(s["ah"], 1)
                if this:
                    weight_high(s["wot"], n + 1, turn_use(g, i, 9 if i == 0 else 5, this, nxt)[1], wo_t[0][:, i, :])

            weight_high(s["wqt"], 1, 4, wq_t[0][:, :, :].rearrange("p c d -> p (c d)"))
            queries_high(0)
            run(act, head)

        @block.vector
        def _(dve):
            def high_count(g, i, k, this=True, nxt=True):
                if isinstance(g, int) and g == 0 and i == 0:
                    return 2 if k == 0 else 3
                outputs_to_come = TT if i == 0 and k < 5 else 0
                late = 0 if nxt else 1 if this else 2
                return 24 * g + HEAD_FIRST_USE[i] + k - 6 + outputs_to_come - late

            def weight_low(count, bank, dst, high):
                dve.wait_ge(s["th"], count)
                dve.tensor_tensor(dst, psum[:, bank, :], high, ALU.subtract).then_inc(s["tl"], 1)

            def queries_low(n):
                dve.wait_ge(s["qh"], n + 1)
                dve.tensor_tensor(q_t[1][:, :], psum[:, 7, :], q_t[0][:, :], ALU.subtract).then_inc(s["ql"], 1)

            def values_low(g):
                dve.wait_ge(s["vh"], 2 * g + 2)
                dve.tensor_tensor(value[1][:, 0:ST, :], v_sel[:, :, bass.ds(g * HD, HD)], value[0][:, 0:ST, :],
                                  ALU.subtract).then_inc(s["vl"], 1)
                dve.tensor_tensor(value[1][0:SEQ, ST, :], v_new[0:SEQ, bass.ds(g, 1), :].rearrange("p a d -> p (a d)"),
                                  value[0][0:SEQ, ST, :], ALU.subtract).then_inc(s["vl"], 1)

            def flat_wq(a):
                return wq_t[a][:, :, :].rearrange("p c d -> p (c d)")

            def after_exp(g, i, this, last, nxt, qt):
                n = REP * g + i
                if last:
                    dve.wait_ge(s["th"], high_count(g, i, 1 + qt, this, nxt))
                    dve.tensor_tensor(probs_t[1][:, 0:ST, qt * P:(qt + 1) * P],
                                      psum[:, turn_use(g, i, 1 + qt, this, nxt)[1], :].rearrange("p (t q) -> p t q", t=ST),
                                      probs_t[0][:, 0:ST, qt * P:(qt + 1) * P], ALU.subtract).then_inc(s["tl"], 1)
                if this:
                    dve.wait_ge(s["exp"], TT * n + qt + 1)
                    wait(dve, s["norm"], TT * (n - 1) + qt + 1)
                    dve.reciprocal(rden[:, qt:qt + 1], den[:, qt:qt + 1]).then_inc(s["rd"], 1)

            def head(g, i, this, last, nxt):
                n = REP * g + i
                if nxt:
                    weight_low(high_count(g, i, 0), turn_use(g, i, 0)[1], flat_wq(1), flat_wq(0))
                for qt in range(TT):
                    if this:
                        dve.wait_ge(s["s"], TT * n + qt + 1)
                        wait(dve, s["exp"], TT * (n - 1) + qt + 1)
                        dve.tensor_reduce(neg_max[:, qt:qt + 1],
                                          psum[:, 2 * (qt % 2):2 * (qt % 2) + 2, :].rearrange("p a k -> p (a k)")[:, 0:KEYS],
                                          AX.X, ALU.max, negate=True).then_inc(s["max"], 1)
                    if qt > 0:
                        after_exp(g, i, this, last, nxt, qt - 1)
                after_exp(g, i, this, last, nxt, TT - 1)
                if last:
                    dve.wait_ge(s["tailh"], n)
                    dve.tensor_tensor(probs_t[1][0:SEQ, ST, :], psum[0:SEQ, 6, :], probs_t[0][0:SEQ, ST, :],
                                      ALU.subtract).then_inc(s["taill"], 1)
                if nxt:
                    queries_low(n + 1)
                if last:
                    dve.wait_ge(s["ah"], n)
                    j = (i - 1) % REP
                    dve.tensor_tensor(mixed_t[1][:, j, :], psum[:, 6, :], mixed_t[0][:, j, :],
                                      ALU.subtract).then_inc(s["al"], 1)
                if i == 0 and last:
                    for qt in range(TT):
                        dve.wait_ge(s["o"], TT * (g - 1) + qt + 1)
                        dve.tensor_tensor(core.x[:, qt, :], psum[:, turn_use(g, 0, 5 + qt, this, nxt)[1], :],
                                          core.x[:, qt, :], ALU.add).then_inc(s["tl"], 1)
                if this:
                    k = 9 if i == 0 else 5
                    weight_low(high_count(g, i, k, this, nxt), turn_use(g, i, k, this, nxt)[1],
                               wo_t[1][:, i, :], wo_t[0][:, i, :])
                if this and i == 0:
                    values_low(g)

            weight_low(1, 4, flat_wq(1), flat_wq(0))
            queries_low(0)
            run(dve, head)
            dve.wait_ge(s["tl"], turn_use(NKV, 0, 1 + 2 * TT, False, False)[0])

        @block.gpsimd
        def _(pool):
            def values(g):
                pool.tensor_copy(value[0][:, 0:ST, :], v_sel[:, :, bass.ds(g * HD, HD)]).then_inc(s["vh"], 1)
                pool.tensor_copy(value[0][0:SEQ, ST, :],
                                 v_new[0:SEQ, bass.ds(g, 1), :].rearrange("p a d -> p (a d)")).then_inc(s["vh"], 1)

            def head(g, i, this, last, nxt):
                n = REP * g + i
                if not this:
                    return
                for qt in range(TT):
                    pool.wait_ge(s["rd"], TT * n + qt + 1)
                    pool.tensor_tensor(probs[:, qt, :], probs[:, qt, :], rden[:, qt:qt + 1].to_broadcast([P, KEYS]),
                                       ALU.mult).then_inc(s["norm"], 1)
                if i == 0:
                    wait(pool, s["pv"], n)
                    values(g)

            pool.wait_ge(core.cache_in, 2 * TOPK * 16)
            run(pool, head)


def feed_forward(core, own, xh, xl):
    nc, arg, psum = core.nc, core.arg, core.psum
    ones = core.sb("ones", [P, P], ctx=own)
    total = core.sb("abs_total", [P, 3], ctx=own)
    coeff = core.sb("coeff", [P, 3], ctx=own)
    raw = [core.sb(f"ffn_raw{i}", [P, 3, 2, DIM], ctx=own) for i in range(2)]
    diff = core.sb("ffn_diff", [P, 3, DIM], ctx=own)
    sign = [core.sb(f"ffn_sign{i}", [P, 3, DIM], ctx=own) for i in range(2)]
    quant = core.sb("ffn_quant", [P, 3, DIM], ctx=own)
    w_t = [core.sb(f"ffn_w_t_{s}", [P, 3, DIM], F32R, ctx=own) for s in ("high", "low")]
    gate = core.sb("gate", [P, TOK], ctx=own)
    hidden = core.sb("hidden", [P, TOK], ctx=own)
    hid = [core.sb(f"hidden_{s}", [P, TOK], F32R, ctx=own) for s in ("high", "low")]
    s_raw = [core.sem(f"ffn_raw_in{i}", own) for i in range(2)]
    s_ones = core.sem("ones_ready", own)
    s_tot = core.sem("abs_summed", own)
    s_all = core.sem("abs_spread", own)
    s_co = core.sem("coeff_ready", own)
    s_diff = core.sem("ffn_diff_done", own)
    s_sign = core.sem("ffn_sign_done", own)
    s_quant = [core.sem(f"ffn_quant_done{k}", own) for k in range(3)]
    s_turn = [core.sem(f"ffn_turned{k}", own) for k in range(3)]
    s_wh = [core.sem(f"ffn_high_done{k}", own) for k in range(3)]
    s_wl = [core.sem(f"ffn_low_done{k}", own) for k in range(3)]
    s_gu = [core.sem(f"gate_up_done{k}", own) for k in range(2)]
    s_silu = core.sem("silu_done", own)
    s_h = core.sem("hidden_done", own)
    s_hh = core.sem("hidden_high_done", own)
    s_hl = core.sem("hidden_low_done", own)
    s_d = core.sem("down_done", own)
    s_x = core.sem("final_sum_done", own)
    s_out = core.sem("out_written", own)
    turn_bank = (4, 5, 4)

    def run(eng, chunk):
        chunk(0, 0)
        chunk(1, 1)
        with eng.Fori(1, CH // 2 - 1) as j:
            chunk(2 * j, 0)
            chunk(2 * j + 1, 1)
        chunk(CH - 2, 0)
        chunk(CH - 1, 1)

    def within(c, ahead):
        return not isinstance(c, int) or c + ahead < CH

    with nc.Block() as block:

        @block.sync
        def _(sp):
            def load(c, par):
                wait(sp, s_quant[2], c - 1)
                wait(sp, s_quant[1], c - 1)
                for k, pair in enumerate((("w1", "mean_w1"), ("w3", "mean_w3"))):
                    for i, name in enumerate(pair):
                        sp.dma_start(raw[par][:, k, i, :], arg[name][bass.ds(c * P, P), :]).then_inc(s_raw[par], 16)
                for i, name in enumerate(("w2", "mean_w2")):
                    sp.dma_start(raw[par][:, 2, i, :].rearrange("p (o n) -> p o n", o=DC),
                                 arg[name].rearrange("(o p) n -> p o n", p=P)[:, :, bass.ds(c * P, P)]
                                 ).then_inc(s_raw[par], 16)

            run(sp, load)
            out = core.out.rearrange("b n e -> (b n) e").rearrange("(j p) e -> p j e", p=P)
            for j in range(TT):
                sp.wait_ge(s_x, j + 1)
                sp.dma_start(out[:, j, :], core.x[:, j, :]).then_inc(s_out, 16)
            sp.wait_ge(s_out, 16 * TT)

        @block.gpsimd
        def _(pool):
            def chunk(c, par):
                pool.wait_ge(s_raw[par], 48 * c + (96 if par == 0 else 48))
                wait(pool, s_sign, c)
                pool.tensor_tensor(diff[:, :, :], raw[par][:, :, 0, :], raw[par][:, :, 1, :],
                                   ALU.subtract).then_inc(s_diff, 1)

            pool.memset(ones[:, :], 1.0).then_inc(s_ones, 1)
            run(pool, chunk)

        @block.tensor
        def _(pe):
            def turn(c, k):
                bank = turn_bank[k]
                pe.wait_ge(s_quant[k], c + 1)
                if k == 0:
                    wait(pe, s_wl[2], c - 1)
                elif k == 1:
                    wait(pe, s_wl[1], c)
                else:
                    pe.wait_ge(s_wl[0], c + 2 if within(c, 1) else CH)
                for i in range(DC):
                    mm = pe.transpose(psum[:, bank, i * P:(i + 1) * P], quant[:, k, i * P:(i + 1) * P],
                                      core.ident[:, :])
                mm.then_inc(s_turn[k], 1)

            def gates(c, k):
                wait(pe, s_silu if k == 0 else s_h, c)
                pe.wait_ge(s_wl[k], c + 1)
                for step, (a, b) in enumerate(PASSES):
                    for i in range(DC):
                        mm = pe.matmul(psum[:, 6 + k, :], w_t[a][:, k, i * P:(i + 1) * P], (xh, xl)[b][:, i, :],
                                       start=(step == 0 and i == 0), stop=(step == 2 and i == DC - 1))
                mm.then_inc(s_gu[k], 1)

            def down(c):
                first, last = isinstance(c, int) and c == 0, isinstance(c, int) and c == CH - 1
                pe.wait_ge(s_hl, c + 1)
                pe.wait_ge(s_wl[2], c + 1)
                for qt in range(TT):
                    for step, (a, b) in enumerate(PASSES):
                        mm = pe.matmul(psum[:, qt, :], hid[a][:, qt * P:(qt + 1) * P], w_t[b][:, 2, :],
                                       start=(first and step == 0), stop=(last and step == 2),
                                       skip_group_check=True)
                mm.then_inc(s_d, 1)

            def chunk(c, par):
                gates(c, 0)
                gates(c, 1)
                if within(c, 1):
                    turn(c + 1, 0)
                    turn(c + 1, 1)
                if not (isinstance(c, int) and c == 0):
                    down(c - 1)
                turn(c, 2)

            pe.wait_ge(s_ones, 1)
            pe.wait_ge(s_tot, 1)
            pe.matmul(psum[:, 0, 0:3], ones[:, :], total[:, :], start=True, stop=True).then_inc(s_all, 1)
            pe.wait_ge(s_co, 1)
            turn(0, 0)
            turn(0, 1)
            run(pe, chunk)
            down(CH - 1)

        @block.scalar
        def _(act):
            def signs(c, par):
                act.wait_ge(s_diff, c + 1)
                wait(act, s_quant[2], c - 1)
                wait(act, s_quant[1], c - 1)
                act.activation(sign[par][:, :, :], diff[:, :, :], ACT.Sign).then_inc(s_sign, 1)

            def high(c, k):
                act.wait_ge(s_turn[k], c + 1)
                act.activation(w_t[0][:, k, :], psum[:, turn_bank[k], :], ACT.Copy).then_inc(s_wh[k], 1)

            def chunk(c, par):
                act.wait_ge(s_gu[0], c + 1)
                wait(act, s_h, c)
                act.activation(gate[:, :], psum[:, 6, :], ACT.Silu).then_inc(s_silu, 1)
                if within(c, 1):
                    high(c + 1, 0)
                    high(c + 1, 1)
                act.wait_ge(s_h, c + 1)
                wait(act, s_d, c)
                act.activation(hid[0][:, :], hidden[:, :], ACT.Copy).then_inc(s_hh, 1)
                high(c, 2)
                if within(c, 2):
                    signs(c + 2, par)

            signs(0, 0)
            high(0, 0)
            high(0, 1)
            signs(1, 1)
            run(act, chunk)

        @block.vector
        def _(dve):
            def quantise(c, par, k):
                dve.wait_ge(s_sign, c + 1)
                wait(dve, s_turn[k], c)
                dve.scalar_tensor_tensor(out=quant[:, k, :], in0=sign[par][:, k, :], scalar=coeff[:, k:k + 1],
                                         in1=raw[par][:, k, 1, :], op0=ALU.mult, op1=ALU.add).then_inc(s_quant[k], 1)

            def low(c, k):
                dve.wait_ge(s_wh[k], c + 1)
                dve.tensor_tensor(w_t[1][:, k, :], psum[:, turn_bank[k], :], w_t[0][:, k, :],
                                  ALU.subtract).then_inc(s_wl[k], 1)

            def chunk(c, par):
                dve.wait_ge(s_silu, c + 1)
                dve.wait_ge(s_gu[1], c + 1)
                wait(dve, s_hl, c)
                dve.tensor_tensor(hidden[:, :], psum[:, 7, :], gate[:, :], ALU.mult).then_inc(s_h, 1)
                if within(c, 1):
                    low(c + 1, 0)
                    low(c + 1, 1)
                dve.wait_ge(s_hh, c + 1)
                dve.tensor_tensor(hid[1][:, :], hidden[:, :], hid[0][:, :], ALU.subtract).then_inc(s_hl, 1)
                low(c, 2)
                if within(c, 2):
                    quantise(c + 2, par, 0)
                    quantise(c + 2, par, 1)
                if within(c, 1):
                    quantise(c + 1, 1 - par, 2)

            dve.tensor_reduce(total[:, :], core.abs_sum[:, :, :].rearrange("p b k -> p k b"), AX.X,
                              ALU.add).then_inc(s_tot, 1)
            dve.wait_ge(s_all, 1)
            dve.tensor_scalar(coeff[:, :], psum[:, 0, 0:3], 1.0 / WSIZE, None, ALU.mult).then_inc(s_co, 1)
            dve.wait_ge(s_co, 1)
            for k in range(3):
                quantise(0, 0, k)
            low(0, 0)
            low(0, 1)
            quantise(1, 1, 0)
            quantise(1, 1, 1)
            run(dve, chunk)
            dve.wait_ge(s_d, CH)
            for j in range(TT):
                dve.tensor_tensor(core.x[:, j, :], psum[:, j, :], core.x[:, j, :], ALU.add).then_inc(s_x, 1)


def layer(nc, out, **arg):
    with ExitStack() as ctx:
        core = Core(nc, ctx, arg, out)
        with ExitStack() as own:
            w = {
                "wkv_d": core.sb("wkv_d", [P, DC, LKV], ctx=own),
                "wv_u": core.sb("wv_u", [P, XH, OW], ctx=own),
                "c_nat": core.sb("c_nat", [P, 2, KT, UW], ctx=own),
                "c_stack": core.sb("c_stack", [P, KT, STACK], ctx=own),
                "c_stage": core.sb("c_stage", [P, KT, LKV], ctx=own),
                "c_t": core.sb("c_t", [P, 2, KT * P], F32R, ctx=own),
                "max_row": core.sb("max_row", [P, QTILES, STACK], ctx=own),
                "q_t": core.sb("q_t", [SHIFT, BATCH, XH, SEQ], F32R, ctx=own),
            }
            with ExitStack() as first:
                w["w_qk"] = core.sb("w_qk", [LQ, XH, 3, LKV], ctx=first)
                w["wq_d"] = core.sb("wq_d", [P, DC, LQ], ctx=first)
                xn_t = core.sb("xn_t", [P, DC, TOK], ctx=first)
                load_and_constants(core, w)
                layer_norm_t(core, "norm1", None, first, exact=xn_t, exact_tokens=TOK)
                cross_queries(core, w, xn_t)
            cross_attention(core, w, own)
        with ExitStack() as own:
            k_high = core.sb("k_high", [P, NKV * KEYS], F32R, ctx=own)
            k_low = core.sb("k_low", [P, NKV * KEYS], F32R, ctx=own)
            v_sel = core.sb("v_sel", [P, ST, NKV * HD], ctx=own)
            v_new = core.sb("v_new", [P, NKV, HD], ctx=own)
            xh = core.sb("attn_x_high", [P, DC, TOK], F32R, ctx=own)
            xl = core.sb("attn_x_low", [P, DC, TOK], F32R, ctx=own)
            with ExitStack() as first:
                k_sel = core.sb("k_sel", [P, ST, NKV * HD], ctx=first)
                xe = core.sb("new_tokens", [P, DC, SEQ], ctx=first)
                gather_cache(core, k_sel, v_sel)
                layer_norm_t(core, "norm2", (xh, xl), first, exact=xe, exact_tokens=SEQ)
                rotated_keys(core, first, k_sel, xe, k_high, k_low, v_new)
            grouped_attention(core, own, xh, xl, k_high, k_low, v_sel, v_new)
        with ExitStack() as own:
            xh = core.sb("ffn_x_high", [P, DC, TOK], F32R, ctx=own)
            xl = core.sb("ffn_x_low", [P, DC, TOK], F32R, ctx=own)
            layer_norm_t(core, "norm3", (xh, xl), own)
            feed_forward(core, own, xh, xl)


INPUTS = {
    "x": "x", "ctx": "ctx_4096", "Wq_d": "L0_xattn_Wq_d", "W_qk": "L0_xattn_W_qk", "Wkv_d": "L0_xattn_Wkv_d",
    "Wv_u": "L0_xattn_Wv_u", "cos": "L0_attn_freqs_cos", "sin": "L0_attn_freqs_sin", "wq": "L0_attn_wq",
    "wk": "L0_attn_wk", "wv": "L0_attn_wv", "wo": "L0_attn_wo", "k_cache": "L0_attn_k_cache",
    "v_cache": "L0_attn_v_cache", "block_idx": "L0_attn_block_idx", "w1": "L0_ffn_w1",
    "mean_w1": "L0_ffn_mean_w1", "w2": "L0_ffn_w2", "mean_w2": "L0_ffn_mean_w2", "w3": "L0_ffn_w3",
    "mean_w3": "L0_ffn_mean_w3",
}


def kernel(**inputs):
    import numpy as _np
    import concourse.bacc as _bacc
    from concourse import mybir as _mybir
    from concourse.bass_utils import run_bass_kernel_spmd as _run

    nc = _bacc.Bacc("TRN2", target_bir_lowering=False, num_devices=1)
    arrays, args = {}, {}
    for short, name in INPUTS.items():
        a = _np.ascontiguousarray(inputs[name])
        arrays[f"in_{name}_dram"] = a
        args[short] = nc.dram_tensor(f"in_{name}_dram", a.shape, _mybir.dt.from_np(a.dtype),
                                     kind="ExternalInput").ap()
    out = nc.dram_tensor("out_0_dram", (BATCH, SEQ, DIM), F32, kind="ExternalOutput").ap()
    layer(nc, out, **args)
    r = _run(nc, [arrays], core_ids=[0])
    return r.results[0]["out_0_dram"]
```

```python
from contextlib import ExitStack

import concourse.bass as bass
from concourse import mybir

F32 = mybir.dt.float32
F32R = mybir.dt.float32r
I32 = mybir.dt.int32
ALU = mybir.AluOpType
ACT = mybir.ActivationFunctionType
AX = mybir.AxisListType

P = 128
BANK = 512

BATCH, SEQ, DIM = 8, 64, 512
TOK = BATCH * SEQ
TT = TOK // P
DC = DIM // P
EPS = 1e-5

XH, LQ, LKV, XHD = 16, 64, 32, 32
NCTX = 1601
FULL = NCTX // P
TAIL = NCTX - FULL * P
KT = FULL + 1
XQ = XH * SEQ
QTILES = XQ // P
GROUPS = P // LKV
PER_GROUP = FULL // GROUPS
MAIN = PER_GROUP * P
SHIFT = 3 * LKV
STACK = SHIFT + 1
UW = 64
OW = XHD + 2
XSCALE = float(LKV) ** -0.5

NH, NKV, HD = 32, 8, 128
REP = NH // NKV
BLOCK, NBLK, TOPK = 32, 128, 16
NSEL = TOPK * BLOCK
ST = NSEL // P
KEYS = NSEL + SEQ
GSCALE = float(HD) ** -0.5

INTER = 1792
CH = INTER // P
SLOTS = 3
PASSES = ((0, 0), (0, 1), (1, 0))

WSIZE = INTER * DIM
PIECE = WSIZE // P // BATCH


def wait(eng, sem, count):
    if isinstance(count, int) and count <= 0:
        return
    eng.wait_ge(sem, count)


def stand_alone(eng, core):
    eng.wait_ge(core.first_stage, 1)


class Core:

    def __init__(self, nc, ctx, arg, out):
        self.nc, self.ctx, self.arg, self.out = nc, ctx, arg, out
        self.psum = ctx.enter_context(nc.psum_tensor("psum", [P, 8, BANK], F32))
        self.x = self.sb("x", [P, TT, DIM])
        self.ident = self.sb("ident", [P, P])
        self.rope = self.sb("rope", [P, P])
        self.rope_t = self.sb("rope_t", [P, P])
        self.abs_sum = self.sb("abs_sum", [P, BATCH, 3])
        self.cache = self.sb("cache", [P, 2, ST, NKV * HD])
        self.cache_in = self.sem("cache_in")
        self.ctx_in = [self.sem(f"ctx_in{i}") for i in range(2)]
        self.first_stage = self.sem("first_stage_reached")

    def sb(self, name, shape, dt=F32, ctx=None):
        return (ctx or self.ctx).enter_context(self.nc.sbuf_tensor(name, shape, dt))

    def sem(self, name, ctx=None):
        return (ctx or self.ctx).enter_context(self.nc.semaphore(name))


def layer_norm_t(core, name, parts, ctx, exact=None, exact_tokens=0, prefetch=None):
    nc = core.nc
    with ExitStack() as own:
        stats = core.sb(f"{name}_stats", [P, TT, 6], ctx=own)
        mean_var = core.sb(f"{name}_mean_var", [P, TT, 2], ctx=own)
        rstd = core.sb(f"{name}_rstd", [P, TT], ctx=own)
        normed = core.sb(f"{name}_normed", [P, TT, DIM], ctx=own)
        s_stats = core.sem(f"{name}_stats_done", own)
        s_agg = core.sem(f"{name}_moments_done", own)
        s_var = core.sem(f"{name}_variance_done", own)
        s_root = core.sem(f"{name}_root_done", own)
        s_rstd = core.sem(f"{name}_rstd_done", own)
        s_norm = core.sem(f"{name}_normed_done", own)
        s_tr = core.sem(f"{name}_transposed", own)
        s_high = core.sem(f"{name}_high_done", own)
        s_exact = core.sem(f"{name}_exact_done", own)
        with nc.Block() as block:

            @block.sync
            def _(sp):
                if prefetch is not None:
                    prefetch(sp)

            @block.vector
            def _(dve):
                for j in range(TT):
                    dve.bn_stats(stats[:, j, :], core.x[:, j, :]).then_inc(s_stats, 1)
                for j in range(TT):
                    dve.wait_ge(s_stats, j + 1)
                    dve.bn_aggr(mean_var[:, j, :], stats[:, j, :]).then_inc(s_agg, 1)
                dve.wait_ge(s_agg, TT)
                dve.tensor_scalar(rstd[:, :], mean_var[:, :, 1], EPS, None, ALU.add).then_inc(s_var, 1)
                dve.wait_ge(s_root, 1)
                dve.reciprocal(rstd[:, :], rstd[:, :]).then_inc(s_rstd, 1)
                dve.wait_ge(s_rstd, 1)
                for j in range(TT):
                    dve.tensor_scalar(normed[:, j, :], core.x[:, j, :], mean_var[:, j, 0:1], rstd[:, j:j + 1],
                                      ALU.subtract, ALU.mult).then_inc(s_norm, 1)
                if parts:
                    for j in range(TT):
                        dve.wait_ge(s_tr, j + 1)
                        dve.wait_ge(s_high, j + 1)
                        cols = slice(j * P, (j + 1) * P)
                        dve.tensor_tensor(parts[1][:, :, cols],
                                          core.psum[:, j, :].rearrange("p (c t) -> p c t", c=DC),
                                          parts[0][:, :, cols], ALU.subtract)
                if exact is not None:
                    dve.wait_ge(s_exact, (exact_tokens + P - 1) // P)

            @block.tensor
            def _(pe):
                for j in range(TT):
                    pe.wait_ge(s_norm, j + 1)
                    for c in range(DC):
                        mm = pe.transpose(core.psum[:, j, c * P:(c + 1) * P],
                                          normed[:, j, c * P:(c + 1) * P], core.ident[:, :])
                    mm.then_inc(s_tr, 1)

            @block.scalar
            def _(act):
                act.wait_ge(s_var, 1)
                act.activation(rstd[:, :], rstd[:, :], ACT.Sqrt).then_inc(s_root, 1)
                for j in range(TT):
                    act.wait_ge(s_tr, j + 1)
                    src = core.psum[:, j, :].rearrange("p (c t) -> p c t", c=DC)
                    cols = slice(j * P, (j + 1) * P)
                    n = min(P, exact_tokens - j * P)
                    if exact is not None and n > 0:
                        act.activation(exact[:, :, j * P:j * P + n], src[:, :, 0:n], ACT.Copy).then_inc(s_exact, 1)
                    if parts:
                        act.activation(parts[0][:, :, cols], src, ACT.Copy).then_inc(s_high, 1)


def load_and_constants(core, w):
    nc, arg = core.nc, core.arg
    with ExitStack() as own:
        cos_col = core.sb("cos_col", [P, 1], ctx=own)
        sin_col = core.sb("sin_col", [P, 1], ctx=own)
        swap = core.sb("swap", [P, P], ctx=own)
        turned = core.sb("turned", [P, P], ctx=own)
        diag = core.sb("diag", [P, P], ctx=own)
        s_in = core.sem("x_in", own)
        s_w = core.sem("weights_in", own)
        s_rot = core.sem("angles_in", own)
        s_zero = core.sem("zeroed", own)
        s_rest = core.sem("rest_zeroed", own)
        s_mask = core.sem("masks_done", own)
        s_step = core.sem("rope_step", own)
        with nc.Block() as block:

            @block.sync
            def _(sp):
                sp.dma_start(core.x[:, :, :], arg["x"].rearrange("b n e -> (b n) e")
                             .rearrange("(j p) e -> p j e", p=P)).then_inc(s_in, 16)
                sp.wait_ge(s_in, 16)
                sp.wait_ge(s_w, 7 * 16)
                sp.wait_ge(s_rot, 4 * 16)
                for b in range(2):
                    load_context(core, w["ctx_nat"], sp, b, b)

            @block.scalar
            def _(act):
                act.dma_start(w["wq_d"][:, :, :], arg["Wq_d"].rearrange("(c p) q -> p c q", p=P)).then_inc(s_w, 16)
                qk = arg["W_qk"].rearrange("q (h l) -> q h l", h=XH)
                for r in range(3):
                    act.dma_start(w["w_qk"][:, :, r, :], qk).then_inc(s_w, 16)
                act.dma_start(w["wkv_d"][:, :, :], arg["Wkv_d"].rearrange("(c p) l -> p c l", p=P)).then_inc(s_w, 16)
                act.wait_ge(s_zero, 2)
                for base in (0, UW):
                    act.dma_start(w["wv_u"][base:base + LKV, :, 0:XHD],
                                  arg["Wv_u"].rearrange("l (h d) -> l h d", h=XH)).then_inc(s_w, 16)
                for col, src in ((cos_col, arg["cos"]), (sin_col, arg["sin"])):
                    for odd in range(2):
                        act.dma_start(col[odd:P:2, 0:1], src.rearrange("a i -> i a")).then_inc(s_rot, 16)
                act.wait_ge(s_w, 7 * 16)

            @block.gpsimd
            def _(pool):
                pool.memset(core.ident[:, :], 0.0).then_inc(s_zero, 1)
                pool.memset(swap[:, :], 0.0).then_inc(core.first_stage, 1)
                pool.memset(w["wv_u"][:, :, :], 0.0).then_inc(s_zero, 1)
                pool.memset(w["c_stack"][:, :, :], 0.0).then_inc(s_zero, 1)
                pool.memset(w["c_stage"][:, :, :], 0.0).then_inc(s_zero, 1)
                pool.memset(w["c_nat"][:, :, :, :], 0.0).then_inc(s_zero, 1)
                pool.wait_ge(s_zero, 5)
                pool.wait_ge(core.first_stage, 1)
                pool.memset(w["c_nat"][:, :, :, LKV:LKV + 1], 1.0).then_inc(s_mask, 1)
                pool.wait_ge(s_mask, 1)
                pool.memset(w["c_stack"][:, :, SHIFT:SHIFT + 1], 1.0).then_inc(s_mask, 1)
                for n, base in enumerate((LKV, UW + LKV)):
                    pool.wait_ge(s_mask, 2 + n)
                    pool.memset(w["wv_u"][base:base + 1, :, XHD:XHD + 1], 1.0).then_inc(s_mask, 1)
                pool.wait_ge(s_mask, 4)
                pool.affine_select(out=core.ident[:, :], in_=core.ident[:, :], compare_op=ALU.not_equal, fill=1.0,
                                   base=0, pattern=[[-1, P]], channel_multiplier=1).then_inc(s_mask, 1)
                pair = swap[:, :].rearrange("p (i e) -> p i e", e=2)
                pool.wait_ge(s_mask, 5)
                pool.affine_select(out=pair[:, :, 0], in_=pair[:, :, 0], compare_op=ALU.not_equal, fill=1.0,
                                   base=-1, pattern=[[-2, P // 2]], channel_multiplier=1).then_inc(s_mask, 1)
                pool.wait_ge(s_mask, 6)
                pool.affine_select(out=pair[:, :, 1], in_=pair[:, :, 1], compare_op=ALU.not_equal, fill=-1.0,
                                   base=0, pattern=[[-2, P // 2]], channel_multiplier=1).then_inc(s_mask, 1)
                pool.wait_ge(s_mask, 7)

            @block.vector
            def _(dve):
                dve.memset(w["max_row"][:, :, :], 0.0).then_inc(s_rest, 1)
                dve.memset(w["c_t"][:, :, :].bitcast(F32), 0.0).then_inc(s_rest, 1)
                dve.wait_ge(s_rest, 2)
                dve.wait_ge(s_mask, 7)
                dve.wait_ge(s_rot, 4 * 16)
                dve.tensor_scalar(diag[:, :], core.ident[:, :], cos_col[:, 0:1], None, ALU.mult).then_inc(s_step, 1)
                dve.tensor_scalar(turned[:, :], swap[:, :], sin_col[:, 0:1], None, ALU.mult).then_inc(s_step, 1)
                dve.wait_ge(s_step, 2)
                dve.tensor_tensor(core.rope[:, :], diag[:, :], turned[:, :], ALU.add).then_inc(s_step, 1)
                dve.tensor_tensor(core.rope_t[:, :], diag[:, :], turned[:, :], ALU.subtract).then_inc(s_step, 1)
                dve.wait_ge(s_step, 4)


def load_context(core, ctx_nat, sp, b, par):
    ctx = core.arg["ctx"]
    sp.dma_start(ctx_nat[par][:, 0:FULL, :],
                 ctx[bass.ds(b, 1), 0:FULL * P, :].rearrange("a (p t) e -> p (a t) e", t=FULL)
                 ).then_inc(core.ctx_in[par], 16)
    sp.dma_start(ctx_nat[par][0:TAIL, FULL, :],
                 ctx[bass.ds(b, 1), FULL * P:NCTX, :].rearrange("a p e -> (a p) e")
                 ).then_inc(core.ctx_in[par], 16)


def gather_cache(core, sp, index):
    for n in range(TOPK):
        blk = sp.value_load(index[0:1, n:n + 1], min_val=0, max_val=NBLK - 1)
        rows = slice((n * BLOCK) % P, (n * BLOCK) % P + BLOCK)
        for k, name in enumerate(("k_cache", "v_cache")):
            sp.dma_start(core.cache[rows, k, n * BLOCK // P, :],
                         core.arg[name][bass.ds(blk, 1)].rearrange("a k h d -> (a k) (h d)")
                         ).then_inc(core.cache_in, 16)


def load_kv_weights(core, kv, sp, g, par):
    rows = bass.ds(g * HD, HD)
    for k, name in enumerate(("wk", "wv")):
        sp.dma_start(kv["nat"][par][:, k, :], core.arg[name][rows, :]).then_inc(kv["in"][par], 16)


def load_query_weight(core, qo, sp, g, i):
    sp.dma_start(qo["wq"][:, i, :], core.arg["wq"][bass.ds(g * (REP * HD) + i * HD, HD), :]).then_inc(qo["wq_in"][i], 16)


def load_output_weight(core, qo, sp, g, i):
    sp.dma_start(qo["wo"][:, i, :, :],
                 core.arg["wo"].rearrange("(c o) n -> o c n", o=P)[:, :, bass.ds(g * (REP * HD) + i * HD, HD)]
                 ).then_inc(qo["wo_in"][i], 16)


def load_ffn_weights(core, ffn, sp, c, par):
    raw, done = ffn["raw"][par], ffn["in"][par]
    for k, pair in enumerate((("w1", "mean_w1"), ("w3", "mean_w3"))):
        for i, name in enumerate(pair):
            sp.dma_start(raw[:, k, i, :], core.arg[name][bass.ds(c * P, P), :]).then_inc(done, 16)
    for i, name in enumerate(("w2", "mean_w2")):
        sp.dma_start(raw[:, 2, i, :].rearrange("p (o n) -> p o n", o=DC),
                     core.arg[name].rearrange("(o p) n -> p o n", p=P)[:, :, bass.ds(c * P, P)]).then_inc(done, 16)


def cross_queries(core, w, xn_t):
    nc = core.nc
    with ExitStack() as own:
        cq_t = core.sb("cq_t", [LQ, TOK], ctx=own)
        high_c = core.sb("q_high_c", [P, 2, TOK], F32R, ctx=own)
        s_cq = core.sem("cq_done", own)
        s_cq_sb = core.sem("cq_copied", own)
        s_q = core.sem("q_done", own)
        s_hi = core.sem("q_high_done", own)
        s_lo = core.sem("q_low_done", own)
        qt = w["q_t"]
        with nc.Block() as block:

            @block.tensor
            def _(pe):
                for c in range(DC):
                    mm = pe.matmul(core.psum[0:LQ, 4, :], w["wq_d"][:, c, :], xn_t[:, c, :],
                                   start=(c == 0), stop=(c == DC - 1))
                mm.then_inc(s_cq, 1)
                pe.wait_ge(s_cq_sb, 1)
                for h in range(XH):
                    wait(pe, s_lo, h - 3)
                    wait(pe, s_hi, 2 * (h - 3))
                    pe.matmul(core.psum[0:SHIFT, h % 4, :], w["w_qk"][:, h, :, :], cq_t[:, :],
                              start=True, stop=True).then_inc(s_q, 1)

            @block.scalar
            def _(act):
                act.wait_ge(s_cq, 1)
                act.activation(cq_t[:, :], core.psum[0:LQ, 4, :], ACT.Copy).then_inc(s_cq_sb, 1)
                for h in range(XH):
                    act.wait_ge(s_q, h + 1)
                    act.activation(qt[0:2 * LKV, :, h, :],
                                   core.psum[0:2 * LKV, h % 4, :].rearrange("p (b n) -> p b n", b=BATCH),
                                   ACT.Copy).then_inc(s_hi, 1)
                    wait(act, s_lo, h - 1)
                    act.activation(high_c[2 * LKV:SHIFT, h % 2, :], core.psum[2 * LKV:SHIFT, h % 4, :],
                                   ACT.Copy).then_inc(s_hi, 1)

            @block.vector
            def _(dve):
                for h in range(XH):
                    dve.wait_ge(s_hi, 2 * h + 2)
                    dve.tensor_tensor(qt[2 * LKV:SHIFT, :, h, :],
                                      core.psum[2 * LKV:SHIFT, h % 4, :].rearrange("p (b n) -> p b n", b=BATCH),
                                      high_c[2 * LKV:SHIFT, h % 2, :].rearrange("p (b n) -> p b n", b=BATCH),
                                      ALU.subtract).then_inc(s_lo, 1)
                dve.wait_ge(s_lo, XH)


PREP = [("turn", t) for t in range(KT)] + [("compress", 0), ("natural", 0)] + [("stack", k) for k in range(4)]
PREP_SLOT = [t // 2 for t in range(KT)] + [7, 8, 10, 11, 12, 12]
PREP_ON_ACT = [kind == "turn" and t % 3 < 2 or kind == "compress" or kind == "stack" and t % 2 == 0
               for kind, t in PREP]
PREP_BANK = [(7, 2)[n % 2] for n in range(len(PREP))]
ACT_PREPS = sum(PREP_ON_ACT)
DVE_PREPS = len(PREP) - ACT_PREPS
PIECES = 4
PIECE_KEYS = (402, 400, 400, 400)
PIECE_AT = (0, 402, 802, 1202)
assert sum(PIECE_KEYS) == NCTX + 1
MAXIMA = PIECES * QTILES
MAX_SLOT = [i * (KT - 1) // MAXIMA for i in range(MAXIMA)]
ABS_SLOT = (6, 7, 8)
MIX_BANKS = (3, 6)


def score_bank(b, t):
    return 0 if isinstance(b, int) and b == BATCH - 1 and t % 2 == 1 else 4


def stack_tiles(k):
    return [t for t in range(4 * k, min(4 * k + 4, KT))]


def rows_of(t):
    return P if t < FULL else TAIL


def cross_attention(core, w, own):
    nc, arg, psum = core.nc, core.arg, core.psum
    ctx_nat = w["ctx_nat"]
    index = core.sb("index", [1, TOPK], I32, ctx=own)
    ctx_t = core.sb("ctx_t", [P, DC, KT * P], ctx=own)
    c_parts = core.sb("c_parts", [P, MAIN + TAIL], ctx=own)
    q_now = [core.sb(f"q_now{i}", [P, XQ], F32R, ctx=own) for i in range(2)]
    max_part = core.sb("max_part", [P, QTILES, PIECES], ctx=own)
    probs = [core.sb(f"probs{i}", [P, XQ], ctx=own) for i in range(2)]
    u_t = core.sb("u_t", [P, XQ // 2], ctx=own)
    rden = core.sb("rden", [P, XH], ctx=own)
    mixed = core.sb("mixed", [P, XH, XHD], ctx=own)
    zero = core.sb("zero", [P, 1], ctx=own)
    w_raw = core.sb("w_raw", [P, 3, 2, PIECE], ctx=own)
    c_stage = w["c_stage"]
    c_nat, c_stack, c_t, max_row, q_t = w["c_nat"], w["c_stack"], w["c_t"], w["max_row"], w["q_t"]

    s_ctx = core.ctx_in
    s_idx = core.sem("index_in", own)
    s_zero = core.sem("zero_ready", own)
    s_raw = core.sem("w_raw_in", own)
    s_diff = core.sem("w_diff_done", own)
    s_abs = core.sem("w_abs_done", own)
    s_prep = core.sem("prep_psum_done", own)
    s_pact = core.sem("prep_out_by_act", own)
    s_pdve = core.sem("prep_out_by_dve", own)
    s_part = core.sem("c_stack_part_done", own)
    s_cnat = core.sem("values_placed", own)
    s_qnow = core.sem("q_now_done", own)
    s_sa = core.sem("max_scores_done", own)
    s_max = core.sem("max_part_done", own)
    s_neg = core.sem("max_negated", own)
    s_mt = core.sem("max_turned", own)
    s_shift = core.sem("shift_row_done", own)
    s_sb = core.sem("scores_done", own)
    s_exp = core.sem("probs_done", own)
    s_pv = core.sem("probs_used", own)
    s_u = core.sem("u_copied", own)
    s_o = core.sem("mix_done", own)
    s_rd = core.sem("den_inverted", own)
    s_mix = core.sem("mix_scaled", own)
    s_x = core.sem("x_updated", own)

    wnames = (("w1", "mean_w1"), ("w3", "mean_w3"), ("w2", "mean_w2"))
    flat = {n: arg[n].rearrange("r c -> (r c)").rearrange("(p f) -> p f", p=P) for pair in wnames for n in pair}

    def prep_out_wait(eng, b, n):
        wait(eng, s_pact, ACT_PREPS * b + sum(PREP_ON_ACT[:n]))
        wait(eng, s_pdve, DVE_PREPS * b + n - sum(PREP_ON_ACT[:n]))

    steps_static = [(-2, None, None, 0), (-1, None, 0, 1)]
    steps_end = [(6, 6, 7, None), (7, 7, None, None)]

    def run(eng, step):
        for s, back, lead, prep in steps_static:
            step(back, lead, prep, s % 2, None)
        with eng.Fori(0, (BATCH - 2) // 2) as j:
            step(2 * j, 2 * j + 1, 2 * j + 2, 0, j)
            step(2 * j + 1, 2 * j + 2, 2 * j + 3, 1, j)
        for s, back, lead, prep in steps_end:
            step(back, lead, prep, s % 2, s // 2)

    with nc.Block() as block:

        @block.sync
        def _(sp):
            def load_pieces(b):
                wait(sp, s_abs, 3 * b)
                for k, pair in enumerate(wnames):
                    for i, n in enumerate(pair):
                        sp.dma_start(w_raw[:, k, i, :], flat[n][:, bass.ds(b * PIECE, PIECE)]).then_inc(s_raw, 16)

            def load(b, par):
                wait(sp, s_prep, len(PREP) * (b - 2) + KT)
                load_context(core, ctx_nat, sp, b, par)
                load_pieces(b)

            load_pieces(0)
            load_pieces(1)
            sp.dma_start(index[:, :], arg["block_idx"].rearrange("(a k) -> a k", a=1)).then_inc(s_idx, 16)
            with sp.Fori(1, BATCH // 2) as j:
                load(2 * j, 0)
                load(2 * j + 1, 1)
            sp.wait_ge(s_idx, 16)
            sp.wait_ge(s_prep, len(PREP) * (BATCH - 2) + KT)
            gather_cache(core, sp, index)

        @block.gpsimd
        def _(pool):
            def step(back, lead, prep, par, pair):
                if prep is None:
                    return
                pool.wait_ge(s_raw, 96 * (prep + 1))
                if isinstance(prep, int) and prep == 0:
                    pool.wait_ge(s_zero, 1)
                for k in range(3):
                    pool.tensor_tensor(w_raw[:, k, 0, :], w_raw[:, k, 0, :], w_raw[:, k, 1, :],
                                       ALU.subtract).then_inc(s_diff, 1)
                natural = PREP.index(("natural", 0))
                pool.wait_ge(s_pdve, DVE_PREPS * prep + natural + 1 - sum(PREP_ON_ACT[:natural + 1]))
                stand_alone(pool, core)
                wait(pool, s_prep, len(PREP) * prep)
                hi = c_stack[:, :, 0:LKV]
                pool.tensor_tensor(hi.bitcast(F32R), c_stage[:, :, :],
                                   zero[:, 0:1].unsqueeze(2).to_broadcast([P, KT, LKV]), ALU.add).then_inc(s_part, 1)
                stand_alone(pool, core)
                pool.wait_ge(s_part, 3 * prep + 1)
                pool.tensor_tensor(c_stack[:, :, LKV:2 * LKV], c_stage[:, :, :], hi, ALU.subtract).then_inc(s_part, 1)
                pool.tensor_copy(c_stack[:, :, 2 * LKV:SHIFT], hi).then_inc(s_part, 1)
                stand_alone(pool, core)
                wait(pool, s_sb, KT * (prep - 1))
                pool.tensor_copy(q_now[par][0:SHIFT, :].rearrange("p (h n) -> p h n", h=XH),
                                 q_t[:, bass.ds(prep, 1), :, :].rearrange("p a h n -> p (a h) n")
                                 ).then_inc(s_qnow, 1)
                stand_alone(pool, core)
                wait(pool, s_pv, KT * (prep - 1))
                pool.tensor_copy(c_nat[:, par, :, 0:LKV], c_stage[:, :, :]).then_inc(s_cnat, 1)

            pool.memset(zero[:, :], 0.0).then_inc(s_zero, 1)
            run(pool, step)

        @block.tensor
        def _(pe):
            def prep_item(b, par, n):
                kind, t = PREP[n]
                bank = PREP_BANK[n]
                prep_out_wait(pe, b, n if n == 0 or kind in ("compress", "natural") else n - 1)
                if kind == "turn":
                    if t == 0:
                        pe.wait_ge(s_ctx[par], 16 * b + (32 if par == 0 else 16))
                    rows = rows_of(t)
                    for c in range(DC):
                        mm = pe.transpose(psum[:, bank, c * P:c * P + rows], ctx_nat[par][0:rows, t, c * P:(c + 1) * P],
                                          core.ident[0:rows, 0:rows])
                elif kind == "compress":
                    for c in range(DC):
                        for g in range(GROUPS):
                            pe.matmul(psum[g * LKV:(g + 1) * LKV, bank, 0:MAIN], w["wkv_d"][:, c, :],
                                      ctx_t[:, c, g * MAIN:(g + 1) * MAIN], start=(c == 0), stop=(c == DC - 1))
                    for c in range(DC):
                        mm = pe.matmul(psum[0:LKV, bank, MAIN:MAIN + TAIL], w["wkv_d"][:, c, :],
                                       ctx_t[:, c, FULL * P:NCTX], start=(c == 0), stop=(c == DC - 1))
                elif kind == "natural":
                    for i in range(PER_GROUP):
                        pe.transpose(psum[:, bank, i * P:(i + 1) * P], c_parts[:, i * P:(i + 1) * P], core.ident[:, :])
                    mm = pe.transpose(psum[0:TAIL, bank, MAIN:MAIN + LKV], c_parts[0:LKV, MAIN:MAIN + TAIL],
                                      core.ident[0:LKV, 0:LKV])
                else:
                    pe.wait_ge(s_part, 3 * (b + 1))
                    for i, tile in enumerate(stack_tiles(t)):
                        rows = rows_of(tile)
                        mm = pe.transpose(psum[0:STACK, bank, i * P:i * P + rows], c_stack[0:rows, tile, 0:STACK],
                                          core.ident[0:rows, 0:rows])
                mm.then_inc(s_prep, 1)

            def max_scores(b, par, i):
                qt, piece = divmod(i, PIECES)
                wait(pe, s_max, MAXIMA * b + i - 1)
                if i == 0:
                    prep_out_wait(pe, b, len(PREP))
                    pe.wait_ge(s_qnow, b + 1)
                    wait(pe, s_shift, b)
                width = PIECE_KEYS[piece]
                pe.matmul(psum[:, i % 2, 0:width], q_now[par][0:SHIFT, qt * P:(qt + 1) * P],
                          c_t[0:SHIFT, par, PIECE_AT[piece]:PIECE_AT[piece] + width],
                          start=True, stop=True).then_inc(s_sa, 1)

            def turn_max(b):
                pe.wait_ge(s_neg, b + 1)
                for qt in range(QTILES):
                    mm = pe.transpose(psum[0:STACK, qt // 4, (qt % 4) * P:(qt % 4 + 1) * P], max_row[:, qt, :],
                                      core.ident[:, :])
                mm.then_inc(s_mt, 1)

            def scores(b, par, t):
                alone = isinstance(b, int) and b == BATCH - 1
                wait(pe, s_exp, KT * b + t - (1 if alone and t else 0))
                bank = score_bank(b, t)
                if t == 0:
                    pe.wait_ge(s_shift, b + 1)
                lhs = c_t[0:STACK, par, t * P:t * P + rows_of(t)]
                for half in range(2):
                    mm = pe.matmul(psum[0:rows_of(t), bank + half, :], lhs,
                                   q_now[par][0:STACK, half * BANK:(half + 1) * BANK], start=True, stop=True)
                mm.then_inc(s_sb, 1)

            def values(b, par, t):
                pe.wait_ge(s_exp, KT * b + t + 1)
                if t == 0:
                    pe.wait_ge(s_cnat, b + 1)
                    wait(pe, s_mix, b)
                for half in range(2):
                    mm = pe.matmul(psum[half * UW:(half + 1) * UW, 6, :], c_nat[0:rows_of(t), par, t, :],
                                   probs[t % 2][0:rows_of(t), half * BANK:(half + 1) * BANK],
                                   start=(t == 0), stop=(t == KT - 1))
                mm.then_inc(s_pv, 1)

            def mix(b, par):
                stand_alone(pe, core)
                pe.wait_ge(s_u, b + 1)
                for h in range(XH):
                    base = UW * (h // 8)
                    cols = slice((h % 8) * SEQ, (h % 8 + 1) * SEQ)
                    mm = pe.matmul(psum[par * SEQ:(par + 1) * SEQ, MIX_BANKS[h // 8], (h % 8) * OW:(h % 8 + 1) * OW],
                                   u_t[base:base + LKV + 1, cols], w["wv_u"][base:base + LKV + 1, h, :],
                                   start=True, stop=True)
                mm.then_inc(s_o, 1)

            def step(back, lead, prep, par, pair):
                for slot in range(KT):
                    if back is not None:
                        scores(back, par, slot)
                    preps = [n for n, at in enumerate(PREP_SLOT) if at == slot and prep is not None]
                    maxima = [i for i, at in enumerate(MAX_SLOT) if at == slot and lead is not None]
                    for k in range(max(len(preps), len(maxima))):
                        if k < len(maxima):
                            max_scores(lead, 1 - par, maxima[k])
                        if k < len(preps):
                            prep_item(prep, par, preps[k])
                    if back is not None and slot > 0:
                        values(back, par, slot - 1)
                if back is not None:
                    values(back, par, KT - 1)
                if lead is not None:
                    turn_max(lead)
                if back is not None:
                    mix(back, par)

            run(pe, step)

        def prep_out(eng, on_act, b, par, n):
            kind, t = PREP[n]
            bank = PREP_BANK[n]
            done = s_pact if on_act else s_pdve

            def copy(dst, src):
                return eng.activation(dst, src, ACT.Copy) if on_act else eng.tensor_copy(dst, src)

            eng.wait_ge(s_prep, len(PREP) * b + n + 1)
            if kind == "turn":
                rows = rows_of(t)
                copy(ctx_t[:, :, t * P:t * P + rows],
                     psum[:, bank, :].rearrange("p (c r) -> p c r", c=DC)[:, :, 0:rows]).then_inc(done, 1)
            elif kind == "compress":
                copy(c_parts[:, 0:MAIN], psum[:, bank, 0:MAIN])
                copy(c_parts[0:LKV, MAIN:MAIN + TAIL], psum[0:LKV, bank, MAIN:MAIN + TAIL]).then_inc(done, 1)
            elif kind == "natural":
                wait(eng, s_cnat, b)
                copy(c_stage[:, 0:FULL, :].rearrange("p (g i) l -> p i g l", g=GROUPS),
                     psum[:, bank, 0:MAIN].rearrange("p (i g l) -> p i g l", i=PER_GROUP, g=GROUPS))
                copy(c_stage[0:TAIL, FULL, :], psum[0:TAIL, bank, MAIN:MAIN + LKV]).then_inc(done, 1)
            else:
                tiles = stack_tiles(t)
                width = sum(rows_of(x) for x in tiles)
                wait(eng, s_sb, KT * (b - 2) + tiles[-1] + 1)
                copy(c_t[0:STACK, par, t * BANK:t * BANK + width], psum[0:STACK, bank, 0:width]).then_inc(done, 1)

        @block.scalar
        def _(act):
            def step(back, lead, prep, par, pair):
                for slot in range(KT):
                    if back is not None:
                        rows = rows_of(slot)
                        act.wait_ge(s_sb, KT * back + slot + 1)
                        wait(act, s_pv, KT * back + (slot - 1 if slot else 0))
                        act.activation(probs[slot % 2][0:rows, :].rearrange("p (a n) -> p a n", a=2),
                                       psum[0:rows, score_bank(back, slot):score_bank(back, slot) + 2, :],
                                       ACT.Exp, scale=XSCALE).then_inc(s_exp, 1)
                    if prep is not None:
                        for n, at in enumerate(PREP_SLOT):
                            if at == slot and PREP_ON_ACT[n]:
                                prep_out(act, True, prep, par, n)
                if lead is not None:
                    act.wait_ge(s_mt, lead + 1)
                    act.activation(q_now[1 - par][SHIFT:STACK, :].rearrange("p (a n) -> p a n", a=2),
                                   psum[SHIFT:STACK, 0:2, :], ACT.Copy).then_inc(s_shift, 1)

            run(act, step)

        @block.vector
        def _(dve):
            def take_max(b, i):
                qt, piece = divmod(i, PIECES)
                width = PIECE_KEYS[piece] - (piece == PIECES - 1)
                dve.wait_ge(s_sa, MAXIMA * b + i + 1)
                if i == 0:
                    wait(dve, s_neg, b)
                dve.tensor_reduce(max_part[:, qt, piece:piece + 1], psum[:, i % 2, 0:width],
                                  AX.X, ALU.max).then_inc(s_max, 1)

            def step(back, lead, prep, par, pair):
                for slot in range(KT):
                    preps = [n for n, at in enumerate(PREP_SLOT)
                             if at == slot and prep is not None and not PREP_ON_ACT[n]]
                    maxima = [i for i, at in enumerate(MAX_SLOT) if at == slot and lead is not None]
                    for k in range(max(len(preps), len(maxima))):
                        if k < len(maxima):
                            take_max(lead, maxima[k])
                        if k < len(preps):
                            prep_out(dve, False, prep, par, preps[k])
                    if slot in ABS_SLOT and prep is not None:
                        k = ABS_SLOT.index(slot)
                        if k == 0:
                            dve.wait_ge(s_diff, 3 * (prep + 1))
                        dve.tensor_reduce(core.abs_sum[:, bass.ds(prep, 1), k], w_raw[:, k, 0, :], AX.X, ALU.add,
                                          apply_absolute_value=True).then_inc(s_abs, 1)
                if lead is not None:
                    dve.wait_ge(s_max, MAXIMA * (lead + 1))
                    wait(dve, s_mt, lead)
                    dve.tensor_reduce(max_row[:, :, SHIFT], max_part[:, :, :], AX.X, ALU.max,
                                      negate=True).then_inc(s_neg, 1)
                if back is not None:
                    dve.wait_ge(s_pv, KT * (back + 1))
                    wait(dve, s_o, back)
                    dve.tensor_copy(u_t[:, :], psum[:, 6, :]).then_inc(s_u, 1)
                    half_rows = slice(par * SEQ, (par + 1) * SEQ)
                    out = [psum[half_rows, bank, 0:8 * OW].rearrange("p (h w) -> p h w", h=8) for bank in MIX_BANKS]
                    dve.wait_ge(s_o, back + 1)
                    for a in range(2):
                        inverted = dve.reciprocal(rden[half_rows, 8 * a:8 * a + 8], out[a][:, :, XHD])
                    inverted.then_inc(s_rd, 1)
                    dve.wait_ge(s_rd, back + 1)
                    mixed_v = mixed[half_rows, :, :]
                    for a in range(2):
                        mm = dve.tensor_tensor(mixed_v[:, 8 * a:8 * a + 8, :], out[a][:, :, 0:XHD],
                                               rden[half_rows, 8 * a:8 * a + 8].unsqueeze(2).to_broadcast(
                                                   [SEQ, 8, XHD]), ALU.mult)
                    mm.then_inc(s_mix, 1)
                    dve.wait_ge(s_mix, back + 1)
                    row = core.x[half_rows, bass.ds(pair, 1), :].rearrange("p a e -> p (a e)")
                    dve.tensor_tensor(row, row, mixed_v.rearrange("p h d -> p (h d)"), ALU.add).then_inc(s_x, 1)

            run(dve, step)
            dve.wait_ge(s_x, BATCH)


def rotated_keys(core, own, kv, qo, k_sel, xe, k_high, k_low, v_new):
    nc, arg, psum = core.nc, core.arg, core.psum
    kv_nat, s_w = kv["nat"], kv["in"]
    kv_t = core.sb("kv_weight_t", [P, 2, DC, P], ctx=own)
    k_group = core.sb("k_group", [P, ST, HD], ctx=own)
    new_t = core.sb("new_key_t", [P, SEQ], ctx=own)
    keys_t = core.sb("keys_t", [P, KEYS], ctx=own)
    s_kg = core.sem("group_keys_placed", own)
    s_tr = core.sem("kv_weight_turned", own)
    s_sel = core.sem("group_keys_turned", own)
    s_kt = core.sem("key_weight_copied", own)
    s_vt = core.sem("value_weight_copied", own)
    s_new = core.sem("new_key_done", own)
    s_vnew = core.sem("new_value_done", own)
    s_newsb = core.sem("new_key_copied", own)
    s_vsb = core.sem("new_value_copied", own)
    s_rot = core.sem("new_key_rotated", own)
    s_selsb = core.sem("group_keys_copied", own)
    s_rotsb = core.sem("rotated_copied", own)
    s_back = core.sem("rotated_back", own)
    s_hi = core.sem("keys_high_done", own)
    s_lo = core.sem("keys_low_done", own)

    with nc.Block() as block:

        @block.sync
        def _(sp):
            def load(g, par):
                wait(sp, s_tr, g - 1)
                load_kv_weights(core, kv, sp, g, par)

            for i in range(REP):
                load_query_weight(core, qo, sp, 0, i)
                load_output_weight(core, qo, sp, 0, i)
            with sp.Fori(1, NKV // 2) as j:
                load(2 * j, 0)
                load(2 * j + 1, 1)

        @block.gpsimd
        def _(pool):
            pool.wait_ge(core.cache_in, 2 * TOPK * 16)
            pool.tensor_copy(k_group[:, :, :], k_sel[:, :, 0:HD]).then_inc(s_kg, 1)
            with pool.Fori(1, NKV) as g:
                pool.wait_ge(s_sel, g)
                pool.tensor_copy(k_group[:, :, :], k_sel[:, :, bass.ds(g * HD, HD)]).then_inc(s_kg, 1)

        @block.tensor
        def _(pe):
            def group(g, par):
                pe.wait_ge(s_w[par], 16 * g + (32 if par == 0 else 16))
                wait(pe, s_kt, g)
                wait(pe, s_vt, g)
                for k in range(2):
                    for c in range(DC):
                        mm = pe.transpose(psum[:, k, c * P:(c + 1) * P], kv_nat[par][:, k, c * P:(c + 1) * P],
                                          core.ident[:, :])
                mm.then_inc(s_tr, 1)
                pe.wait_ge(s_kg, g + 1)
                wait(pe, s_selsb, g)
                for t in range(ST):
                    mm = pe.transpose(psum[:, 2, t * P:(t + 1) * P], k_group[:, t, :], core.ident[:, :])
                mm.then_inc(s_sel, 1)
                pe.wait_ge(s_kt, g + 1)
                wait(pe, s_newsb, g)
                for c in range(DC):
                    mm = pe.matmul(psum[:, 3, 0:SEQ], kv_t[:, 0, c, :], xe[:, c, :], start=(c == 0), stop=(c == DC - 1))
                mm.then_inc(s_new, 1)
                pe.wait_ge(s_vt, g + 1)
                wait(pe, s_vsb, g)
                for c in range(DC):
                    mm = pe.matmul(psum[0:SEQ, 4, 0:P], xe[:, c, :], kv_t[:, 1, c, :],
                                   start=(c == 0), stop=(c == DC - 1))
                mm.then_inc(s_vnew, 1)
                pe.wait_ge(s_newsb, g + 1)
                wait(pe, s_rotsb, g)
                pe.matmul(psum[:, 5, 0:SEQ], core.rope_t[:, :], new_t[:, :], start=True, stop=True).then_inc(s_rot, 1)
                pe.wait_ge(s_selsb, g + 1)
                wait(pe, s_lo, 2 * g)
                pe.matmul(psum[:, 6, :], core.rope[:, :], keys_t[:, 0:NSEL], start=True, stop=True).then_inc(s_back, 1)
                pe.wait_ge(s_rotsb, g + 1)
                pe.matmul(psum[:, 7, 0:SEQ], core.rope[:, :], keys_t[:, NSEL:KEYS],
                          start=True, stop=True).then_inc(s_back, 1)

            with pe.Fori(0, NKV // 2) as j:
                group(2 * j, 0)
                group(2 * j + 1, 1)

        @block.scalar
        def _(act):
            with act.Fori(0, NKV) as g:
                act.wait_ge(s_tr, g + 1)
                act.activation(kv_t[:, 0, :, :], psum[:, 0, :].rearrange("p (c t) -> p c t", c=DC),
                               ACT.Copy).then_inc(s_kt, 1)
                act.wait_ge(s_sel, g + 1)
                act.activation(keys_t[:, 0:NSEL], psum[:, 2, :], ACT.Copy).then_inc(s_selsb, 1)
                act.wait_ge(s_vnew, g + 1)
                act.activation(v_new[0:SEQ, bass.ds(g, 1), :].rearrange("p a d -> p (a d)"),
                               psum[0:SEQ, 4, 0:P], ACT.Copy).then_inc(s_vsb, 1)
                for n, (keys, src) in enumerate(((bass.ds(g * KEYS, NSEL), psum[:, 6, :]),
                                                 (bass.ds(g * KEYS + NSEL, SEQ), psum[:, 7, 0:SEQ]))):
                    act.wait_ge(s_back, 2 * g + n + 1)
                    act.activation(k_high[:, keys], src, ACT.Copy, scale=GSCALE).then_inc(s_hi, 1)

        @block.vector
        def _(dve):
            with dve.Fori(0, NKV) as g:
                dve.wait_ge(s_tr, g + 1)
                dve.tensor_copy(kv_t[:, 1, :, :], psum[:, 1, :].rearrange("p (c t) -> p c t", c=DC)).then_inc(s_vt, 1)
                dve.wait_ge(s_new, g + 1)
                dve.tensor_copy(new_t[:, :], psum[:, 3, 0:SEQ]).then_inc(s_newsb, 1)
                dve.wait_ge(s_rot, g + 1)
                dve.tensor_copy(keys_t[:, NSEL:KEYS], psum[:, 5, 0:SEQ]).then_inc(s_rotsb, 1)
                for n, (keys, src) in enumerate(((bass.ds(g * KEYS, NSEL), psum[:, 6, :]),
                                                 (bass.ds(g * KEYS + NSEL, SEQ), psum[:, 7, 0:SEQ]))):
                    dve.wait_ge(s_hi, 2 * g + n + 1)
                    dve.scalar_tensor_tensor(out=k_low[:, keys], in0=src, scalar=GSCALE, in1=k_high[:, keys],
                                             op0=ALU.mult, op1=ALU.subtract).then_inc(s_lo, 1)
            dve.wait_ge(s_lo, 2 * NKV)


HEAD_FIRST_USE = (0, 10, 16, 22)


def turn_use(g, i, k, this=True, nxt=True):
    late = 0 if nxt else 1 if this else 2
    bank = 4 + (k + 1 + late) % 2
    if isinstance(g, int) and g == 0 and i == 0:
        return (1 if k == 0 else 2), bank
    return 28 * g + HEAD_FIRST_USE[i] + k - 7 - late, bank


def grouped_attention(core, own, qo, xh, xl, k_high, k_low, v_sel, v_new):
    nc, arg, psum = core.nc, core.arg, core.psum
    wq_nat, wo_nat, wq_in, wo_in = qo["wq"], qo["wo"], qo["wq_in"], qo["wo_in"]
    wq_t = [core.sb(f"wq_t_{s}", [P, DC, HD], F32R, ctx=own) for s in ("high", "low")]
    wo_t = [core.sb(f"wo_t_{s}", [P, REP, DIM], F32R, ctx=own) for s in ("high", "low")]
    q_t = [core.sb(f"query_t_{s}", [P, TOK], F32R, ctx=own) for s in ("high", "low")]
    value = [core.sb(f"value_{s}", [P, ST + 1, HD], F32R, ctx=own) for s in ("high", "low")]
    probs = core.sb("head_probs", [P, TT, KEYS], ctx=own)
    probs_t = [core.sb(f"probs_t_{s}", [P, ST + 1, TOK], F32R, ctx=own) for s in ("high", "low")]
    mixed_t = [core.sb(f"mixed_t_{s}", [P, REP, TOK], F32R, ctx=own) for s in ("high", "low")]
    neg_max = core.sb("neg_max", [P, TT], ctx=own)
    den = core.sb("den", [P, TT], ctx=own)
    rden = core.sb("inverse_den", [P, TT], ctx=own)
    names = {
        "wqt": "query_weight_turned",
        "wot": "output_weight_turned", "q": "queries_done", "qh": "queries_high_done", "ql": "queries_low_done",
        "s": "head_scores_done", "max": "head_max_done", "exp": "head_probs_done", "rd": "head_den_inverted",
        "norm": "head_probs_scaled", "pt": "head_probs_turned", "th": "turned_high_done", "tl": "turned_low_done",
        "tailh": "tail_high_done", "taill": "tail_low_done", "wqh": "query_weight_high_done",
        "woh": "output_weight_high_done", "vh": "value_high_done", "vl": "value_low_done", "pv": "head_mix_done",
        "ah": "mix_high_done", "al": "mix_low_done", "o": "output_tile_done",
    }
    s = {k: core.sem(v, own) for k, v in names.items()}

    def run(eng, head):
        for i in range(REP):
            head(0, i, True, i > 0, True)
        with eng.Fori(1, NKV - 1) as g:
            for i in range(REP):
                head(g, i, True, True, True)
        for i in range(REP):
            head(NKV - 1, i, True, True, i < REP - 1)
        head(NKV, 0, False, True, False)

    with nc.Block() as block:

        @block.sync
        def _(sp):
            with sp.Fori(1, NKV) as g:
                for i in range(REP):
                    wait(sp, s["wqt"], REP * (g - 1) + i + 1)
                    load_query_weight(core, qo, sp, g, i)
                    stand_alone(sp, core)
                    wait(sp, s["wot"], REP * (g - 1) + i + 1)
                    load_output_weight(core, qo, sp, g, i)

        @block.tensor
        def _(pe):
            def use_bank(use):
                before, bank = use
                wait(pe, s["tl"], before - 1)
                return psum[:, bank, :]

            def queries(n):
                for step, (a, b) in enumerate(PASSES):
                    for c in range(DC):
                        mm = pe.matmul(psum[:, 7, :], wq_t[a][:, c, :], (xh, xl)[b][:, c, :],
                                       start=(step == 0 and c == 0), stop=(step == 2 and c == DC - 1))
                mm.then_inc(s["q"], 1)

            def score(g, n, qt):
                wait(pe, s["exp"], TT * n + qt - 1)
                if qt == 0:
                    pe.wait_ge(s["ql"], n + 1)
                for k0, width, bank in ((0, NSEL, 2 * (qt % 2)), (NSEL, SEQ, 2 * (qt % 2) + 1)):
                    keys = bass.ds(g * KEYS + k0, width)
                    for step, (a, b) in enumerate(PASSES):
                        mm = pe.matmul(psum[:, bank, 0:width], q_t[a][:, qt * P:(qt + 1) * P],
                                       (k_high, k_low)[b][:, keys], start=(step == 0), stop=(step == 2))
                mm.then_inc(s["s"], 1)

            def turn_probs(bank, last, qt):
                pe.wait_ge(s["norm"], TT * last + qt + 1)
                if qt == 0:
                    wait(pe, s["al"], last)
                for t in range(ST):
                    pe.transpose(bank[:, t * P:(t + 1) * P], probs[:, qt, t * P:(t + 1) * P], core.ident[:, :])
                pe.transpose(psum[0:SEQ, 6, qt * P:(qt + 1) * P], probs[:, qt, NSEL:KEYS],
                             core.ident[:, :]).then_inc(s["pt"], 1)

            def mix(last):
                pe.wait_ge(s["taill"], last + 1)
                pe.wait_ge(s["vl"], 2 * ((last // REP) + 1) if isinstance(last, int) else vl_at[0])
                for step, (a, b) in enumerate(PASSES):
                    for t in range(ST + 1):
                        rows = P if t < ST else SEQ
                        mm = pe.matmul(psum[:, 6, :], value[a][0:rows, t, :], probs_t[b][0:rows, t, :],
                                       start=(step == 0 and t == 0), stop=(step == 2 and t == ST))
                mm.then_inc(s["pv"], 1)

            def output(g, qt, bank):
                wait(pe, s["al"], REP * g)
                for i in range(REP):
                    for step, (a, b) in enumerate(PASSES):
                        mm = pe.matmul(bank, mixed_t[a][:, i, qt * P:(qt + 1) * P], wo_t[b][:, i, :],
                                       start=(i == 0 and step == 0), stop=(i == REP - 1 and step == 2))
                mm.then_inc(s["o"], 1)

            vl_at = [None]

            def head(g, i, this, last, nxt):
                n = REP * g + i
                vl_at[0] = 2 * g + (2 if i else 0)
                if nxt:
                    weight = turn_use(g, i, 0)
                    bank = use_bank(weight)
                    j = (i + 1) % REP
                    pe.wait_ge(wq_in[j], 16 * (g + (2 if j == 0 else 1)))
                    for c in range(DC):
                        mm = pe.transpose(bank[:, c * P:(c + 1) * P], wq_nat[:, j, c * P:(c + 1) * P], core.ident[:, :])
                    mm.then_inc(s["wqt"], 1)
                for qt in range(TT):
                    if this:
                        score(g, n, qt)
                    if last:
                        turn_probs(use_bank(turn_use(g, i, 1 + qt, this, nxt)), n - 1, qt)
                if nxt:
                    pe.wait_ge(s["tl"], weight[0] + 1)
                    queries(n + 1)
                if this and i > 0:
                    turn_output_weight(g, i, nxt)
                if last:
                    mix(n - 1)
                if i == 0 and last:
                    for qt in range(TT):
                        output(g, qt, use_bank(turn_use(g, 0, 5 + qt, this, nxt)))
                if this and i == 0:
                    turn_output_weight(g, i, nxt)

            def turn_output_weight(g, i, nxt):
                bank = use_bank(turn_use(g, i, 9 if i == 0 else 5, True, nxt))
                pe.wait_ge(wo_in[i], 16 * (g + 1))
                for c in range(DC):
                    mm = pe.transpose(bank[:, c * P:(c + 1) * P], wo_nat[:, i, c, :], core.ident[:, :])
                mm.then_inc(s["wot"], 1)

            pe.wait_ge(wq_in[0], 16)
            for c in range(DC):
                mm = pe.transpose(psum[:, 4, c * P:(c + 1) * P], wq_nat[:, 0, c * P:(c + 1) * P], core.ident[:, :])
            mm.then_inc(s["wqt"], 1)
            pe.wait_ge(s["tl"], 1)
            queries(0)
            run(pe, head)

        @block.scalar
        def _(act):
            def weight_high(done, count, bank, dst):
                act.wait_ge(done, count)
                act.activation(dst, psum[:, bank, :], ACT.Copy).then_inc(s["th"], 1)

            def queries_high(n):
                act.wait_ge(s["q"], n + 1)
                act.activation(q_t[0][:, :], psum[:, 7, :], ACT.Copy).then_inc(s["qh"], 1)

            def head(g, i, this, last, nxt):
                n = REP * g + i
                if nxt:
                    weight_high(s["wqt"], n + 2, turn_use(g, i, 0)[1], wq_t[0][:, :, :].rearrange("p c d -> p (c d)"))
                for qt in range(TT - 1):
                    if this:
                        exponential(n, qt)
                    if last:
                        turned_high(g, i, this, nxt, qt)
                if last:
                    turned_high(g, i, this, nxt, TT - 1)
                    act.activation(probs_t[0][0:SEQ, ST, :], psum[0:SEQ, 6, :], ACT.Copy).then_inc(s["tailh"], 1)
                if this:
                    exponential(n, TT - 1)
                if nxt:
                    queries_high(n + 1)
                if this and i > 0:
                    output_weight_high(g, i, nxt)
                if last:
                    act.wait_ge(s["pv"], n)
                    act.activation(mixed_t[0][:, (i - 1) % REP, :], psum[:, 6, :], ACT.Copy).then_inc(s["ah"], 1)
                if this and i == 0:
                    output_weight_high(g, i, nxt)

            def exponential(n, qt):
                act.wait_ge(s["max"], TT * n + qt + 1)
                wait(act, s["pt"], TT * (n - 1) + qt + 1)
                act.activation(probs[:, qt, :],
                               psum[:, 2 * (qt % 2):2 * (qt % 2) + 2, :].rearrange("p a k -> p (a k)")[:, 0:KEYS],
                               ACT.Exp, bias=neg_max[:, qt:qt + 1], accum_out=den[:, qt:qt + 1]).then_inc(s["exp"], 1)

            def turned_high(g, i, this, nxt, qt):
                act.wait_ge(s["pt"], TT * (REP * g + i - 1) + qt + 1)
                act.activation(probs_t[0][:, 0:ST, qt * P:(qt + 1) * P],
                               psum[:, turn_use(g, i, 1 + qt, this, nxt)[1], :].rearrange("p (t q) -> p t q", t=ST),
                               ACT.Copy).then_inc(s["th"], 1)

            def output_weight_high(g, i, nxt):
                weight_high(s["wot"], REP * g + i + 1, turn_use(g, i, 9 if i == 0 else 5, True, nxt)[1],
                            wo_t[0][:, i, :])

            weight_high(s["wqt"], 1, 4, wq_t[0][:, :, :].rearrange("p c d -> p (c d)"))
            queries_high(0)
            run(act, head)

        @block.vector
        def _(dve):
            def high_count(g, i, k, this=True, nxt=True):
                if isinstance(g, int) and g == 0 and i == 0:
                    return 2 if k == 0 else 3
                outputs_to_come = TT if i == 0 and k < 5 else 0
                late = 0 if nxt else 1 if this else 2
                return 24 * g + HEAD_FIRST_USE[i] + k - 6 + outputs_to_come - late

            def weight_low(count, bank, dst, high):
                dve.wait_ge(s["th"], count)
                dve.tensor_tensor(dst, psum[:, bank, :], high, ALU.subtract).then_inc(s["tl"], 1)

            def queries_low(n):
                dve.wait_ge(s["qh"], n + 1)
                dve.tensor_tensor(q_t[1][:, :], psum[:, 7, :], q_t[0][:, :], ALU.subtract).then_inc(s["ql"], 1)

            def values_low(g):
                dve.wait_ge(s["vh"], 2 * g + 2)
                dve.tensor_tensor(value[1][:, 0:ST, :], v_sel[:, :, bass.ds(g * HD, HD)], value[0][:, 0:ST, :],
                                  ALU.subtract).then_inc(s["vl"], 1)
                dve.tensor_tensor(value[1][0:SEQ, ST, :], v_new[0:SEQ, bass.ds(g, 1), :].rearrange("p a d -> p (a d)"),
                                  value[0][0:SEQ, ST, :], ALU.subtract).then_inc(s["vl"], 1)

            def flat_wq(a):
                return wq_t[a][:, :, :].rearrange("p c d -> p (c d)")

            def turned_low(g, i, this, nxt, qt):
                dve.wait_ge(s["th"], high_count(g, i, 1 + qt, this, nxt))
                dve.tensor_tensor(probs_t[1][:, 0:ST, qt * P:(qt + 1) * P],
                                  psum[:, turn_use(g, i, 1 + qt, this, nxt)[1], :].rearrange("p (t q) -> p t q", t=ST),
                                  probs_t[0][:, 0:ST, qt * P:(qt + 1) * P], ALU.subtract).then_inc(s["tl"], 1)

            def invert(n, qt):
                dve.wait_ge(s["exp"], TT * n + qt + 1)
                wait(dve, s["norm"], TT * (n - 1) + qt + 1)
                dve.reciprocal(rden[:, qt:qt + 1], den[:, qt:qt + 1]).then_inc(s["rd"], 1)

            def output_weight_low(g, i, nxt):
                k = 9 if i == 0 else 5
                weight_low(high_count(g, i, k, True, nxt), turn_use(g, i, k, True, nxt)[1],
                           wo_t[1][:, i, :], wo_t[0][:, i, :])

            def head(g, i, this, last, nxt):
                n = REP * g + i
                for qt in range(TT):
                    if this:
                        dve.wait_ge(s["s"], TT * n + qt + 1)
                        wait(dve, s["exp"], TT * (n - 1) + qt + 1)
                        dve.tensor_reduce(neg_max[:, qt:qt + 1],
                                          psum[:, 2 * (qt % 2):2 * (qt % 2) + 2, :].rearrange("p a k -> p (a k)")[:, 0:KEYS],
                                          AX.X, ALU.max, negate=True).then_inc(s["max"], 1)
                    if qt == 0 and nxt:
                        weight_low(high_count(g, i, 0), turn_use(g, i, 0)[1], flat_wq(1), flat_wq(0))
                    if qt > 0 and last:
                        turned_low(g, i, this, nxt, qt - 1)
                    if qt > 0 and this:
                        invert(n, qt - 1)
                if last:
                    turned_low(g, i, this, nxt, TT - 1)
                    dve.wait_ge(s["tailh"], n)
                    dve.tensor_tensor(probs_t[1][0:SEQ, ST, :], psum[0:SEQ, 6, :], probs_t[0][0:SEQ, ST, :],
                                      ALU.subtract).then_inc(s["taill"], 1)
                if this:
                    invert(n, TT - 1)
                if nxt:
                    queries_low(n + 1)
                if this and i > 0:
                    output_weight_low(g, i, nxt)
                if last:
                    dve.wait_ge(s["ah"], n)
                    j = (i - 1) % REP
                    dve.tensor_tensor(mixed_t[1][:, j, :], psum[:, 6, :], mixed_t[0][:, j, :],
                                      ALU.subtract).then_inc(s["al"], 1)
                if i == 0 and last:
                    for qt in range(TT):
                        dve.wait_ge(s["o"], TT * (g - 1) + qt + 1)
                        dve.tensor_tensor(core.x[:, qt, :], psum[:, turn_use(g, 0, 5 + qt, this, nxt)[1], :],
                                          core.x[:, qt, :], ALU.add).then_inc(s["tl"], 1)
                if this and i == 0:
                    output_weight_low(g, i, nxt)
                    values_low(g)

            weight_low(1, 4, flat_wq(1), flat_wq(0))
            queries_low(0)
            run(dve, head)
            dve.wait_ge(s["tl"], turn_use(NKV, 0, 1 + 2 * TT, False, False)[0])

        @block.gpsimd
        def _(pool):
            def values(g):
                pool.tensor_copy(value[0][:, 0:ST, :], v_sel[:, :, bass.ds(g * HD, HD)]).then_inc(s["vh"], 1)
                pool.tensor_copy(value[0][0:SEQ, ST, :],
                                 v_new[0:SEQ, bass.ds(g, 1), :].rearrange("p a d -> p (a d)")).then_inc(s["vh"], 1)

            def head(g, i, this, last, nxt):
                n = REP * g + i
                if not this:
                    return
                for qt in range(TT):
                    pool.wait_ge(s["rd"], TT * n + qt + 1)
                    pool.tensor_tensor(probs[:, qt, :], probs[:, qt, :], rden[:, qt:qt + 1].to_broadcast([P, KEYS]),
                                       ALU.mult).then_inc(s["norm"], 1)
                if i == 0:
                    wait(pool, s["pv"], n)
                    values(g)

            pool.wait_ge(core.cache_in, 2 * TOPK * 16)
            run(pool, head)


def feed_forward(core, own, ffn, xh, xl):
    nc, arg, psum = core.nc, core.arg, core.psum
    ones = core.sb("ones", [P, P], ctx=own)
    total = core.sb("abs_total", [P, 3], ctx=own)
    coeff = core.sb("coeff", [P, 3], ctx=own)
    raw, s_raw = ffn["raw"], ffn["in"]
    diff = core.sb("ffn_diff", [P, 3, DIM], ctx=own)
    sign = [core.sb(f"ffn_sign{i}", [P, 3, DIM], ctx=own) for i in range(SLOTS)]
    quant = core.sb("ffn_quant", [P, 3, DIM], ctx=own)
    w_t = [core.sb(f"ffn_w_t_{s}", [P, 3, DIM], F32R, ctx=own) for s in ("high", "low")]
    gate = core.sb("gate", [P, TOK], ctx=own)
    hidden = core.sb("hidden", [P, TOK], ctx=own)
    hid = [core.sb(f"hidden_{s}", [P, TOK], F32R, ctx=own) for s in ("high", "low")]
    s_ones = core.sem("ones_ready", own)
    s_tot = core.sem("abs_summed", own)
    s_all = core.sem("abs_spread", own)
    s_co = core.sem("coeff_ready", own)
    s_diff = core.sem("ffn_diff_done", own)
    s_sign = core.sem("ffn_sign_done", own)
    s_quant = [core.sem(f"ffn_quant_done{k}", own) for k in range(3)]
    s_turn = [core.sem(f"ffn_turned{k}", own) for k in range(3)]
    s_wh = [core.sem(f"ffn_high_done{k}", own) for k in range(3)]
    s_wl = [core.sem(f"ffn_low_done{k}", own) for k in range(3)]
    s_gu = [core.sem(f"gate_up_done{k}", own) for k in range(2)]
    s_silu = core.sem("silu_done", own)
    s_h = core.sem("hidden_done", own)
    s_hh = core.sem("hidden_high_done", own)
    s_hl = core.sem("hidden_low_done", own)
    s_d = core.sem("down_done", own)
    s_x = core.sem("final_sum_done", own)
    s_out = core.sem("out_written", own)
    turn_bank = (4, 5, 4)

    def run(eng, chunk):
        for c in range(2):
            chunk(c, c % SLOTS)
        with eng.Fori(0, (CH - 5) // SLOTS) as j:
            for k in range(SLOTS):
                chunk(SLOTS * j + 2 + k, (2 + k) % SLOTS)
        for c in range(CH - 3, CH):
            chunk(c, c % SLOTS)

    assert (CH - 5) % SLOTS == 0

    def within(c, ahead):
        return not isinstance(c, int) or c + ahead < CH

    with nc.Block() as block:

        @block.sync
        def _(sp):
            def load(c, par):
                wait(sp, s_quant[2], c - SLOTS + 1)
                wait(sp, s_quant[1], c - SLOTS + 1)
                load_ffn_weights(core, ffn, sp, c, par)

            for c in range(SLOTS, SLOTS + 2):
                load(c, c % SLOTS)
            with sp.Fori(0, (CH - 5) // SLOTS) as j:
                for k in range(SLOTS):
                    load(SLOTS * j + 5 + k, (5 + k) % SLOTS)
            out = core.out.rearrange("b n e -> (b n) e").rearrange("(j p) e -> p j e", p=P)
            for j in range(TT):
                sp.wait_ge(s_x, j + 1)
                sp.dma_start(out[:, j, :], core.x[:, j, :]).then_inc(s_out, 16)
            sp.wait_ge(s_out, 16 * TT)

        @block.gpsimd
        def _(pool):
            def chunk(c, par):
                pool.wait_ge(s_raw[par], 96 // SLOTS * c + 96 - 96 // SLOTS * par)
                wait(pool, s_sign, c)
                pool.tensor_tensor(diff[:, :, :], raw[par][:, :, 0, :], raw[par][:, :, 1, :],
                                   ALU.subtract).then_inc(s_diff, 1)

            pool.memset(ones[:, :], 1.0).then_inc(s_ones, 1)
            run(pool, chunk)

        @block.tensor
        def _(pe):
            def turn(c, k):
                bank = turn_bank[k]
                pe.wait_ge(s_quant[k], c + 1)
                if k == 0:
                    wait(pe, s_wl[2], c - 1)
                elif k == 1:
                    wait(pe, s_wl[1], c)
                else:
                    pe.wait_ge(s_wl[0], c + 2 if within(c, 1) else CH)
                for i in range(DC):
                    mm = pe.transpose(psum[:, bank, i * P:(i + 1) * P], quant[:, k, i * P:(i + 1) * P],
                                      core.ident[:, :])
                mm.then_inc(s_turn[k], 1)

            def gates(c, k):
                wait(pe, s_silu if k == 0 else s_h, c)
                pe.wait_ge(s_wl[k], c + 1)
                for step, (a, b) in enumerate(PASSES):
                    for i in range(DC):
                        mm = pe.matmul(psum[:, 6 + k, :], w_t[a][:, k, i * P:(i + 1) * P], (xh, xl)[b][:, i, :],
                                       start=(step == 0 and i == 0), stop=(step == 2 and i == DC - 1))
                mm.then_inc(s_gu[k], 1)

            def down(c):
                first, last = isinstance(c, int) and c == 0, isinstance(c, int) and c == CH - 1
                pe.wait_ge(s_hl, c + 1)
                pe.wait_ge(s_wl[2], c + 1)
                for qt in range(TT):
                    for step, (a, b) in enumerate(PASSES):
                        mm = pe.matmul(psum[:, qt, :], hid[a][:, qt * P:(qt + 1) * P], w_t[b][:, 2, :],
                                       start=(first and step == 0), stop=(last and step == 2),
                                       skip_group_check=True)
                mm.then_inc(s_d, 1)

            def chunk(c, par):
                gates(c, 0)
                gates(c, 1)
                if within(c, 1):
                    turn(c + 1, 0)
                    turn(c + 1, 1)
                if not (isinstance(c, int) and c == 0):
                    down(c - 1)
                turn(c, 2)

            pe.wait_ge(s_ones, 1)
            pe.wait_ge(s_tot, 1)
            pe.matmul(psum[:, 0, 0:3], ones[:, :], total[:, :], start=True, stop=True).then_inc(s_all, 1)
            pe.wait_ge(s_co, 1)
            turn(0, 0)
            turn(0, 1)
            run(pe, chunk)
            down(CH - 1)

        @block.scalar
        def _(act):
            def signs(c, par):
                act.wait_ge(s_diff, c + 1)
                wait(act, s_quant[2], c - SLOTS + 1)
                wait(act, s_quant[1], c - SLOTS + 1)
                act.activation(sign[par][:, :, :], diff[:, :, :], ACT.Sign).then_inc(s_sign, 1)

            def high(c, k):
                act.wait_ge(s_turn[k], c + 1)
                act.activation(w_t[0][:, k, :], psum[:, turn_bank[k], :], ACT.Copy).then_inc(s_wh[k], 1)

            def chunk(c, par):
                act.wait_ge(s_gu[0], c + 1)
                wait(act, s_h, c)
                act.activation(gate[:, :], psum[:, 6, :], ACT.Silu).then_inc(s_silu, 1)
                if within(c, 1):
                    high(c + 1, 0)
                    high(c + 1, 1)
                act.wait_ge(s_h, c + 1)
                wait(act, s_d, c)
                act.activation(hid[0][:, :], hidden[:, :], ACT.Copy).then_inc(s_hh, 1)
                high(c, 2)
                if within(c, 2):
                    signs(c + 2, (par + 2) % SLOTS)

            signs(0, 0)
            high(0, 0)
            high(0, 1)
            signs(1, 1)
            run(act, chunk)

        @block.vector
        def _(dve):
            def quantise(c, par, k):
                dve.wait_ge(s_sign, c + 1)
                wait(dve, s_turn[k], c)
                dve.scalar_tensor_tensor(out=quant[:, k, :], in0=sign[par][:, k, :], scalar=coeff[:, k:k + 1],
                                         in1=raw[par][:, k, 1, :], op0=ALU.mult, op1=ALU.add).then_inc(s_quant[k], 1)

            def low(c, k):
                dve.wait_ge(s_wh[k], c + 1)
                dve.tensor_tensor(w_t[1][:, k, :], psum[:, turn_bank[k], :], w_t[0][:, k, :],
                                  ALU.subtract).then_inc(s_wl[k], 1)

            def chunk(c, par):
                dve.wait_ge(s_silu, c + 1)
                dve.wait_ge(s_gu[1], c + 1)
                wait(dve, s_hl, c)
                dve.tensor_tensor(hidden[:, :], psum[:, 7, :], gate[:, :], ALU.mult).then_inc(s_h, 1)
                if within(c, 1):
                    low(c + 1, 0)
                    low(c + 1, 1)
                dve.wait_ge(s_hh, c + 1)
                dve.tensor_tensor(hid[1][:, :], hidden[:, :], hid[0][:, :], ALU.subtract).then_inc(s_hl, 1)
                low(c, 2)
                if within(c, 2):
                    quantise(c + 2, (par + 2) % SLOTS, 0)
                    quantise(c + 2, (par + 2) % SLOTS, 1)
                if within(c, 1):
                    quantise(c + 1, (par + 1) % SLOTS, 2)

            dve.tensor_reduce(total[:, :], core.abs_sum[:, :, :].rearrange("p b k -> p k b"), AX.X,
                              ALU.add).then_inc(s_tot, 1)
            dve.wait_ge(s_all, 1)
            dve.tensor_scalar(coeff[:, :], psum[:, 0, 0:3], 1.0 / WSIZE, None, ALU.mult).then_inc(s_co, 1)
            dve.wait_ge(s_co, 1)
            for k in range(3):
                quantise(0, 0, k)
            low(0, 0)
            low(0, 1)
            quantise(1, 1, 0)
            quantise(1, 1, 1)
            run(dve, chunk)
            dve.wait_ge(s_d, CH)
            for j in range(TT):
                dve.tensor_tensor(core.x[:, j, :], psum[:, j, :], core.x[:, j, :], ALU.add).then_inc(s_x, 1)


def layer(nc, out, **arg):
    with ExitStack() as ctx:
        core = Core(nc, ctx, arg, out)
        with ExitStack() as own:
            even_ctx = core.cache.rearrange("p a t c -> p (a t c)")[:, 0:KT * DIM].rearrange("p (t e) -> p t e", t=KT)
            w = {
                "ctx_nat": [even_ctx, core.sb("ctx_nat_odd", [P, KT, DIM], ctx=own)],
                "wkv_d": core.sb("wkv_d", [P, DC, LKV], ctx=own),
                "wv_u": core.sb("wv_u", [P, XH, OW], ctx=own),
                "c_nat": core.sb("c_nat", [P, 2, KT, UW], ctx=own),
                "c_stack": core.sb("c_stack", [P, KT, STACK], ctx=own),
                "c_stage": core.sb("c_stage", [P, KT, LKV], ctx=own),
                "c_t": core.sb("c_t", [P, 2, KT * P], F32R, ctx=own),
                "max_row": core.sb("max_row", [P, QTILES, STACK], ctx=own),
                "q_t": core.sb("q_t", [SHIFT, BATCH, XH, SEQ], F32R, ctx=own),
            }
            with ExitStack() as first:
                w["w_qk"] = core.sb("w_qk", [LQ, XH, 3, LKV], ctx=first)
                w["wq_d"] = core.sb("wq_d", [P, DC, LQ], ctx=first)
                xn_t = core.sb("xn_t", [P, DC, TOK], ctx=first)
                load_and_constants(core, w)
                layer_norm_t(core, "norm1", None, first, exact=xn_t, exact_tokens=TOK)
                cross_queries(core, w, xn_t)
            cross_attention(core, w, own)
        k_sel, v_sel = core.cache[:, 0], core.cache[:, 1]
        with ExitStack() as own:
            k_high = core.sb("k_high", [P, NKV * KEYS], F32R, ctx=own)
            k_low = core.sb("k_low", [P, NKV * KEYS], F32R, ctx=own)
            v_new = core.sb("v_new", [P, NKV, HD], ctx=own)
            xh = core.sb("attn_x_high", [P, DC, TOK], F32R, ctx=own)
            xl = core.sb("attn_x_low", [P, DC, TOK], F32R, ctx=own)
            qo = {
                "wq": core.sb("wq_nat", [P, REP, DIM], ctx=own),
                "wo": core.sb("wo_nat", [P, REP, DC, HD], ctx=own),
                "wq_in": [core.sem(f"query_weight_in{i}", own) for i in range(REP)],
                "wo_in": [core.sem(f"output_weight_in{i}", own) for i in range(REP)],
            }
            with ExitStack() as first:
                kv = {
                    "nat": [core.sb(f"kv_weight{i}", [P, 2, DIM], ctx=first) for i in range(2)],
                    "in": [core.sem(f"kv_weight_in{i}", first) for i in range(2)],
                }
                xe = core.sb("new_tokens", [P, DC, SEQ], ctx=first)

                def kv_prefetch(sp):
                    for g in range(2):
                        load_kv_weights(core, kv, sp, g, g)

                layer_norm_t(core, "norm2", (xh, xl), first, exact=xe, exact_tokens=SEQ, prefetch=kv_prefetch)
                rotated_keys(core, first, kv, qo, k_sel, xe, k_high, k_low, v_new)
            grouped_attention(core, own, qo, xh, xl, k_high, k_low, v_sel, v_new)
        with ExitStack() as own:
            xh = core.sb("ffn_x_high", [P, DC, TOK], F32R, ctx=own)
            xl = core.sb("ffn_x_low", [P, DC, TOK], F32R, ctx=own)
            ffn = {
                "raw": [core.sb(f"ffn_raw{i}", [P, 3, 2, DIM], ctx=own) for i in range(SLOTS)],
                "in": [core.sem(f"ffn_raw_in{i}", own) for i in range(SLOTS)],
            }

            def ffn_prefetch(sp):
                for c in range(SLOTS):
                    load_ffn_weights(core, ffn, sp, c, c)

            layer_norm_t(core, "norm3", (xh, xl), own, prefetch=ffn_prefetch)
            feed_forward(core, own, ffn, xh, xl)


INPUTS = {
    "x": "x", "ctx": "ctx_4096", "Wq_d": "L0_xattn_Wq_d", "W_qk": "L0_xattn_W_qk", "Wkv_d": "L0_xattn_Wkv_d",
    "Wv_u": "L0_xattn_Wv_u", "cos": "L0_attn_freqs_cos", "sin": "L0_attn_freqs_sin", "wq": "L0_attn_wq",
    "wk": "L0_attn_wk", "wv": "L0_attn_wv", "wo": "L0_attn_wo", "k_cache": "L0_attn_k_cache",
    "v_cache": "L0_attn_v_cache", "block_idx": "L0_attn_block_idx", "w1": "L0_ffn_w1",
    "mean_w1": "L0_ffn_mean_w1", "w2": "L0_ffn_w2", "mean_w2": "L0_ffn_mean_w2", "w3": "L0_ffn_w3",
    "mean_w3": "L0_ffn_mean_w3",
}


def kernel(**inputs):
    import numpy as _np
    import concourse.bacc as _bacc
    from concourse import mybir as _mybir
    from concourse.bass_utils import run_bass_kernel_spmd as _run

    nc = _bacc.Bacc("TRN2", target_bir_lowering=False, num_devices=1)
    arrays, args = {}, {}
    for short, name in INPUTS.items():
        a = _np.ascontiguousarray(inputs[name])
        arrays[f"in_{name}_dram"] = a
        args[short] = nc.dram_tensor(f"in_{name}_dram", a.shape, _mybir.dt.from_np(a.dtype),
                                     kind="ExternalInput").ap()
    out = nc.dram_tensor("out_0_dram", (BATCH, SEQ, DIM), F32, kind="ExternalOutput").ap()
    layer(nc, out, **args)
    r = _run(nc, [arrays], core_ids=[0])
    return r.results[0]["out_0_dram"]
```

```python
from contextlib import ExitStack

import concourse.bass as bass
from concourse import mybir

F32 = mybir.dt.float32
F32R = mybir.dt.float32r
I32 = mybir.dt.int32
ALU = mybir.AluOpType
ACT = mybir.ActivationFunctionType
AX = mybir.AxisListType

P = 128
BANK = 512

BATCH, SEQ, DIM = 8, 64, 512
TOK = BATCH * SEQ
TT = TOK // P
DC = DIM // P
EPS = 1e-5

XH, LQ, LKV, XHD = 16, 64, 32, 32
NCTX = 1601
FULL = NCTX // P
TAIL = NCTX - FULL * P
KT = FULL + 1
XQ = XH * SEQ
QTILES = XQ // P
GROUPS = P // LKV
PER_GROUP = FULL // GROUPS
MAIN = PER_GROUP * P
SHIFT = 3 * LKV
STACK = SHIFT + 1
UW = 64
OW = XHD + 2
XSCALE = float(LKV) ** -0.5

NH, NKV, HD = 32, 8, 128
REP = NH // NKV
BLOCK, NBLK, TOPK = 32, 128, 16
NSEL = TOPK * BLOCK
ST = NSEL // P
KEYS = NSEL + SEQ
HALF = KEYS // 2
GSCALE = float(HD) ** -0.5

INTER = 1792
CH = INTER // P
SLOTS = 3
PASSES = ((0, 0), (0, 1), (1, 0))

WSIZE = INTER * DIM
PIECE = WSIZE // P // BATCH


def wait(eng, sem, count):
    if isinstance(count, int) and count <= 0:
        return
    eng.wait_ge(sem, count)


def stand_alone(eng, core):
    eng.wait_ge(core.first_stage, 1)


class Core:

    def __init__(self, nc, ctx, arg, out):
        self.nc, self.ctx, self.arg, self.out = nc, ctx, arg, out
        self.psum = ctx.enter_context(nc.psum_tensor("psum", [P, 8, BANK], F32))
        self.x = self.sb("x", [P, TT, DIM])
        self.ident = self.sb("ident", [P, P])
        self.rope = self.sb("rope", [P, P])
        self.rope_t = self.sb("rope_t", [P, P])
        self.abs_sum = self.sb("abs_sum", [P, BATCH, 3])
        self.cache = self.sb("cache", [P, 2, ST, NKV * HD])
        self.cache_in = self.sem("cache_in")
        self.ctx_in = [self.sem(f"ctx_in{i}") for i in range(2)]
        self.first_stage = self.sem("first_stage_reached")

    def sb(self, name, shape, dt=F32, ctx=None):
        return (ctx or self.ctx).enter_context(self.nc.sbuf_tensor(name, shape, dt))

    def sem(self, name, ctx=None):
        return (ctx or self.ctx).enter_context(self.nc.semaphore(name))


class LayerNorm:

    def __init__(self, core, name, ctx, parts=None, exact=None, exact_tokens=0, first_bank=0):
        self.core, self.parts, self.exact, self.exact_tokens, self.first_bank = core, parts, exact, exact_tokens, first_bank
        self.stats = core.sb(f"{name}_stats", [P, TT, 6], ctx=ctx)
        self.mean_var = core.sb(f"{name}_mean_var", [P, TT, 2], ctx=ctx)
        self.rstd = core.sb(f"{name}_rstd", [P, TT], ctx=ctx)
        self.normed = core.sb(f"{name}_normed", [P, TT, DIM], ctx=ctx)
        self.s_stats = core.sem(f"{name}_stats_done", ctx)
        self.s_agg = core.sem(f"{name}_moments_done", ctx)
        self.s_var = core.sem(f"{name}_variance_done", ctx)
        self.s_root = core.sem(f"{name}_root_done", ctx)
        self.s_rstd = core.sem(f"{name}_rstd_done", ctx)
        self.s_norm = core.sem(f"{name}_normed_done", ctx)
        self.s_tr = core.sem(f"{name}_transposed", ctx)
        self.s_high = core.sem(f"{name}_high_done", ctx)
        self.s_low = core.sem(f"{name}_low_done", ctx)
        self.s_exact = core.sem(f"{name}_exact_done", ctx)

    def turned(self, j):
        return self.core.psum[:, self.first_bank + j, :].rearrange("p (c t) -> p c t", c=DC)

    def normalise(self, dve):
        for j in range(TT):
            dve.bn_stats(self.stats[:, j, :], self.core.x[:, j, :]).then_inc(self.s_stats, 1)
        for j in range(TT):
            dve.wait_ge(self.s_stats, j + 1)
            dve.bn_aggr(self.mean_var[:, j, :], self.stats[:, j, :]).then_inc(self.s_agg, 1)
        dve.wait_ge(self.s_agg, TT)
        dve.tensor_scalar(self.rstd[:, :], self.mean_var[:, :, 1], EPS, None, ALU.add).then_inc(self.s_var, 1)
        dve.wait_ge(self.s_root, 1)
        dve.reciprocal(self.rstd[:, :], self.rstd[:, :]).then_inc(self.s_rstd, 1)
        dve.wait_ge(self.s_rstd, 1)
        for j in range(TT):
            dve.tensor_scalar(self.normed[:, j, :], self.core.x[:, j, :], self.mean_var[:, j, 0:1],
                              self.rstd[:, j:j + 1], ALU.subtract, ALU.mult).then_inc(self.s_norm, 1)

    def root(self, act):
        act.wait_ge(self.s_var, 1)
        act.activation(self.rstd[:, :], self.rstd[:, :], ACT.Sqrt).then_inc(self.s_root, 1)

    def turn(self, pe):
        for j in range(TT):
            pe.wait_ge(self.s_norm, j + 1)
            for c in range(DC):
                mm = pe.transpose(self.core.psum[:, self.first_bank + j, c * P:(c + 1) * P],
                                  self.normed[:, j, c * P:(c + 1) * P], self.core.ident[:, :])
            mm.then_inc(self.s_tr, 1)

    def copy_out(self, act):
        for j in range(TT):
            act.wait_ge(self.s_tr, j + 1)
            n = min(P, self.exact_tokens - j * P)
            if n > 0:
                act.activation(self.exact[:, :, j * P:j * P + n], self.turned(j)[:, :, 0:n],
                               ACT.Copy).then_inc(self.s_exact, 1)
            if self.parts:
                act.activation(self.parts[0][:, :, j * P:(j + 1) * P], self.turned(j), ACT.Copy).then_inc(self.s_high, 1)

    def low_parts(self, dve):
        for j in range(TT):
            dve.wait_ge(self.s_tr, j + 1)
            dve.wait_ge(self.s_high, j + 1)
            cols = slice(j * P, (j + 1) * P)
            dve.tensor_tensor(self.parts[1][:, :, cols], self.turned(j), self.parts[0][:, :, cols],
                              ALU.subtract).then_inc(self.s_low, 1)


def load_and_constants(core, w, xn_t):
    nc, arg = core.nc, core.arg
    with ExitStack() as own:
        cos_col = core.sb("cos_col", [P, 1], ctx=own)
        sin_col = core.sb("sin_col", [P, 1], ctx=own)
        swap = core.sb("swap", [P, P], ctx=own)
        turned = core.sb("turned", [P, P], ctx=own)
        diag = core.sb("diag", [P, P], ctx=own)
        norm = LayerNorm(core, "norm1", own, exact=xn_t, exact_tokens=TOK)
        s_in = core.sem("x_in", own)
        s_w = core.sem("weights_in", own)
        s_rot = core.sem("angles_in", own)
        s_zero = core.sem("zeroed", own)
        s_rest = core.sem("rest_zeroed", own)
        s_mask = core.sem("masks_done", own)
        s_step = core.sem("rope_step", own)
        with nc.Block() as block:

            @block.sync
            def _(sp):
                sp.dma_start(core.x[:, :, :], arg["x"].rearrange("b n e -> (b n) e")
                             .rearrange("(j p) e -> p j e", p=P)).then_inc(s_in, 16)
                sp.dma_start(w["wq_d"][:, :, :], arg["Wq_d"].rearrange("(c p) q -> p c q", p=P)).then_inc(s_w, 16)
                qk = arg["W_qk"].rearrange("q (h l) -> q h l", h=XH)
                for r in range(2):
                    sp.dma_start(w["w_qk"][:, :, r, :], qk).then_inc(s_w, 16)
                sp.dma_start(w["wkv_d"][:, :, :], arg["Wkv_d"].rearrange("(c p) l -> p c l", p=P)).then_inc(s_w, 16)
                sp.wait_ge(s_in, 16)
                sp.wait_ge(s_w, 6 * 16)
                sp.wait_ge(s_rot, 4 * 16)
                for b in range(2):
                    load_context(core, w["ctx_nat"], sp, b, b)

            @block.scalar
            def _(act):
                for col, src in ((cos_col, arg["cos"]), (sin_col, arg["sin"])):
                    for odd in range(2):
                        act.dma_start(col[odd:P:2, 0:1], src.rearrange("a i -> i a")).then_inc(s_rot, 16)
                act.wait_ge(s_zero, 2)
                for base in (0, UW):
                    act.dma_start(w["wv_u"][base:base + LKV, :, 0:XHD],
                                  arg["Wv_u"].rearrange("l (h d) -> l h d", h=XH)).then_inc(s_w, 16)
                norm.root(act)
                norm.copy_out(act)

            @block.tensor
            def _(pe):
                pe.wait_ge(s_mask, 5)
                norm.turn(pe)

            @block.gpsimd
            def _(pool):
                pool.memset(core.ident[:, :], 0.0).then_inc(s_zero, 1)
                pool.memset(swap[:, :], 0.0).then_inc(core.first_stage, 1)
                pool.memset(w["wv_u"][:, :, :], 0.0).then_inc(s_zero, 1)
                pool.memset(w["c_stack"][:, :, :], 0.0).then_inc(s_zero, 1)
                pool.memset(w["c_stage"][:, :, :], 0.0).then_inc(s_zero, 1)
                pool.memset(w["c_nat"][:, :, :, :], 0.0).then_inc(s_zero, 1)
                pool.wait_ge(s_zero, 5)
                pool.wait_ge(core.first_stage, 1)
                pool.memset(w["c_nat"][:, :, :, LKV:LKV + 1], 1.0).then_inc(s_mask, 1)
                pool.wait_ge(s_mask, 1)
                pool.memset(w["c_stack"][:, :, SHIFT:SHIFT + 1], 1.0).then_inc(s_mask, 1)
                for n, base in enumerate((LKV, UW + LKV)):
                    pool.wait_ge(s_mask, 2 + n)
                    pool.memset(w["wv_u"][base:base + 1, :, XHD:XHD + 1], 1.0).then_inc(s_mask, 1)
                pool.wait_ge(s_mask, 4)
                pool.affine_select(out=core.ident[:, :], in_=core.ident[:, :], compare_op=ALU.not_equal, fill=1.0,
                                   base=0, pattern=[[-1, P]], channel_multiplier=1).then_inc(s_mask, 1)
                pair = swap[:, :].rearrange("p (i e) -> p i e", e=2)
                pool.wait_ge(s_mask, 5)
                pool.affine_select(out=pair[:, :, 0], in_=pair[:, :, 0], compare_op=ALU.not_equal, fill=1.0,
                                   base=-1, pattern=[[-2, P // 2]], channel_multiplier=1).then_inc(s_mask, 1)
                pool.wait_ge(s_mask, 6)
                pool.affine_select(out=pair[:, :, 1], in_=pair[:, :, 1], compare_op=ALU.not_equal, fill=-1.0,
                                   base=0, pattern=[[-2, P // 2]], channel_multiplier=1).then_inc(s_mask, 1)
                pool.wait_ge(s_mask, 7)
                pool.memset(w["max_row"][:, :, :], 0.0).then_inc(s_rest, 1)
                pool.memset(w["c_t"][:, :, :].bitcast(F32), 0.0).then_inc(s_rest, 1)
                pool.wait_ge(s_rest, 2)

            @block.vector
            def _(dve):
                dve.wait_ge(s_in, 16)
                norm.normalise(dve)
                dve.wait_ge(s_mask, 7)
                dve.wait_ge(s_rot, 4 * 16)
                dve.tensor_scalar(diag[:, :], core.ident[:, :], cos_col[:, 0:1], None, ALU.mult).then_inc(s_step, 1)
                dve.tensor_scalar(turned[:, :], swap[:, :], sin_col[:, 0:1], None, ALU.mult).then_inc(s_step, 1)
                dve.wait_ge(s_step, 2)
                dve.tensor_tensor(core.rope[:, :], diag[:, :], turned[:, :], ALU.add).then_inc(s_step, 1)
                dve.tensor_tensor(core.rope_t[:, :], diag[:, :], turned[:, :], ALU.subtract).then_inc(s_step, 1)
                dve.wait_ge(s_step, 4)
                dve.wait_ge(norm.s_exact, TT)


def load_context(core, ctx_nat, sp, b, par):
    ctx = core.arg["ctx"]
    sp.dma_start(ctx_nat[par][:, 0:FULL, :],
                 ctx[bass.ds(b, 1), 0:FULL * P, :].rearrange("a (p t) e -> p (a t) e", t=FULL)
                 ).then_inc(core.ctx_in[par], 16)
    sp.dma_start(ctx_nat[par][0:TAIL, FULL, :],
                 ctx[bass.ds(b, 1), FULL * P:NCTX, :].rearrange("a p e -> (a p) e")
                 ).then_inc(core.ctx_in[par], 16)


def gather_cache(core, sp, index):
    for n in range(TOPK):
        blk = sp.value_load(index[0:1, n:n + 1], min_val=0, max_val=NBLK - 1)
        rows = slice((n * BLOCK) % P, (n * BLOCK) % P + BLOCK)
        for k, name in enumerate(("k_cache", "v_cache")):
            sp.dma_start(core.cache[rows, k, n * BLOCK // P, :],
                         core.arg[name][bass.ds(blk, 1)].rearrange("a k h d -> (a k) (h d)")
                         ).then_inc(core.cache_in, 16)


def load_kv_weights(core, kv, sp, g, par):
    rows = bass.ds(g * HD, HD)
    for k, name in enumerate(("wk", "wv")):
        sp.dma_start(kv["nat"][par][:, k, :], core.arg[name][rows, :]).then_inc(kv["in"][par], 16)


def load_query_weight(core, qo, sp, g, i):
    sp.dma_start(qo["wq"][:, i, :], core.arg["wq"][bass.ds(g * (REP * HD) + i * HD, HD), :]).then_inc(qo["wq_in"][i], 16)


def load_output_weight(core, qo, sp, g, i):
    sp.dma_start(qo["wo"][:, i, :, :],
                 core.arg["wo"].rearrange("(c o) n -> o c n", o=P)[:, :, bass.ds(g * (REP * HD) + i * HD, HD)]
                 ).then_inc(qo["wo_in"][i], 16)


def load_ffn_weights(core, ffn, sp, c, par):
    raw, done = ffn["raw"][par], ffn["in"][par]
    for k, pair in enumerate((("w1", "mean_w1"), ("w3", "mean_w3"))):
        for i, name in enumerate(pair):
            sp.dma_start(raw[:, k, i, :], core.arg[name][bass.ds(c * P, P), :]).then_inc(done, 16)
    for i, name in enumerate(("w2", "mean_w2")):
        sp.dma_start(raw[:, 2, i, :].rearrange("p (o n) -> p o n", o=DC),
                     core.arg[name].rearrange("(o p) n -> p o n", p=P)[:, :, bass.ds(c * P, P)]).then_inc(done, 16)


def cross_queries(core, w, xn_t):
    nc = core.nc
    with ExitStack() as own:
        cq_t = core.sb("cq_t", [LQ, TOK], ctx=own)
        s_cq = core.sem("cq_done", own)
        s_cq_sb = core.sem("cq_copied", own)
        s_q = core.sem("q_done", own)
        s_hi = core.sem("q_high_done", own)
        s_lo = core.sem("q_low_done", own)
        qt = w["q_t"]
        with nc.Block() as block:

            @block.tensor
            def _(pe):
                for c in range(DC):
                    mm = pe.matmul(core.psum[0:LQ, 4, :], w["wq_d"][:, c, :], xn_t[:, c, :],
                                   start=(c == 0), stop=(c == DC - 1))
                mm.then_inc(s_cq, 1)
                pe.wait_ge(s_cq_sb, 1)
                for h in range(XH):
                    wait(pe, s_lo, h - 3)
                    wait(pe, s_hi, h - 3)
                    pe.matmul(core.psum[0:2 * LKV, h % 4, :], w["w_qk"][:, h, :, :], cq_t[:, :],
                              start=True, stop=True).then_inc(s_q, 1)

            @block.scalar
            def _(act):
                act.wait_ge(s_cq, 1)
                act.activation(cq_t[:, :], core.psum[0:LQ, 4, :], ACT.Copy).then_inc(s_cq_sb, 1)
                for h in range(XH):
                    act.wait_ge(s_q, h + 1)
                    act.activation(qt[0:2 * LKV, :, h, :],
                                   core.psum[0:2 * LKV, h % 4, :].rearrange("p (b n) -> p b n", b=BATCH),
                                   ACT.Copy).then_inc(s_hi, 1)

            @block.vector
            def _(dve):
                for h in range(XH):
                    dve.wait_ge(s_hi, h + 1)
                    dve.tensor_tensor(qt[2 * LKV:SHIFT, :, h, :],
                                      core.psum[0:LKV, h % 4, :].rearrange("p (b n) -> p b n", b=BATCH),
                                      qt[0:LKV, :, h, :],
                                      ALU.subtract).then_inc(s_lo, 1)
                dve.wait_ge(s_lo, XH)


PREP = [("turn", t) for t in range(KT)] + [("compress", 0), ("natural", 0)] + [("stack", k) for k in range(4)]
PREP_SLOT = [t // 2 for t in range(KT)] + [7, 8, 11, 11, 12, 12]
PREP_ON_ACT = [kind == "turn" and t % 3 < 2 or kind == "compress" or kind == "stack" and t % 2 == 0
               for kind, t in PREP]
PREP_BANK = [(7, 2)[n % 2] for n in range(len(PREP))]
ACT_PREPS = sum(PREP_ON_ACT)
DVE_PREPS = len(PREP) - ACT_PREPS
PIECES = 4
PIECE_KEYS = (402, 400, 400, 400)
PIECE_AT = (0, 402, 802, 1202)
assert sum(PIECE_KEYS) == NCTX + 1
MAXIMA = PIECES * QTILES
MAX_SLOT = [i * (KT - 1) // MAXIMA for i in range(MAXIMA)]
ABS_SLOT = PREP_SLOT[KT]
MIX_BANKS = (3, 6)
MAX_BANKS = (0, 1, 3)


def score_bank(b, t):
    return 0 if isinstance(b, int) and b == BATCH - 1 and t % 2 == 1 else 4


def stack_tiles(k):
    return [t for t in range(4 * k, min(4 * k + 4, KT))]


def rows_of(t):
    return P if t < FULL else TAIL


def cross_attention(core, w, own):
    nc, arg, psum = core.nc, core.arg, core.psum
    ctx_nat = w["ctx_nat"]
    index = core.sb("index", [1, TOPK], I32, ctx=own)
    ctx_t = core.sb("ctx_t", [P, DC, KT * P], ctx=own)
    c_parts = core.sb("c_parts", [P, MAIN + TAIL], ctx=own)
    q_now = [core.sb(f"q_now{i}", [P, XQ], F32R, ctx=own) for i in range(2)]
    max_part = core.sb("max_part", [P, QTILES, PIECES], ctx=own)
    probs = [core.sb(f"probs{i}", [P, XQ], ctx=own) for i in range(2)]
    u_t = core.sb("u_t", [P, XQ // 2], ctx=own)
    rden = core.sb("rden", [P, XH], ctx=own)
    mixed = core.sb("mixed", [P, XH, XHD], ctx=own)
    zero = core.sb("zero", [P, 1], ctx=own)
    w_raw = core.sb("w_raw", [P, 3, 2, PIECE], ctx=own)
    c_stage = w["c_stage"]
    c_nat, c_stack, c_t, max_row, q_t = w["c_nat"], w["c_stack"], w["c_t"], w["max_row"], w["q_t"]

    s_ctx = core.ctx_in
    s_idx = core.sem("index_in", own)
    s_zero = core.sem("zero_ready", own)
    s_raw = core.sem("w_raw_in", own)
    s_diff = core.sem("w_diff_done", own)
    s_abs = core.sem("w_abs_done", own)
    s_prep = core.sem("prep_psum_done", own)
    s_pact = core.sem("prep_out_by_act", own)
    s_pdve = core.sem("prep_out_by_dve", own)
    s_part = core.sem("c_stack_part_done", own)
    s_cnat = core.sem("values_placed", own)
    s_qnow = core.sem("q_now_done", own)
    s_sa = core.sem("max_scores_done", own)
    s_max = core.sem("max_part_done", own)
    s_neg = core.sem("max_negated", own)
    s_mt = core.sem("max_turned", own)
    s_shift = core.sem("shift_row_done", own)
    s_sb = core.sem("scores_done", own)
    s_exp = core.sem("probs_done", own)
    s_pv = core.sem("probs_used", own)
    s_u = core.sem("u_copied", own)
    s_o = core.sem("mix_done", own)
    s_rd = core.sem("den_inverted", own)
    s_mix = core.sem("mix_scaled", own)
    s_x = core.sem("x_updated", own)

    wnames = (("w1", "mean_w1"), ("w3", "mean_w3"), ("w2", "mean_w2"))
    flat = {n: arg[n].rearrange("r c -> (r c)").rearrange("(p f) -> p f", p=P) for pair in wnames for n in pair}

    def prep_out_wait(eng, b, n):
        wait(eng, s_pact, ACT_PREPS * b + sum(PREP_ON_ACT[:n]))
        wait(eng, s_pdve, DVE_PREPS * b + n - sum(PREP_ON_ACT[:n]))

    steps_static = [(-2, None, None, 0), (-1, None, 0, 1), (0, 0, 1, 2), (1, 1, 2, 3)]
    steps_end = [(6, 6, 7, None), (7, 7, None, None)]

    def run(eng, step):
        for s, back, lead, prep in steps_static:
            step(back, lead, prep, s % 2, s // 2)
        with eng.Fori(1, (BATCH - 2) // 2) as j:
            step(2 * j, 2 * j + 1, 2 * j + 2, 0, j)
            step(2 * j + 1, 2 * j + 2, 2 * j + 3, 1, j)
        for s, back, lead, prep in steps_end:
            step(back, lead, prep, s % 2, s // 2)

    with nc.Block() as block:

        @block.sync
        def _(sp):
            def load_pieces(b):
                wait(sp, s_abs, 3 * b)
                for k, pair in enumerate(wnames):
                    for i, n in enumerate(pair):
                        sp.dma_start(w_raw[:, k, i, :], flat[n][:, bass.ds(b * PIECE, PIECE)]).then_inc(s_raw, 16)

            def load(b, par):
                wait(sp, s_prep, len(PREP) * (b - 2) + KT)
                load_context(core, ctx_nat, sp, b, par)
                load_pieces(b)

            load_pieces(0)
            load_pieces(1)
            sp.dma_start(index[:, :], arg["block_idx"].rearrange("(a k) -> a k", a=1)).then_inc(s_idx, 16)
            with sp.Fori(1, BATCH // 2) as j:
                load(2 * j, 0)
                load(2 * j + 1, 1)
            sp.wait_ge(s_idx, 16)
            sp.wait_ge(s_prep, len(PREP) * (BATCH - 2) + KT)
            gather_cache(core, sp, index)

        @block.gpsimd
        def _(pool):
            def place_queries(b, par):
                wait(pool, s_sb, KT * (b - 1))
                pool.tensor_copy(q_now[par][0:SHIFT, :].rearrange("p (h n) -> p h n", h=XH),
                                 q_t[:, bass.ds(b, 1), :, :].rearrange("p a h n -> p (a h) n")
                                 ).then_inc(s_qnow, 1)

            def step(back, lead, prep, par, pair):
                if prep is None:
                    return
                if back is None:
                    place_queries(prep, par)
                pool.wait_ge(s_raw, 96 * (prep + 1))
                if isinstance(prep, int) and prep == 0:
                    pool.wait_ge(s_zero, 1)
                for k in range(3):
                    pool.tensor_tensor(w_raw[:, k, 0, :], w_raw[:, k, 0, :], w_raw[:, k, 1, :],
                                       ALU.subtract).then_inc(s_diff, 1)
                natural = PREP.index(("natural", 0))
                pool.wait_ge(s_pdve, DVE_PREPS * prep + natural + 1 - sum(PREP_ON_ACT[:natural + 1]))
                stand_alone(pool, core)
                wait(pool, s_prep, len(PREP) * prep)
                hi = c_stack[:, :, 0:LKV]
                pool.tensor_tensor(hi.bitcast(F32R), c_stage[:, :, :],
                                   zero[:, 0:1].unsqueeze(2).to_broadcast([P, KT, LKV]), ALU.add).then_inc(s_part, 1)
                stand_alone(pool, core)
                pool.wait_ge(s_part, 3 * prep + 1)
                pool.tensor_tensor(c_stack[:, :, LKV:2 * LKV], c_stage[:, :, :], hi, ALU.subtract).then_inc(s_part, 1)
                pool.tensor_copy(c_stack[:, :, 2 * LKV:SHIFT], hi).then_inc(s_part, 1)
                if back is not None:
                    stand_alone(pool, core)
                    place_queries(prep, par)
                stand_alone(pool, core)
                wait(pool, s_pv, KT * (prep - 1))
                pool.tensor_copy(c_nat[:, par, :, 0:LKV], c_stage[:, :, :]).then_inc(s_cnat, 1)

            pool.memset(zero[:, :], 0.0).then_inc(s_zero, 1)
            run(pool, step)

        @block.tensor
        def _(pe):
            def prep_item(b, par, n):
                kind, t = PREP[n]
                bank = PREP_BANK[n]
                prep_out_wait(pe, b, n if n == 0 or kind in ("compress", "natural") else n - 1)
                if kind == "turn":
                    if t == 0:
                        pe.wait_ge(s_ctx[par], 16 * b + (32 if par == 0 else 16))
                    rows = rows_of(t)
                    for c in range(DC):
                        mm = pe.transpose(psum[:, bank, c * P:c * P + rows], ctx_nat[par][0:rows, t, c * P:(c + 1) * P],
                                          core.ident[0:rows, 0:rows])
                elif kind == "compress":
                    for c in range(DC):
                        for g in range(GROUPS):
                            pe.matmul(psum[g * LKV:(g + 1) * LKV, bank, 0:MAIN], w["wkv_d"][:, c, :],
                                      ctx_t[:, c, g * MAIN:(g + 1) * MAIN], start=(c == 0), stop=(c == DC - 1))
                    for c in range(DC):
                        mm = pe.matmul(psum[0:LKV, bank, MAIN:MAIN + TAIL], w["wkv_d"][:, c, :],
                                       ctx_t[:, c, FULL * P:NCTX], start=(c == 0), stop=(c == DC - 1))
                elif kind == "natural":
                    for i in range(PER_GROUP):
                        pe.transpose(psum[:, bank, i * P:(i + 1) * P], c_parts[:, i * P:(i + 1) * P], core.ident[:, :])
                    mm = pe.transpose(psum[0:TAIL, bank, MAIN:MAIN + LKV], c_parts[0:LKV, MAIN:MAIN + TAIL],
                                      core.ident[0:LKV, 0:LKV])
                else:
                    pe.wait_ge(s_part, 3 * (b + 1))
                    for i, tile in enumerate(stack_tiles(t)):
                        rows = rows_of(tile)
                        mm = pe.transpose(psum[0:STACK, bank, i * P:i * P + rows], c_stack[0:rows, tile, 0:STACK],
                                          core.ident[0:rows, 0:rows])
                mm.then_inc(s_prep, 1)

            def max_scores(b, par, i):
                qt, piece = divmod(i, PIECES)
                wait(pe, s_max, MAXIMA * b + i - len(MAX_BANKS) + 1)
                if i == MAX_BANKS.index(MIX_BANKS[0]):
                    wait(pe, s_mix, b - 1)
                if i == 0:
                    prep_out_wait(pe, b, len(PREP))
                    pe.wait_ge(s_qnow, b + 1)
                    wait(pe, s_shift, b)
                width = PIECE_KEYS[piece]
                pe.matmul(psum[:, MAX_BANKS[i % len(MAX_BANKS)], 0:width], q_now[par][0:SHIFT, qt * P:(qt + 1) * P],
                          c_t[0:SHIFT, par, PIECE_AT[piece]:PIECE_AT[piece] + width],
                          start=True, stop=True).then_inc(s_sa, 1)

            def turn_max(b):
                pe.wait_ge(s_neg, b + 1)
                for qt in range(QTILES):
                    mm = pe.transpose(psum[0:STACK, qt // 4, (qt % 4) * P:(qt % 4 + 1) * P], max_row[:, qt, :],
                                      core.ident[:, :])
                mm.then_inc(s_mt, 1)

            def scores(b, par, t):
                alone = isinstance(b, int) and b == BATCH - 1
                wait(pe, s_exp, KT * b + t - (1 if alone and t else 0))
                bank = score_bank(b, t)
                if t == 0:
                    pe.wait_ge(s_shift, b + 1)
                lhs = c_t[0:STACK, par, t * P:t * P + rows_of(t)]
                for half in range(2):
                    mm = pe.matmul(psum[0:rows_of(t), bank + half, :], lhs,
                                   q_now[par][0:STACK, half * BANK:(half + 1) * BANK], start=True, stop=True)
                mm.then_inc(s_sb, 1)

            def values(b, par, t):
                pe.wait_ge(s_exp, KT * b + t + 1)
                if t == 0:
                    pe.wait_ge(s_cnat, b + 1)
                    wait(pe, s_mix, b)
                for half in range(2):
                    mm = pe.matmul(psum[half * UW:(half + 1) * UW, 6, :], c_nat[0:rows_of(t), par, t, :],
                                   probs[t % 2][0:rows_of(t), half * BANK:(half + 1) * BANK],
                                   start=(t == 0), stop=(t == KT - 1))
                mm.then_inc(s_pv, 1)

            def mix(b, par):
                stand_alone(pe, core)
                pe.wait_ge(s_u, b + 1)
                for h in range(XH):
                    base = UW * (h // 8)
                    cols = slice((h % 8) * SEQ, (h % 8 + 1) * SEQ)
                    mm = pe.matmul(psum[par * SEQ:(par + 1) * SEQ, MIX_BANKS[h // 8], (h % 8) * OW:(h % 8 + 1) * OW],
                                   u_t[base:base + LKV + 1, cols], w["wv_u"][base:base + LKV + 1, h, :],
                                   start=True, stop=True)
                mm.then_inc(s_o, 1)

            def step(back, lead, prep, par, pair):
                for slot in range(KT):
                    if back is not None:
                        scores(back, par, slot)
                    preps = [n for n, at in enumerate(PREP_SLOT) if at == slot and prep is not None]
                    maxima = [i for i, at in enumerate(MAX_SLOT) if at == slot and lead is not None]
                    for k in range(max(len(preps), len(maxima))):
                        if k < len(maxima):
                            max_scores(lead, 1 - par, maxima[k])
                        if k < len(preps):
                            prep_item(prep, par, preps[k])
                    if back is not None and slot > 0:
                        values(back, par, slot - 1)
                if back is not None:
                    values(back, par, KT - 1)
                if lead is not None:
                    turn_max(lead)
                if back is not None:
                    mix(back, par)

            run(pe, step)

        def prep_out(eng, on_act, b, par, n):
            kind, t = PREP[n]
            bank = PREP_BANK[n]
            done = s_pact if on_act else s_pdve

            def copy(dst, src):
                return eng.activation(dst, src, ACT.Copy) if on_act else eng.tensor_copy(dst, src)

            eng.wait_ge(s_prep, len(PREP) * b + n + 1)
            if kind == "turn":
                rows = rows_of(t)
                copy(ctx_t[:, :, t * P:t * P + rows],
                     psum[:, bank, :].rearrange("p (c r) -> p c r", c=DC)[:, :, 0:rows]).then_inc(done, 1)
            elif kind == "compress":
                copy(c_parts[:, 0:MAIN], psum[:, bank, 0:MAIN])
                copy(c_parts[0:LKV, MAIN:MAIN + TAIL], psum[0:LKV, bank, MAIN:MAIN + TAIL]).then_inc(done, 1)
            elif kind == "natural":
                wait(eng, s_cnat, b)
                copy(c_stage[:, 0:FULL, :].rearrange("p (g i) l -> p i g l", g=GROUPS),
                     psum[:, bank, 0:MAIN].rearrange("p (i g l) -> p i g l", i=PER_GROUP, g=GROUPS))
                copy(c_stage[0:TAIL, FULL, :], psum[0:TAIL, bank, MAIN:MAIN + LKV]).then_inc(done, 1)
            else:
                tiles = stack_tiles(t)
                width = sum(rows_of(x) for x in tiles)
                wait(eng, s_sb, KT * (b - 2) + tiles[-1] + 1)
                copy(c_t[0:STACK, par, t * BANK:t * BANK + width], psum[0:STACK, bank, 0:width]).then_inc(done, 1)

        @block.scalar
        def _(act):
            def step(back, lead, prep, par, pair):
                for slot in range(KT):
                    if back is not None:
                        rows = rows_of(slot)
                        act.wait_ge(s_sb, KT * back + slot + 1)
                        wait(act, s_pv, KT * back + (slot - 1 if slot else 0))
                        act.activation(probs[slot % 2][0:rows, :].rearrange("p (a n) -> p a n", a=2),
                                       psum[0:rows, score_bank(back, slot):score_bank(back, slot) + 2, :],
                                       ACT.Exp, scale=XSCALE).then_inc(s_exp, 1)
                    if prep is not None:
                        for n, at in enumerate(PREP_SLOT):
                            if at == slot and PREP_ON_ACT[n]:
                                prep_out(act, True, prep, par, n)
                if lead is not None:
                    act.wait_ge(s_mt, lead + 1)
                    act.activation(q_now[1 - par][SHIFT:STACK, :].rearrange("p (a n) -> p a n", a=2),
                                   psum[SHIFT:STACK, 0:2, :], ACT.Copy).then_inc(s_shift, 1)

            run(act, step)

        @block.vector
        def _(dve):
            def take_max(b, i):
                qt, piece = divmod(i, PIECES)
                width = PIECE_KEYS[piece] - (piece == PIECES - 1)
                dve.wait_ge(s_sa, MAXIMA * b + i + 1)
                if i == 0:
                    wait(dve, s_neg, b)
                dve.tensor_reduce(max_part[:, qt, piece:piece + 1], psum[:, MAX_BANKS[i % len(MAX_BANKS)], 0:width],
                                  AX.X, ALU.max).then_inc(s_max, 1)

            def abs_sum(b, k):
                dve.wait_ge(s_diff, 3 * b + k + 1)
                dve.tensor_reduce(core.abs_sum[:, bass.ds(b, 1), k], w_raw[:, k, 0, :], AX.X, ALU.add,
                                  apply_absolute_value=True).then_inc(s_abs, 1)

            def step(back, lead, prep, par, pair):
                for slot in range(KT):
                    preps = [n for n, at in enumerate(PREP_SLOT)
                             if at == slot and prep is not None and not PREP_ON_ACT[n]]
                    maxima = [i for i, at in enumerate(MAX_SLOT) if at == slot and lead is not None]
                    for k in range(max(len(preps), len(maxima), 1)):
                        if k < len(maxima):
                            take_max(lead, maxima[k])
                        if k < len(preps):
                            prep_out(dve, False, prep, par, preps[k])
                        if k == 0 and slot == ABS_SLOT and prep is not None:
                            abs_sum(prep, 0)
                            abs_sum(prep, 1)
                if lead is not None:
                    dve.wait_ge(s_max, MAXIMA * (lead + 1))
                    wait(dve, s_mt, lead)
                    dve.tensor_reduce(max_row[:, :, SHIFT], max_part[:, :, :], AX.X, ALU.max,
                                      negate=True).then_inc(s_neg, 1)
                if prep is not None:
                    abs_sum(prep, 2)
                if back is not None:
                    dve.wait_ge(s_pv, KT * (back + 1))
                    wait(dve, s_o, back)
                    dve.tensor_copy(u_t[:, :], psum[:, 6, :]).then_inc(s_u, 1)
                    half_rows = slice(par * SEQ, (par + 1) * SEQ)
                    out = [psum[half_rows, bank, 0:8 * OW].rearrange("p (h w) -> p h w", h=8) for bank in MIX_BANKS]
                    dve.wait_ge(s_o, back + 1)
                    for a in range(2):
                        inverted = dve.reciprocal(rden[half_rows, 8 * a:8 * a + 8], out[a][:, :, XHD])
                    inverted.then_inc(s_rd, 1)
                    dve.wait_ge(s_rd, back + 1)
                    mixed_v = mixed[half_rows, :, :]
                    for a in range(2):
                        mm = dve.tensor_tensor(mixed_v[:, 8 * a:8 * a + 8, :], out[a][:, :, 0:XHD],
                                               rden[half_rows, 8 * a:8 * a + 8].unsqueeze(2).to_broadcast(
                                                   [SEQ, 8, XHD]), ALU.mult)
                    mm.then_inc(s_mix, 1)
                    dve.wait_ge(s_mix, back + 1)
                    row = core.x[half_rows, bass.ds(pair, 1), :].rearrange("p a e -> p (a e)")
                    dve.tensor_tensor(row, row, mixed_v.rearrange("p h d -> p (h d)"), ALU.add).then_inc(s_x, 1)

            run(dve, step)
            dve.wait_ge(s_x, BATCH)


def rotated_keys(core, own, norm, kv, qo, k_sel, xe, k_high, k_low, v_new):
    nc, arg, psum = core.nc, core.arg, core.psum
    kv_nat, s_w = kv["nat"], kv["in"]
    kv_t = core.sb("kv_weight_t", [P, 2, DC, P], ctx=own)
    k_group = core.sb("k_group", [P, ST, HD], ctx=own)
    new_t = core.sb("new_key_t", [P, SEQ], ctx=own)
    keys_t = core.sb("keys_t", [P, KEYS], ctx=own)
    s_kg = core.sem("group_keys_placed", own)
    s_tr = core.sem("kv_weight_turned", own)
    s_sel = core.sem("group_keys_turned", own)
    s_kt = core.sem("key_weight_copied", own)
    s_vt = core.sem("value_weight_copied", own)
    s_new = core.sem("new_key_done", own)
    s_vnew = core.sem("new_value_done", own)
    s_newsb = core.sem("new_key_copied", own)
    s_vsb = core.sem("new_value_copied", own)
    s_rot = core.sem("new_key_rotated", own)
    s_selsb = core.sem("group_keys_copied", own)
    s_rotsb = core.sem("rotated_copied", own)
    s_back = core.sem("rotated_back", own)
    s_hi = core.sem("keys_high_done", own)
    s_lo = core.sem("keys_low_done", own)

    with nc.Block() as block:

        @block.sync
        def _(sp):
            def load(g, par):
                wait(sp, s_tr, g - 1)
                load_kv_weights(core, kv, sp, g, par)

            for g in range(2):
                load_kv_weights(core, kv, sp, g, g)
            for i in range(REP):
                load_query_weight(core, qo, sp, 0, i)
                load_output_weight(core, qo, sp, 0, i)
            with sp.Fori(1, NKV // 2) as j:
                load(2 * j, 0)
                load(2 * j + 1, 1)

        @block.gpsimd
        def _(pool):
            pool.wait_ge(core.cache_in, 2 * TOPK * 16)
            pool.tensor_copy(k_group[:, :, :], k_sel[:, :, 0:HD]).then_inc(s_kg, 1)
            with pool.Fori(1, NKV) as g:
                pool.wait_ge(s_sel, g)
                pool.tensor_copy(k_group[:, :, :], k_sel[:, :, bass.ds(g * HD, HD)]).then_inc(s_kg, 1)

        def run(eng, group):
            group(0, 0, True)
            group(1, 1, True)
            with eng.Fori(1, NKV // 2 - 1) as j:
                group(2 * j, 0, True)
                group(2 * j + 1, 1, True)
            group(NKV - 2, 0, True)
            group(NKV - 1, 1, False)

        @block.tensor
        def _(pe):
            def turn_weights(g, par):
                pe.wait_ge(s_w[par], 16 * g + (32 if par == 0 else 16))
                wait(pe, s_kt, g)
                wait(pe, s_vt, g)
                for k in range(2):
                    for c in range(DC):
                        mm = pe.transpose(psum[:, k, c * P:(c + 1) * P], kv_nat[par][:, k, c * P:(c + 1) * P],
                                          core.ident[:, :])
                mm.then_inc(s_tr, 1)

            def turn_gathered(g):
                pe.wait_ge(s_kg, g + 1)
                wait(pe, s_selsb, g)
                for t in range(ST):
                    mm = pe.transpose(psum[:, 2, t * P:(t + 1) * P], k_group[:, t, :], core.ident[:, :])
                mm.then_inc(s_sel, 1)

            def group(g, par, more):
                pe.wait_ge(s_kt, g + 1)
                wait(pe, s_newsb, g)
                for c in range(DC):
                    mm = pe.matmul(psum[:, 3, 0:SEQ], kv_t[:, 0, c, :], xe[:, c, :], start=(c == 0), stop=(c == DC - 1))
                mm.then_inc(s_new, 1)
                pe.wait_ge(s_vt, g + 1)
                wait(pe, s_vsb, g)
                for c in range(DC):
                    mm = pe.matmul(psum[0:SEQ, 4, 0:P], xe[:, c, :], kv_t[:, 1, c, :],
                                   start=(c == 0), stop=(c == DC - 1))
                mm.then_inc(s_vnew, 1)
                if more:
                    turn_weights(g + 1, 1 - par)
                pe.wait_ge(s_newsb, g + 1)
                wait(pe, s_rotsb, g)
                pe.matmul(psum[:, 5, 0:SEQ], core.rope_t[:, :], new_t[:, :], start=True, stop=True).then_inc(s_rot, 1)
                pe.wait_ge(s_selsb, g + 1)
                wait(pe, s_lo, 2 * g)
                pe.matmul(psum[:, 6, :], core.rope[:, :], keys_t[:, 0:NSEL], start=True, stop=True).then_inc(s_back, 1)
                if more:
                    turn_gathered(g + 1)
                pe.wait_ge(s_rotsb, g + 1)
                pe.matmul(psum[:, 7, 0:SEQ], core.rope[:, :], keys_t[:, NSEL:KEYS],
                          start=True, stop=True).then_inc(s_back, 1)

            turn_weights(0, 0)
            turn_gathered(0)
            norm.turn(pe)
            pe.wait_ge(norm.s_exact, 1)
            pe.wait_ge(norm.s_low, TT)
            run(pe, group)

        @block.scalar
        def _(act):
            def key_weight(g):
                act.wait_ge(s_tr, g + 1)
                act.activation(kv_t[:, 0, :, :], psum[:, 0, :].rearrange("p (c t) -> p c t", c=DC),
                               ACT.Copy).then_inc(s_kt, 1)

            def gathered(g):
                act.wait_ge(s_sel, g + 1)
                act.activation(keys_t[:, 0:NSEL], psum[:, 2, :], ACT.Copy).then_inc(s_selsb, 1)

            def high(g, n, keys, src):
                act.wait_ge(s_back, 2 * g + n + 1)
                act.activation(k_high[:, keys], src, ACT.Copy, scale=GSCALE).then_inc(s_hi, 1)

            def group(g, par, more):
                act.wait_ge(s_vnew, g + 1)
                for rows in (slice(0, SEQ), slice(SEQ, 2 * SEQ)):
                    copied = act.activation(v_new[rows, bass.ds(g, 1), :].rearrange("p a d -> p (a d)"),
                                            psum[0:SEQ, 4, 0:P], ACT.Copy)
                copied.then_inc(s_vsb, 1)
                if more:
                    key_weight(g + 1)
                high(g, 0, bass.ds(g * KEYS, NSEL), psum[:, 6, :])
                if more:
                    gathered(g + 1)
                high(g, 1, bass.ds(g * KEYS + NSEL, SEQ), psum[:, 7, 0:SEQ])

            norm.root(act)
            key_weight(0)
            gathered(0)
            norm.copy_out(act)
            run(act, group)

        @block.vector
        def _(dve):
            def value_weight(g):
                dve.wait_ge(s_tr, g + 1)
                dve.tensor_copy(kv_t[:, 1, :, :], psum[:, 1, :].rearrange("p (c t) -> p c t", c=DC)).then_inc(s_vt, 1)

            def group(g, par, more):
                dve.wait_ge(s_new, g + 1)
                dve.tensor_copy(new_t[:, :], psum[:, 3, 0:SEQ]).then_inc(s_newsb, 1)
                if more:
                    value_weight(g + 1)
                dve.wait_ge(s_rot, g + 1)
                dve.tensor_copy(keys_t[:, NSEL:KEYS], psum[:, 5, 0:SEQ]).then_inc(s_rotsb, 1)
                for n, (keys, src) in enumerate(((bass.ds(g * KEYS, NSEL), psum[:, 6, :]),
                                                 (bass.ds(g * KEYS + NSEL, SEQ), psum[:, 7, 0:SEQ]))):
                    dve.wait_ge(s_hi, 2 * g + n + 1)
                    dve.scalar_tensor_tensor(out=k_low[:, keys], in0=src, scalar=GSCALE, in1=k_high[:, keys],
                                             op0=ALU.mult, op1=ALU.subtract).then_inc(s_lo, 1)

            norm.normalise(dve)
            value_weight(0)
            norm.low_parts(dve)
            run(dve, group)
            dve.wait_ge(s_lo, 2 * NKV)


HEAD_FIRST_USE = (0, 10, 16, 22)
QUERY_PARTS = ((range(0, 3), range(3, 4), range(4, 5), range(5, 3 * DC)),
               (range(0, 2), range(2, 3), range(3, 4), range(4, 3 * DC)))


def weights_missing(g, i, k):
    if not isinstance(g, int):
        return 0
    before = max(REP * g + i - (NH - 2), 0)
    return before + (1 if k > 4 and REP * g + i >= NH - 2 else 0)


def turn_use(g, i, k):
    late = weights_missing(g, i, k)
    bank = 4 + (k + late) % 2
    if isinstance(g, int) and g == 0 and i == 0:
        return (2 if k == 4 else 3), bank
    return 28 * g + HEAD_FIRST_USE[i] + k - 6 - late, bank


def grouped_attention(core, own, qo, ffn, xh, xl, k_high, k_low, v_sel, v_new):
    nc, arg, psum = core.nc, core.arg, core.psum
    wq_nat, wo_nat, wq_in, wo_in = qo["wq"], qo["wo"], qo["wq_in"], qo["wo_in"]
    wq_t = [core.sb(f"wq_t_{s}", [P, DC, HD], F32R, ctx=own) for s in ("high", "low")]
    wo_t = [core.sb(f"wo_t_{s}", [P, REP, DIM], F32R, ctx=own) for s in ("high", "low")]
    q_t = [core.sb(f"query_t_{s}", [P, TOK], F32R, ctx=own) for s in ("high", "low")]
    value = [core.sb(f"value_{s}", [P, ST + 1, HD], F32R, ctx=own) for s in ("high", "low")]
    probs = core.sb("head_probs", [P, TT, KEYS], ctx=own)
    probs_t = [core.sb("probs_t_high", [P, ST + 1, TOK], F32R, ctx=own),
               core.sb("probs_t_low", [P, ST, TOK], F32R, ctx=own)]
    mixed_t = [core.sb(f"mixed_t_{s}", [P, REP, TOK], F32R, ctx=own) for s in ("high", "low")]
    neg_max = core.sb("neg_max", [P, TT], ctx=own)
    den = core.sb("den", [P, TT], ctx=own)
    rden = core.sb("inverse_den", [P, TT], ctx=own)
    names = {
        "wqt": "query_weight_turned",
        "wot": "output_weight_turned", "q": "queries_done", "qh": "queries_high_done", "ql": "queries_low_done",
        "s": "head_scores_done", "max": "head_max_done", "exp": "head_probs_done", "rd": "head_den_inverted",
        "norm": "head_probs_scaled", "pt": "head_probs_turned", "th": "turned_high_done", "tl": "turned_low_done",
        "tailh": "tail_high_done", "taill": "tail_low_done", "wqh": "query_weight_high_done",
        "woh": "output_weight_high_done", "vh": "value_high_done", "vl": "value_low_done", "pv": "head_mix_done",
        "ah": "mix_high_done", "al": "mix_low_done", "o": "output_tile_done",
    }
    s = {k: core.sem(v, own) for k, v in names.items()}

    def has_weight(g, i):
        return not isinstance(g, int) or REP * g + i < NH - 2

    def run(eng, head):
        for i in range(REP):
            head(0, i, True, i > 0, True)
        with eng.Fori(1, NKV - 1) as g:
            for i in range(REP):
                head(g, i, True, True, True)
        for i in range(REP):
            head(NKV - 1, i, True, True, i < REP - 1)
        head(NKV, 0, False, True, False)

    with nc.Block() as block:

        @block.sync
        def _(sp):
            load_ffn_weights(core, ffn, sp, 0, 0)
            with sp.Fori(1, NKV) as g:
                for i in range(REP):
                    wait(sp, s["wqt"], REP * (g - 1) + i + 1)
                    load_query_weight(core, qo, sp, g, i)
                    stand_alone(sp, core)
                    wait(sp, s["wot"], REP * (g - 1) + i + 1)
                    load_output_weight(core, qo, sp, g, i)

        @block.tensor
        def _(pe):
            def use_bank(use):
                before, bank = use
                wait(pe, s["tl"], before - 1)
                return psum[:, bank, :]

            def queries(products):
                for k in products:
                    (a, b), c = PASSES[k // DC], k % DC
                    mm = pe.matmul(psum[:, 7, :], wq_t[a][:, c, :], (xh, xl)[b][:, c, :],
                                   start=(k == 0), stop=(k == 3 * DC - 1))
                if products[-1] == 3 * DC - 1:
                    mm.then_inc(s["q"], 1)

            def score(g, n, qt):
                wait(pe, s["exp"], TT * n + qt - 1)
                if qt == 0:
                    pe.wait_ge(s["ql"], n + 1)
                for half in range(2):
                    bank = 2 * (qt % 2) + half
                    keys = bass.ds(g * KEYS + half * HALF, HALF)
                    for step, (a, b) in enumerate(PASSES):
                        mm = pe.matmul(psum[:, bank, 0:HALF], q_t[a][:, qt * P:(qt + 1) * P],
                                       (k_high, k_low)[b][:, keys], start=(step == 0), stop=(step == 2))
                mm.then_inc(s["s"], 1)

            def turn_probs(bank, last, qt):
                pe.wait_ge(s["norm"], TT * last + qt + 1)
                if qt == 0:
                    wait(pe, s["al"], last)
                for t in range(ST):
                    pe.transpose(bank[:, t * P:(t + 1) * P], probs[:, qt, t * P:(t + 1) * P], core.ident[:, :])
                pe.transpose(psum[0:SEQ, 6, qt * P:(qt + 1) * P], probs[:, qt, NSEL:KEYS],
                             core.ident[:, :]).then_inc(s["pt"], 1)

            def mix(last):
                pe.wait_ge(s["taill"], last + 1)
                pe.wait_ge(s["vl"], 2 * ((last // REP) + 1) if isinstance(last, int) else vl_at[0])
                for step, (a, b) in enumerate(PASSES):
                    for t in range(ST):
                        pe.matmul(psum[:, 6, :], value[a][:, t, :], probs_t[b][:, t, :],
                                  start=(step == 0 and t == 0), stop=False)
                pe.matmul(psum[:, 6, :], value[0][:, ST, :], probs_t[0][:, ST, :], start=False, stop=False)
                pe.matmul(psum[:, 6, :], value[1][0:SEQ, ST, :], probs_t[0][0:SEQ, ST, :],
                          start=False, stop=True).then_inc(s["pv"], 1)

            def output(g, qt, bank):
                for i in range(REP):
                    if i == REP - 1:
                        wait(pe, s["al"], REP * g)
                    for step, (a, b) in enumerate(PASSES):
                        mm = pe.matmul(bank, mixed_t[a][:, i, qt * P:(qt + 1) * P], wo_t[b][:, i, :],
                                       start=(i == 0 and step == 0), stop=(i == REP - 1 and step == 2))
                mm.then_inc(s["o"], 1)

            vl_at = [None]

            def turn_query_weight(g, i, bank):
                pe.wait_ge(wq_in[i], 16 * (g + 1))
                for c in range(DC):
                    mm = pe.transpose(bank[:, c * P:(c + 1) * P], wq_nat[:, i, c * P:(c + 1) * P], core.ident[:, :])
                mm.then_inc(s["wqt"], 1)

            def turn_output_weight(g, i):
                bank = use_bank(turn_use(g, i, 9 if i == 0 else 5))
                pe.wait_ge(wo_in[i], 16 * (g + 1))
                for c in range(DC):
                    mm = pe.transpose(bank[:, c * P:(c + 1) * P], wo_nat[:, i, c, :], core.ident[:, :])
                mm.then_inc(s["wot"], 1)

            def weight_turned(g, i):
                if isinstance(g, int) and g == 0:
                    return 2 if i == 0 else turn_use(0, i - 1, 4)[0] + 1
                start = turn_use(g, i, 0)[0]
                return start - (1 + TT if i == 1 else 1)

            def head(g, i, this, last, nxt):
                n = REP * g + i
                vl_at[0] = 2 * g + (2 if i else 0)
                for qt in range(TT):
                    if this:
                        score(g, n, qt)
                    if nxt and qt < TT - 1:
                        if qt == 0:
                            pe.wait_ge(s["tl"], weight_turned(g, i))
                        queries(QUERY_PARTS[i == 0][qt])
                    if last:
                        turn_probs(use_bank(turn_use(g, i, qt)), n - 1, qt)
                if nxt:
                    queries(QUERY_PARTS[i == 0][TT - 1])
                if nxt and has_weight(g, i):
                    turn_query_weight(g + (i + 2) // REP, (i + 2) % REP, use_bank(turn_use(g, i, 4)))
                if this and i > 0:
                    turn_output_weight(g, i)
                if last:
                    mix(n - 1)
                if i == 0 and last:
                    for qt in range(TT):
                        output(g, qt, use_bank(turn_use(g, 0, 5 + qt)))
                if this and i == 0:
                    turn_output_weight(g, i)

            turn_query_weight(0, 0, psum[:, 4, :])
            pe.wait_ge(s["tl"], 1)
            queries(range(3 * DC))
            turn_query_weight(0, 1, psum[:, 5, :])
            run(pe, head)

        @block.scalar
        def _(act):
            flat_high = wq_t[0][:, :, :].rearrange("p c d -> p (c d)")

            def weight_high(done, count, bank, dst):
                act.wait_ge(done, count)
                act.activation(dst, psum[:, bank, :], ACT.Copy).then_inc(s["th"], 1)

            def queries_high(n):
                act.wait_ge(s["q"], n + 1)
                act.activation(q_t[0][:, :], psum[:, 7, :], ACT.Copy).then_inc(s["qh"], 1)

            def head(g, i, this, last, nxt):
                n = REP * g + i
                for qt in range(TT - 1):
                    if this:
                        exponential(n, qt)
                    if last:
                        turned_high(g, i, qt)
                if last:
                    turned_high(g, i, TT - 1)
                    act.activation(probs_t[0][0:SEQ, ST, :], psum[0:SEQ, 6, :], ACT.Copy).then_inc(s["tailh"], 1)
                if this:
                    exponential(n, TT - 1)
                if nxt:
                    queries_high(n + 1)
                if nxt and has_weight(g, i):
                    weight_high(s["wqt"], n + 3, turn_use(g, i, 4)[1], flat_high)
                if this and i > 0:
                    output_weight_high(g, i)
                if last:
                    act.wait_ge(s["pv"], n)
                    act.activation(mixed_t[0][:, (i - 1) % REP, :], psum[:, 6, :], ACT.Copy).then_inc(s["ah"], 1)
                if this and i == 0:
                    output_weight_high(g, i)

            def exponential(n, qt):
                act.wait_ge(s["max"], TT * n + qt + 1)
                wait(act, s["pt"], TT * (n - 1) + qt + 1)
                act.activation(probs[:, qt, :].rearrange("p (a k) -> p a k", a=2),
                               psum[:, 2 * (qt % 2):2 * (qt % 2) + 2, 0:HALF],
                               ACT.Exp, bias=neg_max[:, qt:qt + 1], accum_out=den[:, qt:qt + 1]).then_inc(s["exp"], 1)

            def turned_high(g, i, qt):
                act.wait_ge(s["pt"], TT * (REP * g + i - 1) + qt + 1)
                act.activation(probs_t[0][:, 0:ST, qt * P:(qt + 1) * P],
                               psum[:, turn_use(g, i, qt)[1], :].rearrange("p (t q) -> p t q", t=ST),
                               ACT.Copy).then_inc(s["th"], 1)

            def output_weight_high(g, i):
                weight_high(s["wot"], REP * g + i + 1, turn_use(g, i, 9 if i == 0 else 5)[1],
                            wo_t[0][:, i, :])

            weight_high(s["wqt"], 1, 4, flat_high)
            queries_high(0)
            weight_high(s["wqt"], 2, 5, flat_high)
            run(act, head)

        @block.vector
        def _(dve):
            def high_count(g, i, k):
                outputs_to_come = TT if i == 0 and k < 5 else 0
                return 24 * g + HEAD_FIRST_USE[i] + k - 5 + outputs_to_come - weights_missing(g, i, k)

            def weight_low(count, bank, dst, high):
                dve.wait_ge(s["th"], count)
                dve.tensor_tensor(dst, psum[:, bank, :], high, ALU.subtract).then_inc(s["tl"], 1)

            def queries_low(n):
                dve.wait_ge(s["qh"], n + 1)
                dve.tensor_tensor(q_t[1][:, :], psum[:, 7, :], q_t[0][:, :], ALU.subtract).then_inc(s["ql"], 1)

            def values_low(g):
                dve.wait_ge(s["vh"], 2 * g + 2)
                dve.tensor_tensor(value[1][:, 0:ST, :], v_sel[:, :, bass.ds(g * HD, HD)], value[0][:, 0:ST, :],
                                  ALU.subtract).then_inc(s["vl"], 1)
                dve.tensor_tensor(value[1][0:SEQ, ST, :], v_new[0:SEQ, bass.ds(g, 1), :].rearrange("p a d -> p (a d)"),
                                  value[0][0:SEQ, ST, :], ALU.subtract).then_inc(s["vl"], 1)

            def flat_wq(a):
                return wq_t[a][:, :, :].rearrange("p c d -> p (c d)")

            def turned_low(g, i, qt):
                dve.wait_ge(s["th"], high_count(g, i, qt))
                dve.tensor_tensor(probs_t[1][:, 0:ST, qt * P:(qt + 1) * P],
                                  psum[:, turn_use(g, i, qt)[1], :].rearrange("p (t q) -> p t q", t=ST),
                                  probs_t[0][:, 0:ST, qt * P:(qt + 1) * P], ALU.subtract).then_inc(s["tl"], 1)

            def invert(n, qt):
                dve.wait_ge(s["exp"], TT * n + qt + 1)
                wait(dve, s["norm"], TT * (n - 1) + qt + 1)
                dve.reciprocal(rden[:, qt:qt + 1], den[:, qt:qt + 1]).then_inc(s["rd"], 1)

            def output_weight_low(g, i):
                k = 9 if i == 0 else 5
                weight_low(high_count(g, i, k), turn_use(g, i, k)[1],
                           wo_t[1][:, i, :], wo_t[0][:, i, :])

            def head(g, i, this, last, nxt):
                n = REP * g + i
                for qt in range(TT):
                    if this:
                        dve.wait_ge(s["s"], TT * n + qt + 1)
                        wait(dve, s["exp"], TT * (n - 1) + qt + 1)
                        dve.tensor_reduce(neg_max[:, qt:qt + 1],
                                          psum[:, 2 * (qt % 2):2 * (qt % 2) + 2, 0:HALF],
                                          AX.XY, ALU.max, negate=True).then_inc(s["max"], 1)
                    if qt > 0 and last:
                        turned_low(g, i, qt - 1)
                    if qt > 0 and this:
                        invert(n, qt - 1)
                if last:
                    turned_low(g, i, TT - 1)
                    dve.wait_ge(s["tailh"], n)
                    dve.tensor_tensor(probs_t[0][SEQ:P, ST, :], psum[0:SEQ, 6, :], probs_t[0][0:SEQ, ST, :],
                                      ALU.subtract).then_inc(s["taill"], 1)
                if this:
                    invert(n, TT - 1)
                if nxt:
                    queries_low(n + 1)
                if nxt and has_weight(g, i):
                    weight_low(high_count(g, i, 4), turn_use(g, i, 4)[1], flat_wq(1), flat_wq(0))
                if this and i > 0:
                    output_weight_low(g, i)
                if last:
                    dve.wait_ge(s["ah"], n)
                    j = (i - 1) % REP
                    dve.tensor_tensor(mixed_t[1][:, j, :], psum[:, 6, :], mixed_t[0][:, j, :],
                                      ALU.subtract).then_inc(s["al"], 1)
                if i == 0 and last:
                    for qt in range(TT):
                        dve.wait_ge(s["o"], TT * (g - 1) + qt + 1)
                        dve.tensor_tensor(core.x[:, qt, :], psum[:, turn_use(g, 0, 5 + qt)[1], :],
                                          core.x[:, qt, :], ALU.add).then_inc(s["tl"], 1)
                if this and i == 0:
                    output_weight_low(g, i)
                    values_low(g)

            weight_low(1, 4, flat_wq(1), flat_wq(0))
            queries_low(0)
            weight_low(2, 5, flat_wq(1), flat_wq(0))
            run(dve, head)
            dve.wait_ge(s["tl"], turn_use(NKV, 0, 4 + TT)[0] + 1)

        @block.gpsimd
        def _(pool):
            def values(g):
                pool.tensor_copy(value[0][:, 0:ST, :], v_sel[:, :, bass.ds(g * HD, HD)]).then_inc(s["vh"], 1)
                pool.tensor_copy(value[0][:, ST, :],
                                 v_new[:, bass.ds(g, 1), :].rearrange("p a d -> p (a d)")).then_inc(s["vh"], 1)

            def head(g, i, this, last, nxt):
                n = REP * g + i
                if not this:
                    return
                for qt in range(TT):
                    pool.wait_ge(s["rd"], TT * n + qt + 1)
                    pool.tensor_tensor(probs[:, qt, :], probs[:, qt, :], rden[:, qt:qt + 1].to_broadcast([P, KEYS]),
                                       ALU.mult).then_inc(s["norm"], 1)
                if i == 0:
                    wait(pool, s["pv"], n)
                    values(g)

            pool.wait_ge(core.cache_in, 2 * TOPK * 16)
            run(pool, head)


def feed_forward(core, own, norm, ffn, xh, xl):
    nc, arg, psum = core.nc, core.arg, core.psum
    ones = core.sb("ones", [P, P], ctx=own)
    total = core.sb("abs_total", [P, 3], ctx=own)
    coeff = core.sb("coeff", [P, 3], ctx=own)
    raw, s_raw = ffn["raw"], ffn["in"]
    diff = core.sb("ffn_diff", [P, 3, DIM], ctx=own)
    sign = [core.sb(f"ffn_sign{i}", [P, 3, DIM], ctx=own) for i in range(SLOTS)]
    quant = core.sb("ffn_quant", [P, 3, DIM], ctx=own)
    w_t = [core.sb(f"ffn_w_t_{s}", [P, 3, DIM], F32R, ctx=own) for s in ("high", "low")]
    gate = core.sb("gate", [P, TOK], ctx=own)
    hidden = core.sb("hidden", [P, TOK], ctx=own)
    hid = [core.sb(f"hidden_{s}", [P, TOK], F32R, ctx=own) for s in ("high", "low")]
    s_ones = core.sem("ones_ready", own)
    s_tot = core.sem("abs_summed", own)
    s_all = core.sem("abs_spread", own)
    s_co = core.sem("coeff_ready", own)
    s_diff = core.sem("ffn_diff_done", own)
    s_sign = core.sem("ffn_sign_done", own)
    s_quant = [core.sem(f"ffn_quant_done{k}", own) for k in range(3)]
    s_turn = [core.sem(f"ffn_turned{k}", own) for k in range(3)]
    s_wh = [core.sem(f"ffn_high_done{k}", own) for k in range(3)]
    s_wl = [core.sem(f"ffn_low_done{k}", own) for k in range(3)]
    s_gu = [core.sem(f"gate_up_done{k}", own) for k in range(2)]
    s_silu = core.sem("silu_done", own)
    s_h = core.sem("hidden_done", own)
    s_hh = core.sem("hidden_high_done", own)
    s_hl = core.sem("hidden_low_done", own)
    s_d = core.sem("down_done", own)
    s_x = core.sem("final_sum_done", own)
    s_out = core.sem("out_written", own)
    turn_bank = (4, 5, 4)

    def run(eng, chunk):
        for c in range(2):
            chunk(c, c % SLOTS)
        with eng.Fori(0, (CH - 5) // SLOTS) as j:
            for k in range(SLOTS):
                chunk(SLOTS * j + 2 + k, (2 + k) % SLOTS)
        for c in range(CH - 3, CH):
            chunk(c, c % SLOTS)

    assert (CH - 5) % SLOTS == 0

    def within(c, ahead):
        return not isinstance(c, int) or c + ahead < CH

    with nc.Block() as block:

        @block.sync
        def _(sp):
            def load(c, par):
                wait(sp, s_quant[2], c - SLOTS + 1)
                wait(sp, s_quant[1], c - SLOTS + 1)
                load_ffn_weights(core, ffn, sp, c, par)

            for c in range(1, SLOTS + 2):
                load(c, c % SLOTS)
            with sp.Fori(0, (CH - 5) // SLOTS) as j:
                for k in range(SLOTS):
                    load(SLOTS * j + 5 + k, (5 + k) % SLOTS)
            out = core.out.rearrange("b n e -> (b n) e").rearrange("(j p) e -> p j e", p=P)
            for j in range(TT):
                sp.wait_ge(s_x, j + 1)
                sp.dma_start(out[:, j, :], core.x[:, j, :]).then_inc(s_out, 16)
            sp.wait_ge(s_out, 16 * TT)

        @block.gpsimd
        def _(pool):
            def chunk(c, par):
                pool.wait_ge(s_raw[par], 96 // SLOTS * c + 96 - 96 // SLOTS * par)
                wait(pool, s_sign, c)
                pool.tensor_tensor(diff[:, :, :], raw[par][:, :, 0, :], raw[par][:, :, 1, :],
                                   ALU.subtract).then_inc(s_diff, 1)

            pool.memset(ones[:, :], 1.0).then_inc(s_ones, 1)
            run(pool, chunk)

        @block.tensor
        def _(pe):
            def turn(c, k):
                bank = turn_bank[k]
                pe.wait_ge(s_quant[k], c + 1)
                if k == 0:
                    wait(pe, s_wl[2], c - 1)
                elif k == 1:
                    wait(pe, s_wl[1], c)
                else:
                    pe.wait_ge(s_wl[0], c + 2 if within(c, 1) else CH)
                for i in range(DC):
                    mm = pe.transpose(psum[:, bank, i * P:(i + 1) * P], quant[:, k, i * P:(i + 1) * P],
                                      core.ident[:, :])
                mm.then_inc(s_turn[k], 1)

            def gates(c, k):
                wait(pe, s_silu if k == 0 else s_h, c)
                pe.wait_ge(s_wl[k], c + 1)
                for step, (a, b) in enumerate(PASSES):
                    for i in range(DC):
                        mm = pe.matmul(psum[:, 6 + k, :], w_t[a][:, k, i * P:(i + 1) * P], (xh, xl)[b][:, i, :],
                                       start=(step == 0 and i == 0), stop=(step == 2 and i == DC - 1))
                mm.then_inc(s_gu[k], 1)

            def down(c):
                first, last = isinstance(c, int) and c == 0, isinstance(c, int) and c == CH - 1
                pe.wait_ge(s_hl, c + 1)
                pe.wait_ge(s_wl[2], c + 1)
                for qt in range(TT):
                    for step, (a, b) in enumerate(PASSES):
                        mm = pe.matmul(psum[:, qt, :], hid[a][:, qt * P:(qt + 1) * P], w_t[b][:, 2, :],
                                       start=(first and step == 0), stop=(last and step == 2),
                                       skip_group_check=True)
                mm.then_inc(s_d, 1)

            def chunk(c, par):
                gates(c, 0)
                gates(c, 1)
                if within(c, 1):
                    turn(c + 1, 0)
                    turn(c + 1, 1)
                if not (isinstance(c, int) and c == 0):
                    down(c - 1)
                turn(c, 2)

            pe.wait_ge(s_ones, 1)
            pe.wait_ge(s_tot, 1)
            pe.matmul(psum[:, 6, 0:3], ones[:, :], total[:, :], start=True, stop=True).then_inc(s_all, 1)
            norm.turn(pe)
            pe.wait_ge(s_co, 1)
            turn(0, 0)
            turn(0, 1)
            pe.wait_ge(norm.s_low, TT)
            run(pe, chunk)
            down(CH - 1)

        @block.scalar
        def _(act):
            def signs(c, par):
                act.wait_ge(s_diff, c + 1)
                wait(act, s_quant[2], c - SLOTS + 1)
                wait(act, s_quant[1], c - SLOTS + 1)
                act.activation(sign[par][:, :, :], diff[:, :, :], ACT.Sign).then_inc(s_sign, 1)

            def high(c, k):
                act.wait_ge(s_turn[k], c + 1)
                act.activation(w_t[0][:, k, :], psum[:, turn_bank[k], :], ACT.Copy).then_inc(s_wh[k], 1)

            def chunk(c, par):
                act.wait_ge(s_gu[0], c + 1)
                wait(act, s_h, c)
                act.activation(gate[:, :], psum[:, 6, :], ACT.Silu).then_inc(s_silu, 1)
                if within(c, 1):
                    high(c + 1, 0)
                    high(c + 1, 1)
                act.wait_ge(s_h, c + 1)
                wait(act, s_d, c)
                act.activation(hid[0][:, :], hidden[:, :], ACT.Copy).then_inc(s_hh, 1)
                high(c, 2)
                if within(c, 2):
                    signs(c + 2, (par + 2) % SLOTS)

            norm.root(act)
            signs(0, 0)
            norm.copy_out(act)
            high(0, 0)
            high(0, 1)
            signs(1, 1)
            run(act, chunk)

        @block.vector
        def _(dve):
            def quantise(c, par, k):
                dve.wait_ge(s_sign, c + 1)
                wait(dve, s_turn[k], c)
                dve.scalar_tensor_tensor(out=quant[:, k, :], in0=sign[par][:, k, :], scalar=coeff[:, k:k + 1],
                                         in1=raw[par][:, k, 1, :], op0=ALU.mult, op1=ALU.add).then_inc(s_quant[k], 1)

            def low(c, k):
                dve.wait_ge(s_wh[k], c + 1)
                dve.tensor_tensor(w_t[1][:, k, :], psum[:, turn_bank[k], :], w_t[0][:, k, :],
                                  ALU.subtract).then_inc(s_wl[k], 1)

            def chunk(c, par):
                dve.wait_ge(s_silu, c + 1)
                dve.wait_ge(s_gu[1], c + 1)
                wait(dve, s_hl, c)
                dve.tensor_tensor(hidden[:, :], psum[:, 7, :], gate[:, :], ALU.mult).then_inc(s_h, 1)
                if within(c, 1):
                    low(c + 1, 0)
                    low(c + 1, 1)
                dve.wait_ge(s_hh, c + 1)
                dve.tensor_tensor(hid[1][:, :], hidden[:, :], hid[0][:, :], ALU.subtract).then_inc(s_hl, 1)
                low(c, 2)
                if within(c, 2):
                    quantise(c + 2, (par + 2) % SLOTS, 0)
                    quantise(c + 2, (par + 2) % SLOTS, 1)
                if within(c, 1):
                    quantise(c + 1, (par + 1) % SLOTS, 2)

            dve.tensor_reduce(total[:, :], core.abs_sum[:, :, :].rearrange("p b k -> p k b"), AX.X,
                              ALU.add).then_inc(s_tot, 1)
            dve.wait_ge(s_all, 1)
            dve.tensor_scalar(coeff[:, :], psum[:, 6, 0:3], 1.0 / WSIZE, None, ALU.mult).then_inc(s_co, 1)
            norm.normalise(dve)
            dve.wait_ge(s_co, 1)
            for k in range(3):
                quantise(0, 0, k)
            norm.low_parts(dve)
            low(0, 0)
            low(0, 1)
            quantise(1, 1, 0)
            quantise(1, 1, 1)
            run(dve, chunk)
            dve.wait_ge(s_d, CH)
            for j in range(TT):
                dve.tensor_tensor(core.x[:, j, :], psum[:, j, :], core.x[:, j, :], ALU.add).then_inc(s_x, 1)


def layer(nc, out, **arg):
    with ExitStack() as ctx:
        core = Core(nc, ctx, arg, out)
        with ExitStack() as own:
            even_ctx = core.cache.rearrange("p a t c -> p (a t c)")[:, 0:KT * DIM].rearrange("p (t e) -> p t e", t=KT)
            w = {
                "ctx_nat": [even_ctx, core.sb("ctx_nat_odd", [P, KT, DIM], ctx=own)],
                "wkv_d": core.sb("wkv_d", [P, DC, LKV], ctx=own),
                "wv_u": core.sb("wv_u", [P, XH, OW], ctx=own),
                "c_nat": core.sb("c_nat", [P, 2, KT, UW], ctx=own),
                "c_stack": core.sb("c_stack", [P, KT, STACK], ctx=own),
                "c_stage": core.sb("c_stage", [P, KT, LKV], ctx=own),
                "c_t": core.sb("c_t", [P, 2, KT * P], F32R, ctx=own),
                "max_row": core.sb("max_row", [P, QTILES, STACK], ctx=own),
                "q_t": core.sb("q_t", [SHIFT, BATCH, XH, SEQ], F32R, ctx=own),
            }
            with ExitStack() as first:
                w["w_qk"] = core.sb("w_qk", [LQ, XH, 2, LKV], ctx=first)
                w["wq_d"] = core.sb("wq_d", [P, DC, LQ], ctx=first)
                xn_t = core.sb("xn_t", [P, DC, TOK], ctx=first)
                load_and_constants(core, w, xn_t)
                cross_queries(core, w, xn_t)
            cross_attention(core, w, own)
        k_sel, v_sel = core.cache[:, 0], core.cache[:, 1]
        ffn = {
            "raw": [core.sb("ffn_raw0", [P, 3, 2, DIM])],
            "in": [core.sem(f"ffn_raw_in{i}") for i in range(SLOTS)],
        }
        with ExitStack() as own:
            k_high = core.sb("k_high", [P, NKV * KEYS], F32R, ctx=own)
            k_low = core.sb("k_low", [P, NKV * KEYS], F32R, ctx=own)
            v_new = core.sb("v_new", [P, NKV, HD], ctx=own)
            xh = core.sb("attn_x_high", [P, DC, TOK], F32R, ctx=own)
            xl = core.sb("attn_x_low", [P, DC, TOK], F32R, ctx=own)
            qo = {
                "wq": core.sb("wq_nat", [P, REP, DIM], ctx=own),
                "wo": core.sb("wo_nat", [P, REP, DC, HD], ctx=own),
                "wq_in": [core.sem(f"query_weight_in{i}", own) for i in range(REP)],
                "wo_in": [core.sem(f"output_weight_in{i}", own) for i in range(REP)],
            }
            with ExitStack() as first:
                kv = {
                    "nat": [core.sb(f"kv_weight{i}", [P, 2, DIM], ctx=first) for i in range(2)],
                    "in": [core.sem(f"kv_weight_in{i}", first) for i in range(2)],
                }
                xe = core.sb("new_tokens", [P, DC, SEQ], ctx=first)

                norm = LayerNorm(core, "norm2", first, parts=(xh, xl), exact=xe, exact_tokens=SEQ, first_bank=3)
                rotated_keys(core, first, norm, kv, qo, k_sel, xe, k_high, k_low, v_new)
            grouped_attention(core, own, qo, ffn, xh, xl, k_high, k_low, v_sel, v_new)
        with ExitStack() as own:
            xh = core.sb("ffn_x_high", [P, DC, TOK], F32R, ctx=own)
            xl = core.sb("ffn_x_low", [P, DC, TOK], F32R, ctx=own)
            ffn["raw"] += [core.sb(f"ffn_raw{i}", [P, 3, 2, DIM], ctx=own) for i in range(1, SLOTS)]
            norm = LayerNorm(core, "norm3", own, parts=(xh, xl))
            feed_forward(core, own, norm, ffn, xh, xl)


INPUTS = {
    "x": "x", "ctx": "ctx_4096", "Wq_d": "L0_xattn_Wq_d", "W_qk": "L0_xattn_W_qk", "Wkv_d": "L0_xattn_Wkv_d",
    "Wv_u": "L0_xattn_Wv_u", "cos": "L0_attn_freqs_cos", "sin": "L0_attn_freqs_sin", "wq": "L0_attn_wq",
    "wk": "L0_attn_wk", "wv": "L0_attn_wv", "wo": "L0_attn_wo", "k_cache": "L0_attn_k_cache",
    "v_cache": "L0_attn_v_cache", "block_idx": "L0_attn_block_idx", "w1": "L0_ffn_w1",
    "mean_w1": "L0_ffn_mean_w1", "w2": "L0_ffn_w2", "mean_w2": "L0_ffn_mean_w2", "w3": "L0_ffn_w3",
    "mean_w3": "L0_ffn_mean_w3",
}


def kernel(**inputs):
    import numpy as _np
    import concourse.bacc as _bacc
    from concourse import mybir as _mybir
    from concourse.bass_utils import run_bass_kernel_spmd as _run

    nc = _bacc.Bacc("TRN2", target_bir_lowering=False, num_devices=1)
    arrays, args = {}, {}
    for short, name in INPUTS.items():
        a = _np.ascontiguousarray(inputs[name])
        arrays[f"in_{name}_dram"] = a
        args[short] = nc.dram_tensor(f"in_{name}_dram", a.shape, _mybir.dt.from_np(a.dtype),
                                     kind="ExternalInput").ap()
    out = nc.dram_tensor("out_0_dram", (BATCH, SEQ, DIM), F32, kind="ExternalOutput").ap()
    layer(nc, out, **args)
    r = _run(nc, [arrays], core_ids=[0])
    return r.results[0]["out_0_dram"]
```
